# Optimizing a Trainium2 kernel written in Bass

```python
import numpy as np
import jax
import jax.numpy as jnp

def _softmax(x, axis=-1):
    return jax.nn.softmax(x, axis=axis)

def _gelu(x):
    return jax.nn.gelu(x, approximate=True)

def _silu(x):
    return jax.nn.silu(x)

def _sigmoid(x):
    return jax.nn.sigmoid(x)

def _layernorm(x, axis=-1, eps=1e-05):
    m = jnp.mean(x, axis=axis, keepdims=True)
    v = jnp.var(x, axis=axis, keepdims=True)
    return (x - m) / jnp.sqrt(v + eps)

def _scatter_add(tgt, idx, src, axis=0):
    return tgt.at[idx].add(src)

def _segment_sum(src, seg, n):
    return jax.ops.segment_sum(src, seg, n)
kernel_name = 'mk_perceiver_d1_seqx_r8_4dff60'

def setup_inputs(seed: int=0):
    np.random.seed(seed)
    _w = jnp.asarray

    def _rec_inputs():
        import jax
        import jax.numpy as jnp
        _rk = jax.random.key(seed)
        x = 7.22e-05 + 1 * jax.random.normal(jax.random.fold_in(_rk, 1), (64, 64, 128), jnp.float32)
        _lenS = 64 - jax.random.randint(jax.random.fold_in(_rk, 7), (64,), 0, max(1, 64 // 4) + 1, jnp.int32)
        _lenS2 = 128 - jax.random.randint(jax.random.fold_in(_rk, 8), (64,), 0, max(1, 128 // 4) + 1, jnp.int32)
        _ctx_1024P = jax.random.normal(jax.random.fold_in(_rk, 11), (64, 16, 128), jnp.float32)
        _ctx_1024c = jax.random.dirichlet(jax.random.fold_in(_rk, 511), 0.3 * jnp.ones((16,), jnp.float32), (64, 128))
        _ctx_1024t = jnp.einsum('bsk,bkd->bsd', _ctx_1024c, _ctx_1024P)
        _ctx_1024t = _ctx_1024t * jax.lax.rsqrt(jnp.mean(jnp.square(_ctx_1024t)) + 1e-12) * 0.953939
        ctx_1024 = 4.13588e-05 + 0.999923 * (_ctx_1024t + 0.3 * jax.random.normal(jax.random.fold_in(_rk, 611), (64, 128, 128), jnp.float32))
        return (x, ctx_1024)
    x, ctx_1024 = _rec_inputs()

    def _L0_xattn_setup():
        import jax, jax.numpy as jnp
        import numpy as np
        DIM = 128
        H = 16
        HD = DIM // H
        EPS = 1e-05
        key = jax.random.key(seed)
        ks = jax.random.split(key, 12)
        B, S = (4, 256)
        s = 0.02
        return {'q': jax.random.normal(ks[0], (B, S, DIM), jnp.float32), 'k': jax.random.normal(ks[1], (B, S, DIM), jnp.float32), 'v': jax.random.normal(ks[2], (B, S, DIM), jnp.float32), 'Wq': jax.random.normal(ks[3], (DIM, DIM), jnp.float32) * s, 'bq': jnp.zeros((DIM,), jnp.float32), 'Wk': jax.random.normal(ks[4], (DIM, DIM), jnp.float32) * s, 'bk': jnp.zeros((DIM,), jnp.float32), 'Wv': jax.random.normal(ks[5], (DIM, DIM), jnp.float32) * s, 'bv': jnp.zeros((DIM,), jnp.float32), 'Wo': jax.random.normal(ks[6], (DIM, DIM), jnp.float32) * s, 'bo': jnp.zeros((DIM,), jnp.float32), 'gamma': jnp.ones((DIM,), jnp.float32), 'beta': jnp.zeros((DIM,), jnp.float32)}
    _L0_xattn_all = _L0_xattn_setup()
    _L0_xattn_in = {k: v for k, v in _L0_xattn_all.items() if k in ('Wq', 'bq', 'Wk', 'bk', 'Wv', 'bv', 'Wo', 'bo', 'gamma', 'beta')}
    del _L0_xattn_all

    def _L0_attn_setup():
        import jax, jax.numpy as jnp
        import numpy as np
        D_IN, HEAD_DIM = (128, 128)
        key = jax.random.key(seed)
        ks = jax.random.split(key, 9)
        s = 0.02
        return {'x': jax.random.normal(ks[0], (4, 512, D_IN), dtype=jnp.float32), 'Wq': jax.random.normal(ks[1], (HEAD_DIM, D_IN), dtype=jnp.float32) * s, 'bq': jnp.zeros((HEAD_DIM,), dtype=jnp.float32), 'Wk': jax.random.normal(ks[2], (HEAD_DIM, D_IN), dtype=jnp.float32) * s, 'bk': jnp.zeros((HEAD_DIM,), dtype=jnp.float32), 'Wv': jax.random.normal(ks[3], (HEAD_DIM, D_IN), dtype=jnp.float32) * s, 'bv': jnp.zeros((HEAD_DIM,), dtype=jnp.float32), 'Wo': jax.random.normal(ks[4], (D_IN, HEAD_DIM), dtype=jnp.float32) * s, 'bo': jnp.zeros((D_IN,), dtype=jnp.float32)}
    _L0_attn_all = _L0_attn_setup()
    _L0_attn_in = {k: v for k, v in _L0_attn_all.items() if k in ('Wq', 'bq', 'Wk', 'bk', 'Wv', 'bv', 'Wo', 'bo')}
    del _L0_attn_all

    def _L0_ffn_setup():
        import jax, jax.numpy as jnp
        import numpy as np
        D_MODEL = 128
        N_EXPERTS = 8
        TOP_K = 2
        HIDDEN = 4 * D_MODEL
        key = jax.random.key(seed)
        ks = jax.random.split(key, 6)
        B, S = (2, 256)
        x = jax.random.normal(ks[0], (B, S, D_MODEL), dtype=jnp.float32)
        shared_w1 = jax.random.normal(ks[1], (HIDDEN, D_MODEL), dtype=jnp.float32) * 0.02
        shared_w2 = jax.random.normal(ks[2], (D_MODEL, HIDDEN), dtype=jnp.float32) * 0.02
        experts_w1 = jax.random.normal(ks[3], (N_EXPERTS, HIDDEN, D_MODEL), dtype=jnp.float32) * 0.02
        experts_w2 = jax.random.normal(ks[4], (N_EXPERTS, D_MODEL, HIDDEN), dtype=jnp.float32) * 0.02
        gate_w = jax.random.normal(ks[5], (N_EXPERTS, D_MODEL), dtype=jnp.float32) * 0.02
        return {'x': x, 'shared_w1': shared_w1, 'shared_w2': shared_w2, 'experts_w1': experts_w1, 'experts_w2': experts_w2, 'gate_w': gate_w}
    _L0_ffn_all = _L0_ffn_setup()
    _L0_ffn_in = {k: v for k, v in _L0_ffn_all.items() if k in ('shared_w1', 'shared_w2', 'experts_w1', 'experts_w2', 'gate_w')}
    del _L0_ffn_all
    return {'x': x, 'ctx_1024': ctx_1024, 'L0_xattn_Wq': _L0_xattn_in['Wq'], 'L0_xattn_bq': _L0_xattn_in['bq'], 'L0_xattn_Wk': _L0_xattn_in['Wk'], 'L0_xattn_bk': _L0_xattn_in['bk'], 'L0_xattn_Wv': _L0_xattn_in['Wv'], 'L0_xattn_bv': _L0_xattn_in['bv'], 'L0_xattn_Wo': _L0_xattn_in['Wo'], 'L0_xattn_bo': _L0_xattn_in['bo'], 'L0_xattn_gamma': _L0_xattn_in['gamma'], 'L0_xattn_beta': _L0_xattn_in['beta'], 'L0_attn_Wq': _L0_attn_in['Wq'], 'L0_attn_bq': _L0_attn_in['bq'], 'L0_attn_Wk': _L0_attn_in['Wk'], 'L0_attn_bk': _L0_attn_in['bk'], 'L0_attn_Wv': _L0_attn_in['Wv'], 'L0_attn_bv': _L0_attn_in['bv'], 'L0_attn_Wo': _L0_attn_in['Wo'], 'L0_attn_bo': _L0_attn_in['bo'], 'L0_ffn_shared_w1': _L0_ffn_in['shared_w1'], 'L0_ffn_shared_w2': _L0_ffn_in['shared_w2'], 'L0_ffn_experts_w1': _L0_ffn_in['experts_w1'], 'L0_ffn_experts_w2': _L0_ffn_in['experts_w2'], 'L0_ffn_gate_w': _L0_ffn_in['gate_w']}

def reference(x, ctx_1024, L0_xattn_Wq, L0_xattn_bq, L0_xattn_Wk, L0_xattn_bk, L0_xattn_Wv, L0_xattn_bv, L0_xattn_Wo, L0_xattn_bo, L0_xattn_gamma, L0_xattn_beta, L0_attn_Wq, L0_attn_bq, L0_attn_Wk, L0_attn_bk, L0_attn_Wv, L0_attn_bv, L0_attn_Wo, L0_attn_bo, L0_ffn_shared_w1, L0_ffn_shared_w2, L0_ffn_experts_w1, L0_ffn_experts_w2, L0_ffn_gate_w):
    import jax
    import jax.numpy as jnp

    def _L0_xattn_ref(q, k, v, Wq, bq, Wk, bk, Wv, bv, Wo, bo, gamma, beta):
        import jax, jax.numpy as jnp
        import numpy as np
        DIM = 128
        H = 16
        HD = DIM // H
        EPS = 1e-05
        B, S, _ = q.shape
        scale = HD ** (-0.5)

        def proj(x, W, b):
            return (x @ W.T + b).reshape(B, -1, H, HD).transpose(0, 2, 1, 3)
        qh = proj(q, Wq, bq)
        kh = proj(k, Wk, bk)
        vh = proj(v, Wv, bv)
        scores = jnp.einsum('bhsd,bhtd->bhst', qh, kh) * scale
        attn = jax.nn.softmax(scores, axis=-1)
        out = jnp.einsum('bhst,bhtd->bhsd', attn, vh)
        out = out.transpose(0, 2, 1, 3).reshape(B, S, DIM)
        out = out @ Wo.T + bo
        mu = out.mean(-1, keepdims=True)
        var = out.var(-1, keepdims=True)
        return (out - mu) * jax.lax.rsqrt(var + EPS) * gamma + beta

    def _L0_attn_ref(x, Wq, bq, Wk, bk, Wv, bv, Wo, bo):
        import jax, jax.numpy as jnp
        import numpy as np
        D_IN, HEAD_DIM = (128, 128)
        B, S, D = x.shape
        Q = jnp.einsum('bsd,hd->bsh', x, Wq) + bq
        K = jnp.einsum('bsd,hd->bsh', x, Wk) + bk
        V = jnp.einsum('bsd,hd->bsh', x, Wv) + bv
        scores = jnp.einsum('bqh,bkh->bqk', Q, K)
        causal = jnp.tril(jnp.ones((S, S), dtype=bool))
        scores = jnp.where(causal, scores, -jnp.inf)
        scale = jnp.float32(HEAD_DIM) ** (-0.5)
        attn = jax.nn.softmax(scores * scale, axis=-1)
        out = jnp.einsum('bqk,bkh->bqh', attn, V)
        return jnp.einsum('bsh,dh->bsd', out, Wo) + bo

    def _L0_ffn_ref(x, shared_w1, shared_w2, experts_w1, experts_w2, gate_w):
        import jax, jax.numpy as jnp
        import numpy as np
        D_MODEL = 128
        N_EXPERTS = 8
        TOP_K = 2
        HIDDEN = 4 * D_MODEL
        B, S, D = x.shape
        T = B * S
        x_flat = x.reshape(T, D)
        shared = jnp.einsum('td,dh->th', x_flat, shared_w1.T)
        shared = jnp.einsum('th,hd->td', jax.nn.silu(shared), shared_w2.T)
        gate_logits = x_flat @ gate_w.T
        top_k_gates, top_k_idx = jax.lax.top_k(gate_logits, TOP_K)
        top_k_gates = jax.nn.softmax(top_k_gates, axis=1)
        gates = jnp.zeros((T, N_EXPERTS), dtype=x.dtype)
        gates = gates.at[jnp.arange(T)[:, None], top_k_idx].set(top_k_gates)
        h = jnp.einsum('td,ehd->teh', x_flat, experts_w1)
        expert_out = jnp.einsum('teh,edh->ted', jax.nn.silu(h), experts_w2)
        selected = jnp.einsum('ted,te->td', expert_out, gates)
        return (shared + selected).reshape(B, S, D)
    x = x + _L0_xattn_ref(_layernorm(x, axis=-1), ctx_1024, ctx_1024, L0_xattn_Wq, L0_xattn_bq, L0_xattn_Wk, L0_xattn_bk, L0_xattn_Wv, L0_xattn_bv, L0_xattn_Wo, L0_xattn_bo, L0_xattn_gamma, L0_xattn_beta)
    x = x + _L0_attn_ref(_layernorm(x, axis=-1), L0_attn_Wq, L0_attn_bq, L0_attn_Wk, L0_attn_bk, L0_attn_Wv, L0_attn_bv, L0_attn_Wo, L0_attn_bo)
    x = x + _L0_ffn_ref(_layernorm(x, axis=-1), L0_ffn_shared_w1, L0_ffn_shared_w2, L0_ffn_experts_w1, L0_ffn_experts_w2, L0_ffn_gate_w)
    return x

_drawn_inputs = setup_inputs


def setup_inputs(seed=0):
    import zlib

    import numpy as np

    out = dict(_drawn_inputs(seed))
    spreads = {'L0_xattn_bq': (0.0, 0.8),
     'L0_xattn_bk': (0.0, 2.0),
     'L0_xattn_bv': (0.0, 0.1),
     'L0_xattn_bo': (0.0, 0.1),
     'L0_xattn_gamma': (1.0, 0.2),
     'L0_xattn_beta': (0.0, 0.1),
     'L0_attn_bq': (0.0, 2.0),
     'L0_attn_bk': (0.0, 2.0),
     'L0_attn_bv': (0.0, 0.519),
     'L0_attn_bo': (0.0, 0.1)}
    factors = {'L0_xattn_Wq': 8.0, 'L0_xattn_Wk': 8.0, 'L0_attn_Wq': 30.064, 'L0_attn_Wk': 29.653}
    for name, (base, spread) in spreads.items():
        noise = np.random.default_rng([zlib.crc32(name.encode()), seed]).standard_normal(out[name].shape)
        drawn = base * np.exp(spread * noise) if base else spread * noise
        out[name] = jnp.asarray(drawn.astype(out[name].dtype))
    for name, factor in factors.items():
        out[name] = (out[name] * factor).astype(out[name].dtype)
    return out
```

```python
import numpy as np
import concourse.bass as bass
from concourse import mybir
from contextlib import ExitStack

F32 = mybir.dt.float32
F16 = mybir.dt.float16
BF16 = mybir.dt.bfloat16
U32 = mybir.dt.uint32
ALU = mybir.AluOpType
ACT = mybir.ActivationFunctionType
AX = mybir.AxisListType

B, S, SK, D = 64, 64, 128, 128
HEADS = 16
HD = D // HEADS
P = 128
EPS = 1e-5
E, HID = 8, 512
XSCALE = float(HD) ** -0.5
ASCALE = float(D) ** -0.5
MASKED = -1e30
CONSTS = 23

NT = B * S // P
HALVES = 16
PAIRS = 2
CB = 4
GROUPS = 4
JH = 4
UNITS = PAIRS * GROUPS
VW = 2 * HD + 1
NE = E + 1
CH = HID // P
GT = 4
FG = NT // GT
NK = NE * CH
RING = 4

ROWS = ["xbq", "xbk", "xbv", "xbo", "abq", "abk", "abv", "abo", "gamma", "beta"]
MATS = ["xWq", "xWk", "xWv", "xWo", "aWq", "aWk", "aWv", "aWo"]

MISC = [("xnT", 0, 1, 0), ("qk", 0, -2, 1),
        ("v2", 1, -2, 0), ("ctxT", 1, 1, 1), ("s", 1, -2, 0),
        ("q", 2, 1, 1), ("oT", 2, -1, 0),
        ("k", 3, 1, 1), ("y", 3, -1, 0), ("pT", 3, -2, 1),
        ("v", 4, 1, 0), ("av", 4, -2, 1),
        ("z", 5, -2, 0),
        ("x1T", 7, -1, 0), ("x2T", 7, -2, 1)]
LAG = 2
ON_POOL = (1, 4, 6)
WSCALE = 256.0
SLOT_OF = {n: s for n, s, _, _ in MISC}


def valid(h):
    return not isinstance(h, int) or 0 <= h < HALVES


def need(eng, sem, value):
    if not isinstance(value, int) or value > 0:
        eng.wait_ge(sem, value)


def perceiver(nc, x, ctx, mats, rows, sw1, sw2, ew1, ew2, gate_w, out):
    es = ExitStack()
    with es:
        def sb(name, shape, dt=F32):
            return es.enter_context(nc.sbuf_tensor(name, shape, dt))

        def sem(name):
            return es.enter_context(nc.semaphore(name))

        attention = ExitStack()

        def asb(name, shape, dt=F32):
            return attention.enter_context(nc.sbuf_tensor(name, shape, dt))

        x_all = sb("x_all", [P, NT, D])
        x2T_hi = sb("x2T_hi", [P, NT * P], F16)
        x2T_lo = sb("x2T_lo", [P, NT * P], F16)
        ident = sb("ident", [P, P])
        neg_ident = sb("neg_ident", [P, P], BF16)
        ones_row = sb("ones_row", [1, P])
        head_sel = sb("head_sel", [P, GROUPS, JH])
        head_mask = sb("head_mask", [P, JH])
        causal = sb("causal", [P, P])
        minus_half = sb("minus_half", [P, 2])
        eps2 = sb("eps2", [P, 2])
        scratch = sb("scratch", [P, 8])
        row_in = sb("row_in", [len(ROWS), D])
        row1 = sb("row1", [1, 4, D])
        vec = sb("vec", [P, len(ROWS) + E])
        bcast = sb("bcast", [P, 4, D])
        gate_in = sb("gate_in", [E, D])
        gateT = vec[:, len(ROWS):len(ROWS) + E]
        gate_hi = sb("gate_hi", [P, E], F16)
        gate_lo = sb("gate_lo", [P, E], F16)
        iota8 = sb("iota8", [P, E])
        mat_in = asb("mat_in", [P, len(MATS), D])
        WT = asb("WT", [P, len(MATS), D])
        ctx_in = asb("ctx_in", [P, 2, CB, D])
        mv = asb("mv", [P, 4, 2, 2])
        st = asb("st", [P, 4, 2, 6])
        rstd = asb("rstd", [P, 4, 2])
        vpe = asb("vpe", [P, 4, 2])
        xn = asb("xn", [P, 2, D])
        xnT_sb = asb("xnT_sb", [P, 2 * P])
        cT = asb("cT", [P, CB * SK])
        q32 = asb("q32", [P, 2 * P])
        q_hi = asb("q_hi", [P, 2 * P], F16)
        q_lo = asb("q_lo", [P, 2 * P])
        qm_hi = [asb(f"qm_hi{r}", [P, CB, JH, S], F16) for r in range(2)]
        qm_lo = [asb(f"qm_lo{r}", [P, CB, JH, S], F16) for r in range(2)]
        k_hi = [asb(f"k_hi{r}", [P, CB * SK], F16) for r in range(2)]
        k_lo = [asb(f"k_lo{r}", [P, CB * SK], F16) for r in range(2)]
        V_hi = [asb(f"V_hi{r}", [P, CB * HEADS // 2, VW], F16) for r in range(2)]
        V_lo = [asb(f"V_lo{r}", [P, CB * HEADS // 2, VW], F16) for r in range(2)]
        m_bf = asb("m_bf", [P, 2 * UNITS, 4], BF16)
        p32 = asb("p32", [P, 2, 512])
        p_hi = asb("p_hi", [P, 4, 512], F16)
        p_lo = asb("p_lo", [P, 4, 512], F16)
        rden = asb("rden", [P, 2, 16])
        O_tok = asb("O_tok", [P, PAIRS, HEADS // 2, 2, HD])
        OT = asb("OT", [P, 2 * P])
        yb = asb("yb", [P, 2, D])
        yn = asb("yn", [P, 2, D])
        yg = asb("yg", [P, 2, D])
        xb = asb("xb", [P, 2, D])
        x1 = [asb(f"x1_{r}", [P, 2, D]) for r in range(2)]
        x1b = [asb(f"x1b_{r}", [P, 2, D]) for r in range(2)]
        x1n = asb("x1n", [P, 2, D])
        x1T_sb = asb("x1T_sb", [P, 2 * P])
        QT = asb("QT", [P, 2 * P])
        KT = asb("KT", [P, 2 * P])
        V2 = asb("V2", [P, 2, D])
        sm = asb("sm", [P, 2, P])
        smax = asb("smax", [P, 2])
        nbias = asb("nbias", [P, 2])
        rs = asb("rs", [P, 2])
        rrs = asb("rrs", [P, 2])
        P2 = asb("P2", [P, 2, P])
        P2T = asb("P2T", [P, 2 * P])
        AT = asb("AT", [P, 2 * P])
        x2n = asb("x2n", [P, 2, D])
        attention.close()
        w_in = sb("w_in", [P, 2, CH, P])
        W1_hi = sb("W1_hi", [P, NE, HID], F16)
        W1_lo = sb("W1_lo", [P, NE, HID], F16)
        W2_hi = sb("W2_hi", [P, NE, CH, D], F16)
        W2_lo = sb("W2_lo", [P, NE, CH, D], F16)
        lg = sb("lg", [P, NT, E])
        top = sb("top", [P, NT, 8])
        idx = sb("idx", [P, NT, 8], U32)
        idxf = sb("idxf", [P, NT, 2])
        g12 = sb("g12", [P, NT, 2])
        gtmp = sb("gtmp", [P, NT])
        oneh = sb("oneh", [P, NT, E])
        gates = sb("gates", [P, NT, E])
        h32 = [sb(f"h32_{r}", [P, GT * P]) for r in range(RING)]
        h_hi = [sb(f"h_hi{r}", [P, GT * P], F16) for r in range(RING)]
        h_lo = [sb(f"h_lo{r}", [P, GT * P], F16) for r in range(RING)]

        bank = [es.enter_context(nc.psum_tensor(f"bank{n}", [P, 512], F32)) for n in range(8)]
        T_ps = bank[0:2]
        M_ps = bank[2:4]
        PV_ps = bank[4:6]
        X_ps = bank[6:8]
        XB = {n: X_ps[b] for n, _, _, b in MISC}
        U_ps = bank[0:4]
        Y_ps = bank[4:7]

        mats_in, rows_in, x_in, ctx_loaded = sem("mats_in"), sem("rows_in"), sem("x_in"), sem("ctx_loaded")
        w_loaded = [sem(f"w_loaded{r}") for r in range(2)]
        gate_loaded, gate_split = sem("gate_loaded"), sem("gate_split")
        consts, consts_pool = sem("consts"), sem("consts_pool")
        setup_pe, setup_ev, setup_dve = sem("setup_pe"), sem("setup_ev"), sem("setup_dve")
        mm = {n: sem(f"mm_{n}") for n in SLOT_OF}
        ev = {n: sem(f"ev_{n}") for n in SLOT_OF}
        m_done, max_done = sem("m_done"), sem("max_done")
        t_done, exp_done = sem("t_done"), sem("exp_done")
        v_done, norm_done, norm_step = sem("v_done"), sem("norm_done"), sem("norm_step")
        p_hi_done, p_lo_dve, p_lo_pool = sem("p_hi_done"), sem("p_lo_dve"), sem("p_lo_pool")
        q_ready, k_hi_ready, v_hi_ready = sem("q_ready"), sem("k_hi_ready"), sem("v_hi_ready")
        qm_hi_ready, qlo_full, qm_lo_ready = sem("qm_hi_ready"), sem("qlo_full"), sem("qm_lo_ready")
        LN = ["x", "y", "x1", "x2"]
        stat = {n: sem(f"stat_{n}") for n in LN}
        vpe_done = {n: sem(f"vpe_{n}") for n in LN}
        rstd_done = {n: sem(f"rstd_{n}") for n in LN}
        normed = {n: sem(f"normed_{n}") for n in LN}
        xb_done, yg_done, x1_done, x1b_done = sem("xb_done"), sem("yg_done"), sem("x1_done"), sem("x1b_done")
        x2_done = ev["z"]
        sm_max, nbias_done, p2_done, rrs_done = sem("sm_max"), sem("nbias_done"), sem("p2_done"), sem("rrs_done")
        x2T_hi_done = sem("x2T_hi_done")
        wt_pe, wt_hi, wt_lo = sem("wt_pe"), sem("wt_hi"), sem("wt_lo")
        lg_pe, lg_ev, gate_step, gate_exp = sem("lg_pe"), sem("lg_ev"), sem("gate_step"), sem("gate_exp")
        u_done, silu_done, hhi_done, hlo_done = sem("u_done"), sem("silu_done"), sem("hhi_done"), sem("hlo_done")
        d_done, acc_done = sem("d_done"), sem("acc_done")
        stored = sem("stored")

        block = es.enter_context(nc.Block())

        x_v = x.rearrange("(t two) s d -> (two s) t d", two=2)
        out_v = out.rearrange("(t two) s d -> (two s) t d", two=2)
        ctx_v = ctx.rearrange("b k d -> k b d")

        def two_tiles(h):
            return slice(2 * h, 2 * h + 2) if isinstance(h, int) else bass.ds(h * 2, 2)

        def one_tile(h, t):
            return slice(2 * h + t, 2 * h + t + 1) if isinstance(h, int) else bass.ds(h * 2 + t, 1)

        def half_cols(h):
            return slice(2 * P * h, 2 * P * (h + 1)) if isinstance(h, int) else bass.ds(h * (2 * P), 2 * P)

        def all_steps(eng, step):
            for h in range(-2, 2):
                step(h, h % 2)
            with eng.Fori(1, (HALVES - 2) // 2) as i:
                step(i * 2, 0)
                step(i * 2 + 1, 1)
            for h in range(HALVES - 2, HALVES + 2):
                step(h, h % 2)

        def low_of(h, s):
            if s in ON_POOL:
                return p_lo_pool, h * len(ON_POOL) + ON_POOL.index(s) + 1
            others = [n for n in range(UNITS) if n not in ON_POOL]
            return p_lo_dve, h * len(others) + others.index(s) + 1

        def low_part(eng, h, s):
            eng.wait_ge(p_hi_done, UNITS * h + s + 1)
            need(eng, v_done, UNITS * h + s - 3)
            eng.tensor_tensor(p_lo[:, s % 4, :], p32[:, s % 2, :], p_hi[:, s % 4, :],
                              ALU.subtract).then_inc(low_of(h, s)[0], 1)

        def bank_free(eng, name, h):
            at = [n for n, *_ in MISC].index(name)
            own = MISC[at][3]
            for back in list(range(at - 1, -1, -1)) + list(range(len(MISC) - 1, at, -1)):
                n, _, rel, b = MISC[back]
                hh = h + rel - (1 if back > at else 0)
                if b == own and valid(hh):
                    eng.wait_ge(ev[n], (hh + 1) * (2 if n == "z" else 1))
                    return

        @block.sync
        def _(sp):
            for n, m in enumerate(mats):
                sp.dma_start(mat_in[:, n, :], m).then_inc(mats_in, 16)
            def load(h, r):
                tiles = two_tiles(h)
                batches = slice(CB * h, CB * h + CB) if isinstance(h, int) else bass.ds(h * CB, CB)
                need(sp, x_in, 16 * h)
                sp.dma_start(x_all[:, tiles, :], x_v[:, tiles, :]).then_inc(x_in, 16)
                need(sp, mm["ctxT"], h - 1)
                need(sp, ctx_loaded, 16 * h)
                sp.dma_start(ctx_in[:, r, :, :],
                             ctx_v[:, batches, :]).then_inc(ctx_loaded, 16)
            load(0, 0)
            load(1, 1)
            with sp.Fori(1, HALVES // 2) as i:
                load(i * 2, 0)
                load(i * 2 + 1, 1)
            for e in range(NE):
                w1 = ew1[e] if e < E else sw1
                w2 = ew2[e] if e < E else sw2
                if e > 0:
                    sp.wait_ge(wt_pe, 2 * e - 1)
                sp.dma_start(w_in[:, 0, :, :], w1.rearrange("(c p) d -> p c d", p=P)).then_inc(w_loaded[0], 16)
                if e > 0:
                    sp.wait_ge(wt_pe, 2 * e)
                sp.dma_start(w_in[:, 1, :, :], w2.rearrange("d (c h) -> d c h", h=P)).then_inc(w_loaded[1], 16)
            with sp.Fori(0, FG) as i:
                tiles = bass.ds(i * GT, GT)
                sp.wait_ge(acc_done, (i + 1) * (1 + GT * E))
                sp.dma_start(out_v[:, tiles, :], x_all[:, tiles, :]).then_inc(stored, 16)
            sp.wait_ge(stored, 16 * FG)

        @block.gpsimd
        def _(pool):
            pool.dma_start(gate_in[:, :], gate_w).then_inc(gate_loaded, 16)
            pool.memset(ident[:, :], 0.0).then_inc(consts_pool, 1)
            pool.memset(head_sel[:, :, :], 1.0).then_inc(consts_pool, 1)
            pool.memset(causal[:, :], 0.0).then_inc(consts_pool, 1)
            pool.wait_ge(consts_pool, 3)
            pool.affine_select(out=ident[:, :], in_=ident[:, :], compare_op=ALU.not_equal, fill=1.0, base=0,
                               pattern=[[-1, P]], channel_multiplier=1).then_inc(consts_pool, 1)
            pool.affine_select(out=head_sel[:, :, :], in_=head_sel[:, :, :], compare_op=ALU.is_ge, fill=0.0, base=0,
                               pattern=[[-JH * HD, GROUPS], [-HD, JH]], channel_multiplier=1).then_inc(consts_pool, 1)
            pool.affine_select(out=causal[:, :], in_=causal[:, :], compare_op=ALU.is_ge, fill=MASKED, base=0,
                               pattern=[[-1, P]], channel_multiplier=1).then_inc(consts_pool, 1)
            pool.wait_ge(consts_pool, 6)
            pool.affine_select(out=head_sel[:, :, :], in_=head_sel[:, :, :], compare_op=ALU.is_ge, fill=0.0,
                               base=HD - 1, pattern=[[JH * HD, GROUPS], [HD, JH]],
                               channel_multiplier=-1).then_inc(consts_pool, 1)
            pool.wait_ge(consts_pool, 7)
            pool.memset(causal[S:P, 0:S], MASKED).then_inc(consts_pool, 1)
            pool.wait_ge(consts_pool, 8)
            pool.memset(minus_half[:, :], -0.5).then_inc(consts_pool, 1)
            pool.memset(ones_row[:, :], 1.0).then_inc(consts_pool, 1)
            pool.memset(eps2[:, :], EPS).then_inc(consts_pool, 1)
            for r in range(2):
                pool.memset(V_hi[r][:, :, 2 * HD:VW], 1.0).then_inc(consts_pool, 1)
                pool.memset(V_lo[r][:, :, 2 * HD:VW], 0.0).then_inc(consts_pool, 1)
            for e in range(E):
                pool.memset(iota8[:, e:e + 1], float(e)).then_inc(consts_pool, 1)

            def root(n, h):
                i = LN.index(n)
                pool.wait_ge(stat[n], h * 4 + 4)
                need(pool, normed[n], h * 2)
                pool.tensor_tensor(vpe[:, i, :], mv[:, i, :, 1], eps2[:, :], ALU.add).then_inc(vpe_done[n], 1)
                pool.wait_ge(vpe_done[n], h + 1)
                pool.tensor_tensor(rstd[:, i, :], vpe[:, i, :], minus_half[:, :], ALU.pow).then_inc(rstd_done[n], 1)

            def step(h, r):
                for s in range(UNITS):
                    back, hb = (s - 1) % UNITS, h if s else h - 1
                    if back in ON_POOL and valid(hb):
                        low_part(pool, hb, back)
                    if s == 2 and valid(h + 2):
                        root("x", h + 2)
                    if s == 3 and valid(h + 1):
                        pool.wait_ge(q_ready, h + 2)
                        pool.wait_ge(ev["q"], h + 2)
                        need(pool, qm_lo_ready, h + 1)
                        pool.tensor_tensor(q_lo[:, :], q32[:, :], q_hi[:, :], ALU.subtract).then_inc(qlo_full, 1)
                        pool.wait_ge(qlo_full, h + 2)
                        need(pool, t_done, UNITS * h)
                        pool.tensor_tensor(qm_lo[1 - r][:, :, :, :],
                                           q_lo[:, :].rearrange("p (b q) -> p b q", q=S).unsqueeze(2).broadcast_to([P, CB, JH, S]),
                                           head_mask[:, :].unsqueeze(1).unsqueeze(3).broadcast_to([P, CB, JH, S]),
                                           ALU.mult).then_inc(qm_lo_ready, 1)
                    if s == 3 and valid(h - 1):
                        root("y", h - 1)
                    if s == 4 and valid(h - 1):
                        pool.wait_ge(normed["y"], (h - 1) * 2 + 2)
                        pool.tensor_tensor(yg[:, :, :], yn[:, :, :],
                                           bcast[:, 2:3, :].broadcast_to([P, 2, D]), ALU.mult).then_inc(yg_done, 1)
                        pool.wait_ge(yg_done, h)
                        pool.wait_ge(xb_done, h)
                        need(pool, x2_done, (h - 2) * 2)
                        need(pool, normed["x1"], (h - 2) * 2)
                        pool.tensor_tensor(x1[1 - r][:, :, :], yg[:, :, :], xb[:, :, :], ALU.add).then_inc(x1_done, 1)
                    if s == 5 and valid(h - 1):
                        root("x1", h - 1)
                        pool.wait_ge(x1_done, h)
                        pool.tensor_tensor(x1b[1 - r][:, :, :], x1[1 - r][:, :, :],
                                           bcast[:, 1:2, :].broadcast_to([P, 2, D]), ALU.add).then_inc(x1b_done, 1)
                    if s == 5 and valid(h - 2):
                        root("x2", h - 2)
                    if s == 7 and valid(h):
                        pool.wait_ge(x_in, (h + 1) * 16)
                        need(pool, x1_done, h)
                        pool.tensor_tensor(xb[:, :, :], x_all[:, two_tiles(h), :],
                                           bcast[:, 3:4, :].broadcast_to([P, 2, D]), ALU.add).then_inc(xb_done, 1)
            pool.wait_ge(setup_dve, 3)
            all_steps(pool, step)

        @block.scalar
        def _(act):
            for n, v in enumerate(rows):
                act.dma_start(row_in[n:n + 1, :], v.rearrange("(a n) -> a n", a=1)).then_inc(rows_in, 16)
            for n, name in enumerate(("xbo", "abo", "gamma", "beta")):
                act.dma_start(row1[:, n, :], rows[ROWS.index(name)].rearrange("(a n) -> a n", a=1)).then_inc(rows_in, 16)
            for n in range(2):
                act.wait_ge(setup_pe, n + 1)
                act.activation(WT[:, 4 * n:4 * n + 4, :], X_ps[n][:, :], ACT.Copy).then_inc(setup_ev, 1)
            act.wait_ge(setup_pe, 3)
            act.activation(vec[:, :], X_ps[0][:, 0:len(ROWS) + E], ACT.Copy).then_inc(setup_ev, 1)
            act.wait_ge(setup_pe, 4)
            act.activation(bcast[:, :, :], X_ps[1][:, :], ACT.Copy).then_inc(setup_ev, 1)
            act.wait_ge(setup_ev, 3)

            def col(name):
                n = ROWS.index(name)
                return vec[:, n:n + 1]

            def evacuate(name, h, dst, src, func=ACT.Copy, **kw):
                act.wait_ge(mm[name], h + 1)
                act.activation(dst, src, func, **kw).then_inc(ev[name], 1)

            def step(h, r):
                a, b, c = h + 1, h - 1, h - 2
                for s in range(UNITS):
                    u = UNITS * h + s
                    if valid(h):
                        act.wait_ge(t_done, u + 1)
                        hl, sl = (h, s - 2) if s > 1 else (h - 1, s + UNITS - 2)
                        if valid(hl):
                            act.wait_ge(*low_of(hl, sl))
                        act.activation(p32[:, s % 2, :], T_ps[s % 2][:, :], ACT.Exp,
                                       scale=XSCALE).then_inc(exp_done, 1)
                    if s == 0 and valid(a):
                        need(act, mm["q"], a)
                        evacuate("xnT", a, xnT_sb[:, :], XB["xnT"][:, 0:2 * P])
                    if s == 0 and valid(c):
                        act.wait_ge(mm["qk"], c + 1)
                        need(act, mm["s"], c)
                        act.activation(QT[:, :], XB["qk"][:, 0:2 * P], ACT.Identity, bias=col("abq"))
                        act.activation(KT[:, :], XB["qk"][:, 2 * P:4 * P], ACT.Identity, bias=col("abk")).then_inc(ev["qk"], 1)
                    if s == 1 and valid(c):
                        need(act, mm["av"], c)
                        evacuate("v2", c, V2[:, :, :], XB["v2"][:, 0:2 * P])
                    if s == 1 and valid(a):
                        need(act, mm["v"], a)
                        evacuate("ctxT", a, cT[:, :], XB["ctxT"][:, :])
                    if s == 2 and valid(a):
                        act.wait_ge(mm["q"], a + 1)
                        need(act, qm_lo_ready, a)
                        need(act, qm_hi_ready, JH * a)
                        act.activation(q32[:, :], XB["q"][:, 0:2 * P], ACT.Identity, bias=col("xbq")).then_inc(q_ready, 1)
                        act.activation(q_hi[:, :], XB["q"][:, 0:2 * P], ACT.Identity,
                                       bias=col("xbq")).then_inc(ev["q"], 1)
                    if s == 2 and valid(c):
                        act.wait_ge(nbias_done, c + 1)
                        need(act, mm["pT"], c)
                        for t in range(2):
                            act.activation(P2[:, t, :], sm[:, t, :], ACT.Exp, bias=nbias[:, t:t + 1], scale=ASCALE,
                                           accum_out=rs[:, t:t + 1]).then_inc(p2_done, 1)
                    if s == 2 and valid(b):
                        need(act, mm["y"], b)
                        evacuate("oT", b, OT[:, :], XB["oT"][:, 0:2 * P])
                    if s == 3 and valid(a):
                        act.wait_ge(mm["k"], a + 1)
                        need(act, t_done, UNITS * (a - 1))
                        act.activation(k_hi[1 - r][:, :], XB["k"][:, :], ACT.Identity, bias=col("xbk")).then_inc(k_hi_ready, 1)
                    if s == 3 and valid(c):
                        need(act, mm["av"], c)
                        evacuate("pT", c, P2T[:, :], XB["pT"][:, 0:2 * P])
                    if s == 4 and valid(a):
                        act.wait_ge(mm["v"], a + 1)
                        need(act, v_done, UNITS * (a - 1))
                        act.activation(V_hi[1 - r][:, :, 0:2 * HD], XB["v"][:, :].rearrange("p (n w) -> p n w", w=2 * HD),
                                       ACT.Copy).then_inc(v_hi_ready, 1)
                    if s == 4 and valid(c):
                        need(act, mm["z"], c)
                        evacuate("av", c, AT[:, :], XB["av"][:, 0:2 * P])
                    if s == 7 and valid(b):
                        need(act, mm["v2"], b)
                        evacuate("x1T", b, x1T_sb[:, :], XB["x1T"][:, 0:2 * P])
                    if s == 7 and valid(c):
                        act.wait_ge(mm["x2T"], c + 1)
                        act.activation(x2T_hi[:, half_cols(c)], XB["x2T"][:, 0:2 * P], ACT.Copy).then_inc(x2T_hi_done, 1)
                    if valid(h):
                        act.wait_ge(exp_done, u + 1)
                        need(act, v_done, u - 3)
                        act.activation(p_hi[:, s % 4, :], p32[:, s % 2, :], ACT.Copy).then_inc(p_hi_done, 1)
            all_steps(act, step)
            act.wait_ge(gate_step, 1)
            act.activation(gtmp[:, :], g12[:, :, 0], ACT.Exp).then_inc(gate_exp, 1)
            for n in range(2 * NE):
                act.wait_ge(wt_pe, n + 1)
                dst = (W1_hi[:, n // 2, :], W2_hi[:, n // 2, :, :])[n % 2]
                act.activation(dst, X_ps[n % 2][:, :], ACT.Copy, scale=WSCALE).then_inc(wt_hi, 1)

            def split(i, k):
                n = i * NK + k
                act.wait_ge(silu_done, n + 1)
                need(act, d_done, n - RING + 1)
                act.activation(h_hi[k % RING][:, :], h32[k % RING][:, :], ACT.Copy).then_inc(hhi_done, 1)

            def feed(i, last=False):
                for k in range(NK):
                    n = i * NK + k
                    act.wait_ge(u_done, n + 1)
                    need(act, hlo_done, n - RING + 1)
                    act.activation(h32[k % RING][:, :], U_ps[k % 4][:, :], ACT.Silu, scale=1.0 / WSCALE).then_inc(silu_done, 1)
                    if k > 0:
                        split(i, k - 1)
                split(i, NK - 1)
            feed(0)
            with act.Fori(1, FG) as i:
                feed(i)

        @block.vector
        def _(dve):
            dve.wait_ge(consts_pool, CONSTS)
            dve.tensor_reduce(head_mask[:, :], head_sel[:, :, :].rearrange("p a j -> p j a"), AX.X,
                              ALU.add).then_inc(setup_dve, 1)
            dve.tensor_scalar(neg_ident[:, :], ident[:, :], -1.0, None, ALU.mult).then_inc(setup_dve, 1)
            dve.wait_ge(setup_ev, 3)
            dve.tensor_scalar(gate_hi[:, :], gateT, WSCALE, None, ALU.mult).then_inc(gate_split, 1)
            dve.wait_ge(gate_split, 1)
            dve.scalar_tensor_tensor(gate_lo[:, :], gateT, WSCALE, gate_hi[:, :], ALU.mult, ALU.subtract).then_inc(gate_split, 1)
            dve.wait_ge(setup_ev, 4)
            dve.wait_ge(setup_pe, 5)
            dve.tensor_tensor(bcast[:, 0:2, :], bcast[:, 0:2, :],
                              X_ps[0][:, 0:2 * D].rearrange("p (n d) -> p n d", d=D), ALU.add).then_inc(setup_dve, 1)

            def statistics(n, h, src):
                i = LN.index(n)
                need(dve, normed[n], h * 2)
                dve.memset(scratch[:, 2 * i:2 * i + 1], 0.0)
                for t in range(2):
                    dve.bn_stats(st[:, i, t, :], src[:, t, :]).then_inc(stat[n], 1)
                dve.wait_ge(stat[n], h * 4 + 2)
                dve.memset(scratch[:, 2 * i + 1:2 * i + 2], 0.0)
                for t in range(2):
                    dve.bn_aggr(mv[:, i, t, :], st[:, i, t, :]).then_inc(stat[n], 1)

            def normalise(n, h, src, dst):
                i = LN.index(n)
                dve.wait_ge(rstd_done[n], h + 1)
                dve.wait_ge(stat[n], h * 4 + 4)
                for t in range(2):
                    dve.tensor_scalar(dst[:, t, :], src[:, t, :], mv[:, i, t, 0:1], rstd[:, i, t:t + 1],
                                      ALU.subtract, ALU.mult).then_inc(normed[n], 1)

            def normalise_pair(h, p):
                dve.wait_ge(v_done, UNITS * h + GROUPS * (p + 1))
                need(dve, norm_done, h * 2 + p)
                pv = PV_ps[p][:, 0:16 * VW].rearrange("p (n w) -> p n w", w=VW)
                dve.reciprocal(rden[:, p, :], pv[:, :, 2 * HD]).then_inc(norm_step, 1)
                dve.wait_ge(norm_step, h * 2 + p + 1)
                need(dve, mm["oT"], h)
                for b in range(2):
                    for o in range(2):
                        rows_ = slice(S * o, S * o + S)
                        last = dve.tensor_tensor(
                            O_tok[S * b:S * b + S, p, :, o, :], pv[rows_, 8 * b:8 * b + 8, HD * o:HD * o + HD],
                            rden[rows_, p, 8 * b:8 * b + 8].unsqueeze(2).broadcast_to([S, 8, HD]), ALU.mult)
                last.then_inc(norm_done, 1)

            def step(h, r):
                a, b, c = h + 1, h - 1, h - 2
                for s in range(UNITS):
                    hm, u = (h, UNITS * h + s + 2)
                    if s >= UNITS - 2:
                        hm = h + 1
                    if valid(hm):
                        dve.wait_ge(m_done, u + 1)
                        need(dve, t_done, u + 1 - 2 * UNITS)
                        slot = (r * UNITS + s + 2) % (2 * UNITS)
                        dve.tensor_reduce(m_bf[:, slot, :], M_ps[s % 2][:, :].rearrange("p (n k) -> p n k", k=SK),
                                          AX.X, ALU.max).then_inc(max_done, 1)
                    back, hb = (s - 1) % UNITS, h if s else h - 1
                    if back not in ON_POOL and valid(hb):
                        low_part(dve, hb, back)
                    if s == 1 and valid(b):
                        normalise_pair(b, 1)
                    if s == 5 and valid(h):
                        normalise_pair(h, 0)
                    if s == 1 and valid(c):
                        dve.wait_ge(mm["s"], c + 1)
                        need(dve, p2_done, 2 * c)
                        dve.tensor_tensor(sm[:, :, :], XB["s"][:, 0:2 * P].rearrange("p (t k) -> p t k", k=P),
                                          causal[:, :].unsqueeze(1).broadcast_to([P, 2, P]), ALU.add).then_inc(ev["s"], 1)
                        dve.wait_ge(ev["s"], c + 1)
                        dve.tensor_reduce(smax[:, :], sm[:, :, :], AX.X, ALU.max).then_inc(sm_max, 1)
                        dve.wait_ge(sm_max, c + 1)
                        dve.tensor_scalar(nbias[:, :], smax[:, :], -ASCALE, None, ALU.mult).then_inc(nbias_done, 1)
                    if s == 0 and valid(h + 2):
                        dve.wait_ge(x_in, (h + 3) * 16)
                        statistics("x", h + 2, x_all[:, two_tiles(h + 2), :])
                    if s == 3 and valid(b):
                        dve.wait_ge(mm["y"], b + 1)
                        need(dve, normed["y"], 2 * b)
                        dve.tensor_tensor(yb[:, :, :], XB["y"][:, 0:2 * P].rearrange("p (t k) -> p t k", k=P),
                                          bcast[:, 0:1, :].broadcast_to([P, 2, D]), ALU.add).then_inc(ev["y"], 1)
                        dve.wait_ge(ev["y"], b + 1)
                        statistics("y", b, yb)
                    if s == 3 and valid(c):
                        dve.wait_ge(p2_done, 2 * c + 2)
                        need(dve, x2_done, 2 * c)
                        dve.reciprocal(rrs[:, :], rs[:, :]).then_inc(rrs_done, 1)
                    if s == 3 and valid(a):
                        dve.wait_ge(ev["q"], a + 1)
                        need(dve, t_done, UNITS * (a - 1))
                        for j in range(JH):
                            dve.tensor_scalar(qm_hi[1 - r][:, :, j, :],
                                              q_hi[:, :].rearrange("p (b q) -> p b q", q=S),
                                              head_mask[:, j:j + 1], None, ALU.mult).then_inc(qm_hi_ready, 1)
                        dve.wait_ge(k_hi_ready, a + 1)
                        dve.scalar_tensor_tensor(k_lo[1 - r][:, :], XB["k"][:, :], vec[:, 1:2],
                                                 k_hi[1 - r][:, :], ALU.add, ALU.subtract).then_inc(ev["k"], 1)
                    if s == 4 and valid(a):
                        dve.wait_ge(v_hi_ready, a + 1)
                        dve.tensor_tensor(V_lo[1 - r][:, :, 0:2 * HD], XB["v"][:, :].rearrange("p (n w) -> p n w", w=2 * HD),
                                          V_hi[1 - r][:, :, 0:2 * HD], ALU.subtract).then_inc(ev["v"], 1)
                    if s == 4 and valid(b):
                        need(dve, yg_done, b)
                        normalise("y", b, yb, yn)
                    if s == 5 and valid(c):
                        dve.wait_ge(mm["z"], c + 1)
                        dve.wait_ge(rrs_done, c + 1)
                        dve.wait_ge(x1b_done, c + 1)
                        for t in range(2):
                            last = dve.scalar_tensor_tensor(x_all[:, one_tile(c, t), :].rearrange("p t d -> p (t d)"),
                                                            XB["z"][:, t * P:t * P + P],
                                                            rrs[:, t:t + 1], x1b[r][:, t, :], ALU.mult, ALU.add)
                            last.then_inc(x2_done, 1)
                        dve.wait_ge(x2_done, 2 * c + 2)
                        statistics("x2", c, x_all[:, two_tiles(c), :])
                    if s == 5 and valid(b):
                        dve.wait_ge(x1_done, b + 1)
                        statistics("x1", b, x1[1 - r])
                    if s == 5 and valid(h + 2):
                        dve.wait_ge(mm["xnT"], h + 2)
                        normalise("x", h + 2, x_all[:, two_tiles(h + 2), :], xn)
                    if s == 6 and valid(b):
                        need(dve, mm["x1T"], b)
                        normalise("x1", b, x1[1 - r], x1n)
                    if s == 6 and valid(c):
                        need(dve, mm["x2T"], c)
                        normalise("x2", c, x_all[:, two_tiles(c), :], x2n)
                    if s == 7 and valid(c):
                        dve.wait_ge(x2T_hi_done, c + 1)
                        dve.tensor_tensor(x2T_lo[:, half_cols(c)], XB["x2T"][:, 0:2 * P],
                                          x2T_hi[:, half_cols(c)], ALU.subtract).then_inc(ev["x2T"], 1)
            all_steps(dve, step)

            dve.wait_ge(lg_pe, 1)
            dve.tensor_scalar(lg[:, :, :], X_ps[0][:, 0:NT * E].rearrange("p (t e) -> p t e", e=E), 1.0 / WSCALE, None,
                              ALU.mult).then_inc(lg_ev, 1)
            dve.wait_ge(lg_ev, 1)
            for t in range(NT):
                dve.max(top[:, t, :], lg[:, t, :]).then_inc(lg_ev, 1)
            dve.wait_ge(lg_ev, 1 + NT)
            for t in range(NT):
                dve.max_index(idx[:, t, :], top[:, t, :], lg[:, t, :]).then_inc(lg_ev, 1)
            dve.tensor_tensor(g12[:, :, 0], top[:, :, 1], top[:, :, 0], ALU.subtract).then_inc(gate_step, 1)
            dve.wait_ge(lg_ev, 1 + 2 * NT)
            dve.tensor_copy(idxf[:, :, :], idx[:, :, 0:2]).then_inc(gate_step, 1)
            dve.wait_ge(gate_exp, 1)
            dve.tensor_scalar(g12[:, :, 1], gtmp[:, :], 1.0, None, ALU.add).then_inc(gate_step, 1)
            dve.wait_ge(gate_step, 3)
            dve.reciprocal(g12[:, :, 0], g12[:, :, 1]).then_inc(gate_step, 1)
            dve.wait_ge(gate_step, 4)
            dve.tensor_tensor(g12[:, :, 1], g12[:, :, 0], gtmp[:, :], ALU.mult).then_inc(gate_step, 1)
            dve.wait_ge(gate_step, 5)
            for n in range(2):
                dst = (gates, oneh)[n]
                dve.tensor_tensor(dst[:, :, :], iota8[:, :].unsqueeze(1).broadcast_to([P, NT, E]),
                                  idxf[:, :, n].unsqueeze(2).broadcast_to([P, NT, E]), ALU.is_equal).then_inc(gate_step, 1)
            dve.wait_ge(gate_step, 7)
            for n in range(2):
                dst = (gates, oneh)[n]
                dve.tensor_tensor(dst[:, :, :], dst[:, :, :],
                                  g12[:, :, n].unsqueeze(2).broadcast_to([P, NT, E]), ALU.mult).then_inc(gate_step, 1)
            dve.wait_ge(gate_step, 9)
            dve.tensor_tensor(gates[:, :, :], gates[:, :, :], oneh[:, :, :], ALU.add).then_inc(gate_step, 1)
            dve.wait_ge(gate_step, 10)
            dve.tensor_scalar(gates[:, :, :], gates[:, :, :], 1.0 / WSCALE, None, ALU.mult).then_inc(gate_step, 1)
            for n in range(2 * NE):
                dve.wait_ge(wt_hi, n + 1)
                lo = (W1_lo[:, n // 2, :], W2_lo[:, n // 2, :, :])[n % 2]
                hi = (W1_hi[:, n // 2, :], W2_hi[:, n // 2, :, :])[n % 2]
                src = X_ps[0][:, :] if n % 2 == 0 else X_ps[1][:, :].rearrange("p (c d) -> p c d", d=D)
                dve.scalar_tensor_tensor(lo, src, WSCALE, hi, ALU.mult, ALU.subtract).then_inc(wt_lo, 1)
            dve.wait_ge(gate_step, 11)

            def add_up(i, e):
                dve.wait_ge(d_done, i * NK + CH * (e + 1))
                base = i * (1 + GT * E)
                if e == 0:
                    tiles = x_all[:, bass.ds(i * GT, GT) if not isinstance(i, int) else slice(i * GT, (i + 1) * GT), :]
                    dve.scalar_tensor_tensor(tiles, Y_ps[0][:, :].rearrange("p (t d) -> p t d", d=D), 1.0 / WSCALE, tiles,
                                             ALU.mult, ALU.add).then_inc(acc_done, 1)
                    return
                dve.wait_ge(acc_done, base + 1 + GT * (e - 1))
                for t in range(GT):
                    tile = x_all[:, at(i * GT + t), :].rearrange("p t d -> p (t d)")
                    gate = gates[:, at(i * GT + t), e - 1]
                    last = dve.scalar_tensor_tensor(tile, Y_ps[e % 3][:, t * D:t * D + D], gate, tile,
                                                    ALU.mult, ALU.add)
                    last.then_inc(acc_done, 1)

            def at(n):
                return slice(n, n + 1) if isinstance(n, int) else bass.ds(n, 1)

            def feed(i):
                for k in range(NK):
                    n = i * NK + k
                    dve.wait_ge(hhi_done, n + 1)
                    need(dve, d_done, n - RING + 1)
                    dve.tensor_tensor(h_lo[k % RING][:, :], h32[k % RING][:, :], h_hi[k % RING][:, :],
                                      ALU.subtract).then_inc(hlo_done, 1)
                    if k % CH == 1 and k > CH:
                        add_up(i, k // CH - 1)
                add_up(i, NE - 1)
            feed(0)
            with dve.Fori(1, FG) as i:
                feed(i)

        @block.tensor
        def _(pe):
            pe.wait_ge(consts_pool, CONSTS)
            pe.wait_ge(mats_in, 16 * len(MATS))
            for n in range(2):
                for m in range(4):
                    last = pe.transpose(X_ps[n][:, m * P:m * P + P], mat_in[:, 4 * n + m, :], ident[:, :])
                last.then_inc(setup_pe, 1)
            pe.wait_ge(rows_in, 16 * (len(ROWS) + 4))
            pe.wait_ge(gate_loaded, 16)
            pe.wait_ge(setup_ev, 1)
            nv = len(ROWS)
            pe.transpose(X_ps[0][:, 0:nv], row_in[:, :], ident[0:nv, 0:nv])
            pe.transpose(X_ps[0][:, nv:nv + E], gate_in[:, :], ident[0:E, 0:E]).then_inc(setup_pe, 1)
            pe.wait_ge(setup_ev, 2)
            pe.matmul(X_ps[1][:, :], ones_row[:, :], row1[:, :, :], start=True, stop=True).then_inc(setup_pe, 1)
            pe.wait_ge(setup_ev, 3)
            for n, (bv, wo) in enumerate((("xbv", "xWo"), ("abv", "aWo"))):
                c = ROWS.index(bv)
                last = pe.matmul(X_ps[0][:, n * D:n * D + D], vec[:, c:c + 1].broadcast_to([P, P]),
                                 WT[:, MATS.index(wo), :], start=True, stop=True)
            last.then_inc(setup_pe, 1)
            pe.wait_ge(setup_ev, 4)
            pe.wait_ge(setup_dve, 3)

            def W(name):
                return WT[:, MATS.index(name), :]

            def shared_bank(name, h):
                x = XB[name]
                if name == "xnT":
                    pe.wait_ge(normed["x"], 2 * h + 2)
                    for t in range(2):
                        last = pe.transpose(x[:, t * P:t * P + P], xn[:, t, :], ident[:, :])
                if name == "ctxT":
                    pe.wait_ge(ctx_loaded, 16 * h + 16)
                    for b in range(CB):
                        last = pe.transpose(x[:, b * P:b * P + P], ctx_in[:, parity["a"], b, :], ident[:, :])
                if name == "q":
                    pe.wait_ge(ev["xnT"], h + 1)
                    last = pe.matmul(x[:, 0:2 * P], W("xWq"), xnT_sb[:, :], start=True, stop=True)
                if name == "k":
                    pe.wait_ge(ev["ctxT"], h + 1)
                    last = pe.matmul(x[:, :], W("xWk"), cT[:, :], start=True, stop=True)
                if name == "v":
                    for b in range(CB):
                        last = pe.matmul(x[:, b * D:b * D + D], cT[:, b * SK:b * SK + SK], W("xWv"), start=True, stop=True)
                if name == "oT":
                    pe.wait_ge(norm_done, 2 * h + 2)
                    for t in range(2):
                        last = pe.transpose(x[:, t * P:t * P + P],
                                            O_tok[:, t, :, :, :].rearrange("p t o d -> p (t o d)"), ident[:, :])
                if name == "y":
                    pe.wait_ge(ev["oT"], h + 1)
                    for t in range(2):
                        last = pe.matmul(x[:, t * D:t * D + D], OT[:, t * P:t * P + P], W("xWo"), start=True, stop=True)
                if name == "x1T":
                    pe.wait_ge(normed["x1"], 2 * h + 2)
                    for t in range(2):
                        last = pe.transpose(x[:, t * P:t * P + P], x1n[:, t, :], ident[:, :])
                if name == "qk":
                    pe.wait_ge(ev["x1T"], h + 1)
                    pe.matmul(x[:, 0:2 * P], W("aWq"), x1T_sb[:, :], start=True, stop=True)
                    last = pe.matmul(x[:, 2 * P:4 * P], W("aWk"), x1T_sb[:, :], start=True, stop=True)
                if name == "v2":
                    for t in range(2):
                        last = pe.matmul(x[:, t * D:t * D + D], x1T_sb[:, t * P:t * P + P], W("aWv"), start=True, stop=True)
                if name == "s":
                    pe.wait_ge(ev["qk"], h + 1)
                    for t in range(2):
                        last = pe.matmul(x[:, t * P:t * P + P], QT[:, t * P:t * P + P], KT[:, t * P:t * P + P],
                                         start=True, stop=True)
                if name == "pT":
                    pe.wait_ge(p2_done, 2 * h + 2)
                    for t in range(2):
                        last = pe.transpose(x[:, t * P:t * P + P], P2[:, t, :], ident[:, :])
                if name == "av":
                    pe.wait_ge(ev["pT"], h + 1)
                    pe.wait_ge(ev["v2"], h + 1)
                    for t in range(2):
                        last = pe.matmul(x[:, t * P:t * P + P], V2[:, t, :], P2T[:, t * P:t * P + P], start=True, stop=True)
                if name == "z":
                    pe.wait_ge(ev["av"], h + 1)
                    for t in range(2):
                        last = pe.matmul(x[:, t * D:t * D + D], AT[:, t * P:t * P + P], W("aWo"), start=True, stop=True)
                if name == "x2T":
                    pe.wait_ge(normed["x2"], 2 * h + 2)
                    for t in range(2):
                        last = pe.transpose(x[:, t * P:t * P + P], x2n[:, t, :], ident[:, :])
                last.then_inc(mm[name], 1)

            parity = {}

            def step(h, r):
                parity["a"] = 1 - r
                for s in range(UNITS):
                    u, p, g = UNITS * h + s, s // GROUPS, s % GROUPS
                    rows_ = slice(g * 32, g * 32 + 32)
                    if valid(h):
                        pe.wait_ge(max_done, u + 1)
                        need(pe, exp_done, u - 1)
                        if s == 0:
                            pe.wait_ge(qm_lo_ready, h + 1)
                            pe.wait_ge(ev["k"], h + 1)
                        for n in range(4):
                            pe.matmul(T_ps[s % 2][:, n * P:n * P + P],
                                      m_bf[:, r * UNITS + s, n:n + 1].broadcast_to([P, P]), neg_ident[:, :],
                                      start=(n == 0), stop=False)
                        for b in range(2):
                            cb = 2 * p + b
                            for n, (kk, qq) in enumerate(((k_hi, qm_hi), (k_hi, qm_lo), (k_lo, qm_hi))):
                                last = pe.matmul(T_ps[s % 2][:, b * 256:b * 256 + 256],
                                                 kk[r][rows_, cb * SK:cb * SK + SK],
                                                 qq[r][rows_, cb, :, :].rearrange("p j q -> p (j q)"),
                                                 start=False, stop=(b == 1 and n == 2))
                        last.then_inc(t_done, 1)
                    hm, sm_ = (h, s + 2) if s < UNITS - 2 else (h + 1, s + 2 - UNITS)
                    if valid(hm):
                        rm = r if sm_ == s + 2 else 1 - r
                        pm, gm = sm_ // GROUPS, sm_ % GROUPS
                        if sm_ == 0:
                            pe.wait_ge(qm_hi_ready, JH * (hm + 1))
                            pe.wait_ge(k_hi_ready, hm + 1)
                        need(pe, max_done, u + 1)
                        mrows = slice(gm * 32, gm * 32 + 32)
                        for b in range(2):
                            cb = 2 * pm + b
                            for jp in range(2):
                                last = pe.matmul(M_ps[s % 2][:, (2 * b + jp) * P:(2 * b + jp) * P + P],
                                                 qm_hi[rm][mrows, cb, 2 * jp:2 * jp + 2, :].rearrange("p j q -> p (j q)"),
                                                 k_hi[rm][mrows, cb * SK:cb * SK + SK], start=True, stop=True)
                        last.then_inc(m_done, 1)
                    hv, sv = (h, s - LAG) if s >= LAG else (h - 1, s - LAG + UNITS)
                    if valid(hv):
                        rv = r if s >= LAG else 1 - r
                        pv, gv = sv // GROUPS, sv % GROUPS
                        pe.wait_ge(*low_of(hv, sv))
                        if sv == 0:
                            pe.wait_ge(ev["v"], hv + 1)
                        if gv == 0:
                            need(pe, norm_done, hv * 2 + pv - 1)
                        for b in range(2):
                            for jp in range(2):
                                t = 2 * gv + jp
                                c0 = (b * 8 + t) * VW
                                w0 = (2 * b + jp) * P
                                for n, (pp, vv) in enumerate(((p_hi, V_hi), (p_hi, V_lo), (p_lo, V_hi))):
                                    last = pe.matmul(PV_ps[pv][:, c0:c0 + VW], pp[:, sv % 4, w0:w0 + P],
                                                     vv[rv][:, (2 * pv + b) * 8 + t, :], start=(n == 0), stop=(n == 2))
                        last.then_inc(v_done, 1)
                    for name, slot, rel, _ in MISC:
                        if slot == s and valid(h + rel):
                            bank_free(pe, name, h)
                            shared_bank(name, h + rel)
            all_steps(pe, step)
            pe.wait_ge(gate_split, 2)

            for name in ("x2T", "x1T", "z"):
                pe.wait_ge(ev[name], HALVES)
            for t in range(NT):
                for n, (part, g) in enumerate(((x2T_hi, gate_hi), (x2T_hi, gate_lo), (x2T_lo, gate_hi))):
                    last = pe.matmul(X_ps[0][:, t * E:t * E + E], part[:, t * P:t * P + P], g[:, :],
                                     start=(n == 0), stop=(n == 2))
            last.then_inc(lg_pe, 1)
            for n in range(2 * NE):
                pe.wait_ge(w_loaded[n % 2], 16 * (n // 2 + 1))
                if n == 0:
                    pe.wait_ge(lg_ev, 1)
                need(pe, wt_lo, n - 1)
                for c in range(CH):
                    last = pe.transpose(X_ps[n % 2][:, c * P:c * P + P], w_in[:, n % 2, c, :], ident[:, :])
                last.then_inc(wt_pe, 1)
            pe.wait_ge(wt_lo, 2 * NE)

            def cols(i):
                return slice(GT * P * i, GT * P * (i + 1)) if isinstance(i, int) else bass.ds(i * (GT * P), GT * P)

            def expert(n):
                return E if n == 0 else n - 1

            def up(i, k):
                n = i * NK + k
                e, c = expert(k // CH), k % CH
                need(pe, silu_done, n - 3)
                for m, (w, xx) in enumerate(((W1_hi, x2T_hi), (W1_hi, x2T_lo), (W1_lo, x2T_hi))):
                    last = pe.matmul(U_ps[k % 4][:, :], w[:, e, c * P:c * P + P], xx[:, cols(i)],
                                     start=(m == 0), stop=(m == 2))
                last.then_inc(u_done, 1)

            def down(i, k):
                n = i * NK + k
                ei, c = k // CH, k % CH
                e = expert(ei)
                if c == 0:
                    if ei < 3:
                        need(pe, acc_done, (i - 1) * (1 + GT * E) + 1 + GT * (ei + 6))
                    else:
                        pe.wait_ge(acc_done, i * (1 + GT * E) + 1 + GT * (ei - 3))
                pe.wait_ge(hhi_done, n + 1)
                pe.wait_ge(hlo_done, n + 1)
                for t in range(GT):
                    for m, (hh, w) in enumerate(((h_hi, W2_hi), (h_hi, W2_lo), (h_lo, W2_hi))):
                        last = pe.matmul(Y_ps[ei % 3][:, t * D:t * D + D], hh[k % RING][:, t * P:t * P + P], w[:, e, c, :],
                                         start=(c == 0 and t == 0 and m == 0),
                                         stop=(c == CH - 1 and t == GT - 1 and m == 2))
                last.then_inc(d_done, 1)

            AHEAD = 2

            def feed(i, more):
                for k in range(NK):
                    if k + AHEAD < NK:
                        up(i, k + AHEAD)
                    elif more:
                        up(i + 1, k + AHEAD - NK)
                    down(i, k)
            for k in range(AHEAD):
                up(0, k)
            feed(0, True)
            with pe.Fori(1, FG - 1) as i:
                feed(i, True)
            feed(FG - 1, False)

    return nc


_NAMES = {"xWq": "L0_xattn_Wq", "xWk": "L0_xattn_Wk", "xWv": "L0_xattn_Wv", "xWo": "L0_xattn_Wo",
          "aWq": "L0_attn_Wq", "aWk": "L0_attn_Wk", "aWv": "L0_attn_Wv", "aWo": "L0_attn_Wo",
          "xbq": "L0_xattn_bq", "xbk": "L0_xattn_bk", "xbv": "L0_xattn_bv", "xbo": "L0_xattn_bo",
          "abq": "L0_attn_bq", "abk": "L0_attn_bk", "abv": "L0_attn_bv", "abo": "L0_attn_bo",
          "gamma": "L0_xattn_gamma", "beta": "L0_xattn_beta"}


def kernel(**inputs):
    import concourse.bacc as bacc
    from concourse.bass_utils import run_bass_kernel_spmd

    nc = bacc.Bacc("TRN2", target_bir_lowering=False, num_devices=1)
    arrays, aps = {}, {}
    for name, a in inputs.items():
        a = np.ascontiguousarray(a)
        arrays["in_" + name] = a
        aps[name] = nc.dram_tensor("in_" + name, a.shape, mybir.dt.from_np(a.dtype), kind="ExternalInput").ap()
    out = nc.dram_tensor("out_0", (B, S, D), F32, kind="ExternalOutput").ap()
    perceiver(nc, aps["x"], aps["ctx_1024"], [aps[_NAMES[n]] for n in MATS], [aps[_NAMES[n]] for n in ROWS],
              aps["L0_ffn_shared_w1"], aps["L0_ffn_shared_w2"], aps["L0_ffn_experts_w1"],
              aps["L0_ffn_experts_w2"], aps["L0_ffn_gate_w"], out)
    r = run_bass_kernel_spmd(nc, [arrays], core_ids=[0])
    return r.results[0]["out_0"]
```

```python
import numpy as np
import concourse.bass as bass
from concourse import mybir
from contextlib import ExitStack

F32 = mybir.dt.float32
F16 = mybir.dt.float16
BF16 = mybir.dt.bfloat16
U32 = mybir.dt.uint32
I32 = mybir.dt.int32
ALU = mybir.AluOpType
ACT = mybir.ActivationFunctionType
AX = mybir.AxisListType

B, S, SK, D = 64, 64, 128, 128
HEADS = 16
HD = D // HEADS
P = 128
EPS = 1e-5
E, HID = 8, 512
XSCALE = float(HD) ** -0.5
ASCALE = float(D) ** -0.5
MASKED = -1e30
CONSTS = 57

NT = B * S // P
HALVES = 16
PAIRS = 2
CB = 4
GROUPS = 4
JH = 4
UNITS = PAIRS * GROUPS
VW = 2 * HD + 1
NE = E + 1
CH = HID // P
RING = 4

GT = 4
FG = NT // GT
BEFORE = FG // 2
BT = 2
BR = BT * P
U_N = GT * P
BU = CH // 2
T = B * S
REGION = T + BR
ROW = D + 2
BLOCKS = -(-((2 * T + E * (BR - 1)) // BR) // 8) * 8
LB = 8
N0 = BEFORE * CH
N1 = N0 + BLOCKS * BU
NU = N1 + (FG - BEFORE) * CH
NOWHERE = 1 << 20

ROWS = ["xbq", "xbk", "xbv", "xbo", "abq", "abk", "abv", "abo", "gamma", "beta"]
MATS = ["xWq", "xWk", "xWv", "xWo", "aWq", "aWk", "aWv", "aWo"]

MISC = [("xnT", 0, 1, 0), ("qk", 0, -2, 1),
        ("v2", 1, -2, 0), ("s", 1, -2, 1),
        ("q", 2, 1, 0), ("oT", 2, -1, 1),
        ("ctxT", 3, 1, 0), ("y", 3, -1, 1),
        ("k", 4, 1, 0), ("pT", 4, -2, 1),
        ("v", 5, 1, 0), ("av", 5, -2, 1),
        ("x2T", 6, -3, 1), ("z", 6, -2, 0),
        ("x1T", 7, -1, 1)]
LAG = 2
ON_POOL = (1, 4, 6)
WSCALE = 256.0
SLOT_OF = {n: s for n, s, _, _ in MISC}


def valid(h):
    return not isinstance(h, int) or 0 <= h < HALVES


def need(eng, sem, value):
    if not isinstance(value, int) or value > 0:
        eng.wait_ge(sem, value)


def perceiver(nc, x, ctx, mats, rows, sw1, sw2, ew1, ew2, gate_w, out):
    es = ExitStack()
    with es:
        def sb(name, shape, dt=F32):
            return es.enter_context(nc.sbuf_tensor(name, shape, dt))

        def sem(name):
            return es.enter_context(nc.semaphore(name))

        attention = ExitStack()

        def asb(name, shape, dt=F32):
            return attention.enter_context(nc.sbuf_tensor(name, shape, dt))

        x_all = sb("x_all", [P, NT, D])
        x2T_hi = sb("x2T_hi", [P, NT * P], F16)
        x2T_lo = sb("x2T_lo", [P, NT * P], F16)
        rows_of = sb("rows_of", [P, NT, 2, ROW])
        ident = sb("ident", [P, P])
        neg_ident = sb("neg_ident", [P, P], BF16)
        ones_row = sb("ones_row", [1, P])
        head_sel = sb("head_sel", [P, GROUPS, JH])
        head_mask = sb("head_mask", [P, JH])
        causal = sb("causal", [P, P])
        minus_half = sb("minus_half", [P, 2])
        eps2 = sb("eps2", [P, 2])
        scratch = sb("scratch", [P, 8])
        row_in = sb("row_in", [len(ROWS), D])
        row1 = sb("row1", [1, 4, D])
        vec = sb("vec", [P, len(ROWS) + E])
        bcast = sb("bcast", [P, 4, D])
        gate_in = sb("gate_in", [E, D])
        gateT = vec[:, len(ROWS):len(ROWS) + E]
        gate_hi = sb("gate_hi", [P, E], F16)
        gate_lo = sb("gate_lo", [P, E], F16)
        iota8 = sb("iota8", [P, E])
        before = sb("before", [P, P], F16)
        ones16 = sb("ones16", [P, P], F16)
        region = sb("region", [P, E])
        block_no = sb("block_no", [1, BLOCKS + 1])
        block_no_i = sb("block_no_i", [1, BLOCKS + 1], I32)
        fills = sb("fills", [1, T // BR])
        fills_i = sb("fills_i", [1, T // BR], I32)
        upto = sb("upto", [1, E, E])
        padding = sb("padding", [P, BT, ROW])
        wait_mark = sb("wait_mark", [P, 1])
        mat_in = asb("mat_in", [P, len(MATS), D])
        WT = asb("WT", [P, len(MATS), D])
        ctx_in = asb("ctx_in", [P, 2, CB, D])
        mv = asb("mv", [P, 4, 2, 2])
        st = asb("st", [P, 4, 2, 6])
        rstd = asb("rstd", [P, 4, 2])
        vpe = asb("vpe", [P, 4, 2])
        xn = asb("xn", [P, 2, D])
        xnT_sb = asb("xnT_sb", [P, 2 * P])
        cT = asb("cT", [P, CB * SK])
        q32 = asb("q32", [P, 2 * P])
        q_hi = asb("q_hi", [P, 2 * P], F16)
        q_lo = asb("q_lo", [P, 2 * P])
        qm_hi = [asb(f"qm_hi{r}", [P, CB, JH, S], F16) for r in range(2)]
        qm_lo = [asb(f"qm_lo{r}", [P, CB, JH, S], F16) for r in range(2)]
        k_hi = [asb(f"k_hi{r}", [P, CB * SK], F16) for r in range(2)]
        k_lo = [asb(f"k_lo{r}", [P, CB * SK], F16) for r in range(2)]
        V_hi = [asb(f"V_hi{r}", [P, CB * HEADS // 2, VW], F16) for r in range(2)]
        V_lo = [asb(f"V_lo{r}", [P, CB * HEADS // 2, VW], F16) for r in range(2)]
        m_bf = asb("m_bf", [P, 2 * UNITS, 4], BF16)
        p32 = asb("p32", [P, 2, 512])
        p_hi = asb("p_hi", [P, 4, 512], F16)
        p_lo = asb("p_lo", [P, 4, 512], F16)
        rden = asb("rden", [P, 2, 16])
        O_tok = asb("O_tok", [P, PAIRS, HEADS // 2, 2, HD])
        OT = asb("OT", [P, 2 * P])
        yb = asb("yb", [P, 2, D])
        yn = asb("yn", [P, 2, D])
        yg = asb("yg", [P, 2, D])
        xb = asb("xb", [P, 2, D])
        x1 = [asb(f"x1_{r}", [P, 2, D]) for r in range(2)]
        x1b = [asb(f"x1b_{r}", [P, 2, D]) for r in range(2)]
        x1n = asb("x1n", [P, 2, D])
        x1T_sb = asb("x1T_sb", [P, 2 * P])
        QT = asb("QT", [P, 2 * P])
        KT = asb("KT", [P, 2 * P])
        V2 = asb("V2", [P, 2, D])
        sm = asb("sm", [P, 2, P])
        smax = asb("smax", [P, 2])
        nbias = asb("nbias", [P, 2])
        rs = asb("rs", [P, 2])
        rrs = asb("rrs", [P, 2])
        P2 = asb("P2", [P, 2, P])
        P2T = asb("P2T", [P, 2 * P])
        AT = asb("AT", [P, 2 * P])
        x2n = asb("x2n", [P, 2, D])
        attention.close()
        w_in = sb("w_in", [P, 2, CH, P])
        W1_hi = sb("W1_hi", [P, NE * HID], F16)
        W1_lo = sb("W1_lo", [P, NE * HID], F16)
        W2_hi = sb("W2_hi", [P, NE * HID], F16)
        W2_lo = sb("W2_lo", [P, NE * HID], F16)
        lg = sb("lg", [P, NT, E])
        top = sb("top", [P, NT, 8])
        idx = sb("idx", [P, NT, 8], U32)
        idxf = sb("idxf", [P, NT, 2])
        g12 = sb("g12", [P, NT, 2])
        gtmp = sb("gtmp", [P, NT])
        chosen = [sb(f"chosen{n}", [P, NT, E], F16) for n in range(2)]
        either = sb("either", [P, NT, E], F16)
        row_at = sb("row_at", [P, NT, E])
        row_pick = sb("row_pick", [P, NT, E])
        row_f = sb("row_f", [P, NT, 2])
        row_no = sb("row_no", [P, 2, NT], U32)
        per_tile = sb("per_tile", [P, E], F16)
        load = sb("load", [1, E])
        fill = sb("fill", [1, E, T // BR])
        nblocks = sb("nblocks", [1, E])
        last_block = sb("last_block", [1, E])
        t88 = sb("t88", [1, E, E])
        passed = sb("passed", [1, BLOCKS + 1, E])
        t408 = sb("t408", [1, BLOCKS + 1, E])
        b_exp = sb("b_exp", [1, BLOCKS + 1])
        b_row = sb("b_row", [1, BLOCKS + 1])
        b_first = sb("b_first", [1, BLOCKS + 1])
        w_col = sb("w_col", [1, BLOCKS + 1], I32)
        row0 = sb("row0", [1, BLOCKS + 1], I32)
        pad0 = sb("pad0", [1, E], I32)
        h32 = [sb(f"h32_{r}", [P, U_N]) for r in range(RING)]
        h_hi = [sb(f"h_hi{r}", [P, U_N], F16) for r in range(RING)]
        h_lo = [sb(f"h_lo{r}", [P, U_N], F16) for r in range(RING)]
        xrow = [sb(f"xrow{r}", [P, BT, ROW]) for r in range(LB)]
        xT_hi = [sb(f"xT_hi{r}", [P, BR], F16) for r in range(2)]
        xT_lo = [sb(f"xT_lo{r}", [P, BR], F16) for r in range(2)]
        y_sb = [sb(f"y_sb{r}", [P, BT, D]) for r in range(RING)]
        yt = [sb(f"yt{r}", [P, 2, GT, D]) for r in range(2)]

        listed = nc.dram_tensor("listed", (E * REGION + BR, ROW), F32).ap()
        results = nc.dram_tensor("results", (2 * T, D), F32).ap()

        bank = [es.enter_context(nc.psum_tensor(f"bank{n}", [P, 512], F32)) for n in range(8)]
        T_ps = bank[0:2]
        M_ps = bank[2:4]
        PV_ps = bank[4:6]
        X_ps = bank[6:8]
        XB = {n: X_ps[b] for n, _, _, b in MISC}
        U_ps = bank[0:4]
        Y_ps = bank[4:6]
        R_ps = bank[0]

        mats_in, rows_in, x_in, ctx_loaded = sem("mats_in"), sem("rows_in"), sem("x_in"), sem("ctx_loaded")
        w_loaded = [sem(f"w_loaded{r}") for r in range(2)]
        gate_loaded, gate_split = sem("gate_loaded"), sem("gate_split")
        consts, consts_pool = sem("consts"), sem("consts_pool")
        setup_pe, setup_ev, setup_dve = sem("setup_pe"), sem("setup_ev"), sem("setup_dve")
        mm = {n: sem(f"mm_{n}") for n in SLOT_OF}
        ev = {n: sem(f"ev_{n}") for n in SLOT_OF}
        m_done, max_done = sem("m_done"), sem("max_done")
        t_done, exp_done = sem("t_done"), sem("exp_done")
        v_done, norm_done, norm_step = sem("v_done"), sem("norm_done"), sem("norm_step")
        p_hi_done, p_lo_dve, p_lo_pool = sem("p_hi_done"), sem("p_lo_dve"), sem("p_lo_pool")
        q_ready, k_hi_ready, v_hi_ready = sem("q_ready"), sem("k_hi_ready"), sem("v_hi_ready")
        qm_hi_ready, qlo_full, qm_lo_ready = sem("qm_hi_ready"), sem("qlo_full"), sem("qm_lo_ready")
        LN = ["x", "y", "x1", "x2"]
        stat = {n: sem(f"stat_{n}") for n in LN}
        vpe_done = {n: sem(f"vpe_{n}") for n in LN}
        rstd_done = {n: sem(f"rstd_{n}") for n in LN}
        normed = {n: sem(f"normed_{n}") for n in LN}
        xb_done, yg_done, x1_done, x1b_done = sem("xb_done"), sem("yg_done"), sem("x1_done"), sem("x1b_done")
        x2_done = ev["z"]
        sm_max, nbias_done, p2_done, rrs_done = sem("sm_max"), sem("nbias_done"), sem("p2_done"), sem("rrs_done")
        x2T_hi_done = sem("x2T_hi_done")
        wt_pe, wt_hi, wt_lo = sem("wt_pe"), sem("wt_hi"), sem("wt_lo")
        lg_pe, lg_ev, gate_step, gate_exp = sem("lg_pe"), sem("lg_ev"), sem("gate_step"), sem("gate_exp")
        u_done, silu_done, hhi_done, hlo_done = sem("u_done"), sem("silu_done"), sem("hhi_done"), sem("hlo_done")
        d_done, y_done = sem("d_done"), sem("y_done")
        picked, ranked, placed, padded = sem("picked"), sem("ranked"), sem("placed"), sem("padded")
        table, tables_ready = sem("table"), sem("tables_ready")
        row_step, rows_full, block_seen = sem("row_step"), sem("rows_full"), sem("block_seen")
        listed_done = sem("listed_done")
        loaded = [sem(f"loaded{r}") for r in range(LB)]
        xT_pe, xT_hi_done, xT_lo_done = sem("xT_pe"), sem("xT_hi_done"), sem("xT_lo_done")
        scattered = [sem(f"scattered{r}") for r in range(RING)]
        yt_loaded = [sem(f"yt_loaded{r}") for r in range(2)]
        yt_summed, routed_added = sem("yt_summed"), sem("routed_added")
        stored = sem("stored")

        block = es.enter_context(nc.Block())

        x_v = x.rearrange("(t two) s d -> (two s) t d", two=2)
        out_v = out.rearrange("(t two) s d -> (two s) t d", two=2)
        ctx_v = ctx.rearrange("b k d -> k b d")

        def two_tiles(h):
            return slice(2 * h, 2 * h + 2) if isinstance(h, int) else bass.ds(h * 2, 2)

        def one_tile(h, t):
            return slice(2 * h + t, 2 * h + t + 1) if isinstance(h, int) else bass.ds(h * 2 + t, 1)

        def half_cols(h):
            return slice(2 * P * h, 2 * P * (h + 1)) if isinstance(h, int) else bass.ds(h * (2 * P), 2 * P)

        def all_steps(eng, step):
            for h in range(-2, 4):
                step(h, h % 2)
            with eng.Fori(2, (HALVES - 2) // 2) as i:
                step(i * 2, 0)
                step(i * 2 + 1, 1)
            for h in range(HALVES - 2, HALVES + 3):
                step(h, h % 2)

        def low_of(h, s):
            if s in ON_POOL:
                return p_lo_pool, h * len(ON_POOL) + ON_POOL.index(s) + 1
            others = [n for n in range(UNITS) if n not in ON_POOL]
            return p_lo_dve, h * len(others) + others.index(s) + 1

        def low_part(eng, h, s):
            eng.wait_ge(p_hi_done, UNITS * h + s + 1)
            need(eng, v_done, UNITS * h + s - 3)
            eng.tensor_tensor(p_lo[:, s % 4, :], p32[:, s % 2, :], p_hi[:, s % 4, :],
                              ALU.subtract).then_inc(low_of(h, s)[0], 1)

        def bank_free(eng, name, h):
            at = [n for n, *_ in MISC].index(name)
            own = MISC[at][3]
            for back in list(range(at - 1, -1, -1)) + list(range(len(MISC) - 1, at, -1)):
                n, _, rel, b = MISC[back]
                hh = h + rel - (1 if back > at else 0)
                if b == own and valid(hh):
                    eng.wait_ge(ev[n], (hh + 1) * (2 if n == "z" else 1))
                    return

        def one(n):
            return slice(n, n + 1) if isinstance(n, int) else bass.ds(n, 1)

        @block.sync
        def _(sp):
            for n, m in enumerate(mats):
                sp.dma_start(mat_in[:, n, :], m).then_inc(mats_in, 16)
            def load(h, r):
                tiles = two_tiles(h)
                batches = slice(CB * h, CB * h + CB) if isinstance(h, int) else bass.ds(h * CB, CB)
                need(sp, x_in, 16 * h)
                sp.dma_start(x_all[:, tiles, :], x_v[:, tiles, :]).then_inc(x_in, 16)
                need(sp, mm["ctxT"], h - 1)
                need(sp, ctx_loaded, 16 * h)
                sp.dma_start(ctx_in[:, r, :, :],
                             ctx_v[:, batches, :]).then_inc(ctx_loaded, 16)
            load(0, 0)
            load(1, 1)
            with sp.Fori(1, HALVES // 2) as i:
                load(i * 2, 0)
                load(i * 2 + 1, 1)
            for e in range(NE):
                w1 = ew1[e] if e < E else sw1
                w2 = ew2[e] if e < E else sw2
                if e > 0:
                    sp.wait_ge(wt_pe, 2 * e - 1)
                sp.dma_start(w_in[:, 0, :, :], w1.rearrange("(c p) d -> p c d", p=P)).then_inc(w_loaded[0], 16)
                if e > 0:
                    sp.wait_ge(wt_pe, 2 * e)
                sp.dma_start(w_in[:, 1, :, :], w2.rearrange("d (c h) -> d c h", h=P)).then_inc(w_loaded[1], 16)
            sp.wait_ge(consts_pool, CONSTS)
            sp.dma_start(listed[E * REGION:E * REGION + BR, :].rearrange("(a p) d -> p a d", p=P),
                         padding[:, :, :]).then_inc(padded, 16)
            sp.wait_ge(tables_ready, 3)
            for e in range(E):
                first = sp.value_load(pad0[0:1, e:e + 1], min_val=0, max_val=E * REGION - BR)
                sp.dma_start(listed[bass.ds(first, BR), :].rearrange("(a p) d -> p a d", p=P),
                             padding[:, :, :]).then_inc(padded, 16)
            sp.wait_ge(padded, 16 * (E + 1))
            sp.wait_ge(listed_done, 16 * 2 * NT)
            def fetch(i):
                for b in range(LB):
                    need(sp, scattered[b % RING], i * (32 * LB // RING) + 32 * (b // RING - 1))
                    first = sp.value_load(row0[0:1, one(i * LB + b)], min_val=0, max_val=E * REGION)
                    sp.dma_start(xrow[b][:, :, :], listed[bass.ds(first, BR), :].rearrange("(a p) d -> p a d", p=P)
                                 ).then_inc(loaded[b], 16)
            fetch(0)
            with sp.Fori(1, BLOCKS // LB) as i:
                fetch(i)
            for r in range(RING):
                sp.wait_ge(scattered[r], 32 * (BLOCKS // RING))
            res = results.rearrange("(n t p) d -> p n t d", p=P, n=2)
            for g in range(FG):
                if g >= 2:
                    sp.wait_ge(routed_added, g - 1)
                for n in range(2):
                    sp.dma_start(yt[g % 2][:, n, :, :], res[:, n, g * GT:g * GT + GT, :]).then_inc(yt_loaded[g % 2], 16)
            for g in range(FG):
                tiles = slice(g * GT, g * GT + GT)
                sp.wait_ge(routed_added, g + 1)
                if g >= BEFORE:
                    sp.wait_ge(y_done, BEFORE + BLOCKS + g - BEFORE + 1)
                sp.dma_start(out_v[:, tiles, :], x_all[:, tiles, :]).then_inc(stored, 16)
            sp.wait_ge(stored, 16 * FG)

        @block.gpsimd
        def _(pool):
            pool.dma_start(gate_in[:, :], gate_w).then_inc(gate_loaded, 16)
            pool.memset(ident[:, :], 0.0).then_inc(consts_pool, 1)
            pool.memset(head_sel[:, :, :], 1.0).then_inc(consts_pool, 1)
            pool.memset(causal[:, :], 0.0).then_inc(consts_pool, 1)
            pool.wait_ge(consts_pool, 3)
            pool.affine_select(out=ident[:, :], in_=ident[:, :], compare_op=ALU.not_equal, fill=1.0, base=0,
                               pattern=[[-1, P]], channel_multiplier=1).then_inc(consts_pool, 1)
            pool.affine_select(out=head_sel[:, :, :], in_=head_sel[:, :, :], compare_op=ALU.is_ge, fill=0.0, base=0,
                               pattern=[[-JH * HD, GROUPS], [-HD, JH]], channel_multiplier=1).then_inc(consts_pool, 1)
            pool.affine_select(out=causal[:, :], in_=causal[:, :], compare_op=ALU.is_ge, fill=MASKED, base=0,
                               pattern=[[-1, P]], channel_multiplier=1).then_inc(consts_pool, 1)
            pool.wait_ge(consts_pool, 6)
            pool.affine_select(out=head_sel[:, :, :], in_=head_sel[:, :, :], compare_op=ALU.is_ge, fill=0.0,
                               base=HD - 1, pattern=[[JH * HD, GROUPS], [HD, JH]],
                               channel_multiplier=-1).then_inc(consts_pool, 1)
            pool.wait_ge(consts_pool, 7)
            pool.memset(causal[S:P, 0:S], MASKED).then_inc(consts_pool, 1)
            pool.wait_ge(consts_pool, 8)
            pool.memset(minus_half[:, :], -0.5).then_inc(consts_pool, 1)
            pool.memset(ones_row[:, :], 1.0).then_inc(consts_pool, 1)
            pool.memset(eps2[:, :], EPS).then_inc(consts_pool, 1)
            for r in range(2):
                pool.memset(V_hi[r][:, :, 2 * HD:VW], 1.0).then_inc(consts_pool, 1)
                pool.memset(V_lo[r][:, :, 2 * HD:VW], 0.0).then_inc(consts_pool, 1)
            for e in range(E):
                pool.memset(iota8[:, e:e + 1], float(e)).then_inc(consts_pool, 1)
                pool.memset(region[:, e:e + 1], float(e * REGION)).then_inc(consts_pool, 1)
                pool.memset(upto[:, e, 0:e + 1], 1.0).then_inc(consts_pool, 1)
                if e < E - 1:
                    pool.memset(upto[:, e, e + 1:E], 0.0).then_inc(consts_pool, 1)
            pool.memset(ones16[:, :], 1.0).then_inc(consts_pool, 1)
            pool.memset(padding[:, :, :], 0.0).then_inc(consts_pool, 1)
            pool.memset(before[:, :], 1.0).then_inc(consts_pool, 1)
            pool.iota(block_no_i[:, :], pattern=[[1, BLOCKS + 1]], base=0, channel_multiplier=0).then_inc(consts_pool, 1)
            pool.iota(fills_i[:, :], pattern=[[BR, T // BR]], base=0, channel_multiplier=0).then_inc(consts_pool, 1)
            for n in range(2):
                pool.iota(rows_of[:, :, n, D:D + 1].bitcast(I32), pattern=[[P, NT], [0, 1]], base=n * T,
                          channel_multiplier=1).then_inc(consts_pool, 1)
            pool.wait_ge(consts_pool, CONSTS - 4)
            pool.affine_select(out=before[:, :], in_=before[:, :], compare_op=ALU.is_gt, fill=0.0, base=0,
                               pattern=[[1, P]], channel_multiplier=-1).then_inc(consts_pool, 1)
            pool.memset(padding[:, :, D:D + 1].bitcast(I32), NOWHERE).then_inc(consts_pool, 1)
            pool.tensor_copy(block_no[:, :], block_no_i[:, :]).then_inc(consts_pool, 1)
            pool.tensor_copy(fills[:, :], fills_i[:, :]).then_inc(consts_pool, 1)

            def root(n, h):
                i = LN.index(n)
                pool.wait_ge(stat[n], h * 4 + 4)
                need(pool, normed[n], h * 2)
                if n == "x2":
                    need(pool, rows_full, h * 2)
                pool.tensor_tensor(vpe[:, i, :], mv[:, i, :, 1], eps2[:, :], ALU.add).then_inc(vpe_done[n], 1)
                pool.wait_ge(vpe_done[n], h + 1)
                pool.tensor_tensor(rstd[:, i, :], vpe[:, i, :], minus_half[:, :], ALU.pow).then_inc(rstd_done[n], 1)

            def step(h, r):
                for s in range(UNITS):
                    back, hb = (s - 1) % UNITS, h if s else h - 1
                    if back in ON_POOL and valid(hb):
                        low_part(pool, hb, back)
                    if s == 2 and valid(h + 2):
                        root("x", h + 2)
                    if s == 3 and valid(h + 1):
                        pool.wait_ge(q_ready, h + 2)
                        pool.wait_ge(ev["q"], h + 2)
                        need(pool, qm_lo_ready, h + 1)
                        pool.tensor_tensor(q_lo[:, :], q32[:, :], q_hi[:, :], ALU.subtract).then_inc(qlo_full, 1)
                        pool.wait_ge(qlo_full, h + 2)
                        need(pool, t_done, UNITS * h)
                        pool.tensor_tensor(qm_lo[1 - r][:, :, :, :],
                                           q_lo[:, :].rearrange("p (b q) -> p b q", q=S).unsqueeze(2).broadcast_to([P, CB, JH, S]),
                                           head_mask[:, :].unsqueeze(1).unsqueeze(3).broadcast_to([P, CB, JH, S]),
                                           ALU.mult).then_inc(qm_lo_ready, 1)
                    if s == 4 and valid(h - 1):
                        root("y", h - 1)
                        pool.wait_ge(normed["y"], (h - 1) * 2 + 2)
                        pool.tensor_tensor(yg[:, :, :], yn[:, :, :],
                                           bcast[:, 2:3, :].broadcast_to([P, 2, D]), ALU.mult).then_inc(yg_done, 1)
                        pool.wait_ge(yg_done, h)
                        pool.wait_ge(xb_done, h)
                        need(pool, x2_done, (h - 2) * 2)
                        need(pool, normed["x1"], (h - 2) * 2)
                        pool.tensor_tensor(x1[1 - r][:, :, :], yg[:, :, :], xb[:, :, :], ALU.add).then_inc(x1_done, 1)
                    if s == 5 and valid(h - 1):
                        root("x1", h - 1)
                        pool.wait_ge(x1_done, h)
                        pool.tensor_tensor(x1b[1 - r][:, :, :], x1[1 - r][:, :, :],
                                           bcast[:, 1:2, :].broadcast_to([P, 2, D]), ALU.add).then_inc(x1b_done, 1)
                    if s == 7 and valid(h - 2):
                        root("x2", h - 2)
                    if s == 7 and valid(h):
                        pool.wait_ge(x_in, (h + 1) * 16)
                        need(pool, x1_done, h)
                        pool.tensor_tensor(xb[:, :, :], x_all[:, two_tiles(h), :],
                                           bcast[:, 3:4, :].broadcast_to([P, 2, D]), ALU.add).then_inc(xb_done, 1)
            pool.wait_ge(setup_dve, 3)
            all_steps(pool, step)
            for n in range(2):
                pool.wait_ge(placed, 2 + n)
                for t in range(NT):
                    pool.indirect_dma_start(out=listed[:, :], out_offset=bass.IndirectOffsetOnAxis(ap=row_no[:, n, t:t + 1], axis=0),
                                            in_=rows_of[:, t, n, :], in_offset=None).then_inc(listed_done, 16)
            def scatter(i):
                for b in range(LB):
                    pool.wait_ge(y_done, i * LB + BEFORE + b + 1)
                    need(pool, block_seen, i * LB + b)
                    pool.tensor_tensor(wait_mark[:, :], eps2[:, 0:1], eps2[:, 0:1], ALU.add).then_inc(block_seen, 1)
                    for t in range(BT):
                        pool.indirect_dma_start(out=results[:, :],
                                                out_offset=bass.IndirectOffsetOnAxis(ap=xrow[b][:, t, D:D + 1].bitcast(U32), axis=0),
                                                in_=y_sb[b % RING][:, t, :], in_offset=None,
                                                bounds_check=2 * T - 1, oob_is_err=False).then_inc(scattered[b % RING], 16)
            scatter(0)
            with pool.Fori(1, BLOCKS // LB) as i:
                scatter(i)
            for g in range(FG):
                pool.wait_ge(yt_loaded[g % 2], 32 * (g // 2 + 1))
                pool.tensor_tensor(yt[g % 2][:, 0, :, :], yt[g % 2][:, 0, :, :], yt[g % 2][:, 1, :, :],
                                   ALU.add).then_inc(yt_summed, 1)

        @block.scalar
        def _(act):
            for n, v in enumerate(rows):
                act.dma_start(row_in[n:n + 1, :], v.rearrange("(a n) -> a n", a=1)).then_inc(rows_in, 16)
            for n, name in enumerate(("xbo", "abo", "gamma", "beta")):
                act.dma_start(row1[:, n, :], rows[ROWS.index(name)].rearrange("(a n) -> a n", a=1)).then_inc(rows_in, 16)
            for n in range(2):
                act.wait_ge(setup_pe, n + 1)
                act.activation(WT[:, 4 * n:4 * n + 4, :], X_ps[n][:, :], ACT.Copy).then_inc(setup_ev, 1)
            act.wait_ge(setup_pe, 3)
            act.activation(vec[:, :], X_ps[0][:, 0:len(ROWS) + E], ACT.Copy).then_inc(setup_ev, 1)
            act.wait_ge(setup_pe, 4)
            act.activation(bcast[:, :, :], X_ps[1][:, :], ACT.Copy).then_inc(setup_ev, 1)
            act.wait_ge(setup_ev, 3)

            def col(name):
                n = ROWS.index(name)
                return vec[:, n:n + 1]

            def evacuate(name, h, dst, src, func=ACT.Copy, **kw):
                act.wait_ge(mm[name], h + 1)
                act.activation(dst, src, func, **kw).then_inc(ev[name], 1)

            def step(h, r):
                a, b, c, d = h + 1, h - 1, h - 2, h - 3
                for s in range(UNITS):
                    u = UNITS * h + s
                    if valid(h):
                        act.wait_ge(t_done, u + 1)
                        hl, sl = (h, s - 2) if s > 1 else (h - 1, s + UNITS - 2)
                        if valid(hl):
                            act.wait_ge(*low_of(hl, sl))
                        act.activation(p32[:, s % 2, :], T_ps[s % 2][:, :], ACT.Exp,
                                       scale=XSCALE).then_inc(exp_done, 1)
                    if valid(h):
                        act.wait_ge(exp_done, u + 1)
                        need(act, v_done, u - 3)
                        act.activation(p_hi[:, s % 4, :], p32[:, s % 2, :], ACT.Copy).then_inc(p_hi_done, 1)
                    if s == 0 and valid(a):
                        need(act, mm["q"], a)
                        evacuate("xnT", a, xnT_sb[:, :], XB["xnT"][:, 0:2 * P])
                    if s == 0 and valid(c):
                        act.wait_ge(mm["qk"], c + 1)
                        need(act, mm["s"], c)
                        act.activation(QT[:, :], XB["qk"][:, 0:2 * P], ACT.Identity, bias=col("abq"))
                        act.activation(KT[:, :], XB["qk"][:, 2 * P:4 * P], ACT.Identity, bias=col("abk")).then_inc(ev["qk"], 1)
                    if s == 1 and valid(c):
                        need(act, mm["av"], c)
                        evacuate("v2", c, V2[:, :, :], XB["v2"][:, 0:2 * P])
                    if s == 2 and valid(a):
                        act.wait_ge(mm["q"], a + 1)
                        need(act, qm_lo_ready, a)
                        need(act, qm_hi_ready, JH * a)
                        act.activation(q32[:, :], XB["q"][:, 0:2 * P], ACT.Identity, bias=col("xbq")).then_inc(q_ready, 1)
                        act.activation(q_hi[:, :], XB["q"][:, 0:2 * P], ACT.Identity,
                                       bias=col("xbq")).then_inc(ev["q"], 1)
                    if s == 2 and valid(b):
                        need(act, mm["y"], b)
                        evacuate("oT", b, OT[:, :], XB["oT"][:, 0:2 * P])
                    if s == 3 and valid(c):
                        act.wait_ge(nbias_done, c + 1)
                        need(act, mm["pT"], c)
                        for t in range(2):
                            act.activation(P2[:, t, :], sm[:, t, :], ACT.Exp, bias=nbias[:, t:t + 1], scale=ASCALE,
                                           accum_out=rs[:, t:t + 1]).then_inc(p2_done, 1)
                    if s == 3 and valid(a):
                        need(act, mm["v"], a)
                        evacuate("ctxT", a, cT[:, :], XB["ctxT"][:, :])
                    if s == 4 and valid(a):
                        act.wait_ge(mm["k"], a + 1)
                        need(act, t_done, UNITS * (a - 1))
                        act.activation(k_hi[1 - r][:, :], XB["k"][:, :], ACT.Identity, bias=col("xbk")).then_inc(k_hi_ready, 1)
                    if s == 4 and valid(c):
                        need(act, mm["av"], c)
                        evacuate("pT", c, P2T[:, :], XB["pT"][:, 0:2 * P])
                    if s == 5 and valid(a):
                        act.wait_ge(mm["v"], a + 1)
                        need(act, v_done, UNITS * (a - 1))
                        act.activation(V_hi[1 - r][:, :, 0:2 * HD], XB["v"][:, :].rearrange("p (n w) -> p n w", w=2 * HD),
                                       ACT.Copy).then_inc(v_hi_ready, 1)
                    if s == 5 and valid(c):
                        need(act, mm["z"], c)
                        evacuate("av", c, AT[:, :], XB["av"][:, 0:2 * P])
                    if s == 6 and valid(d):
                        act.wait_ge(mm["x2T"], d + 1)
                        act.activation(x2T_hi[:, half_cols(d)], XB["x2T"][:, 0:2 * P], ACT.Copy).then_inc(x2T_hi_done, 1)
                    if s == 7 and valid(b):
                        need(act, mm["v2"], b)
                        evacuate("x1T", b, x1T_sb[:, :], XB["x1T"][:, 0:2 * P])
            all_steps(act, step)
            def weights_hi(n):
                act.wait_ge(wt_pe, n + 1)
                dst = (W1_hi, W2_hi)[n % 2]
                act.activation(dst[:, n // 2 * HID:n // 2 * HID + HID], X_ps[n % 2][:, :], ACT.Copy, scale=WSCALE).then_inc(wt_hi, 1)
            weights_hi(0)
            weights_hi(1)
            act.wait_ge(gate_step, 1)
            act.activation(gtmp[:, :], g12[:, :, 0], ACT.Exp).then_inc(gate_exp, 1)
            for n in range(2, 2 * NE):
                weights_hi(n)

            def unit(n, k):
                act.wait_ge(u_done, n + 1)
                need(act, hlo_done, n - RING + 1)
                act.activation(h32[k % RING][:, :], U_ps[k % RING][:, :], ACT.Silu, scale=1.0 / WSCALE).then_inc(silu_done, 1)
                act.wait_ge(silu_done, n + 1)
                need(act, d_done, n - RING + 1)
                act.activation(h_hi[k % RING][:, :], h32[k % RING][:, :], ACT.Copy).then_inc(hhi_done, 1)

            def block_in(j, b):
                act.wait_ge(xT_pe, j + 1)
                if not isinstance(j, int) or j > 1:
                    act.wait_ge(u_done, j * BU + (N0 - 2 * BU + BU))
                act.activation(xT_hi[b % 2][:, :], X_ps[b % 2][:, 0:BR], ACT.Copy).then_inc(xT_hi_done, 1)

            def routed(i, end):
                for b in range(LB):
                    for q in range(BU):
                        unit(i * (LB * BU) + N0 + b * BU + q, b * BU + q)
                        if q == 0 and not (end and b == LB - 1):
                            block_in(i * LB + b + 1, b + 1)
            for n in range(N0):
                unit(n, n)
                if n == N0 - BU:
                    block_in(0, 0)
            routed(0, False)
            with act.Fori(1, BLOCKS // LB - 1) as i:
                routed(i, False)
            routed(BLOCKS // LB - 1, True)
            for n in range(N1, NU):
                unit(n, n)

        @block.vector
        def _(dve):
            dve.wait_ge(consts_pool, CONSTS)
            dve.tensor_reduce(head_mask[:, :], head_sel[:, :, :].rearrange("p a j -> p j a"), AX.X,
                              ALU.add).then_inc(setup_dve, 1)
            dve.tensor_scalar(neg_ident[:, :], ident[:, :], -1.0, None, ALU.mult).then_inc(setup_dve, 1)
            dve.wait_ge(setup_ev, 3)
            dve.tensor_scalar(gate_hi[:, :], gateT, WSCALE, None, ALU.mult).then_inc(gate_split, 1)
            dve.wait_ge(gate_split, 1)
            dve.scalar_tensor_tensor(gate_lo[:, :], gateT, WSCALE, gate_hi[:, :], ALU.mult, ALU.subtract).then_inc(gate_split, 1)
            dve.wait_ge(setup_ev, 4)
            dve.wait_ge(setup_pe, 5)
            dve.tensor_tensor(bcast[:, 0:2, :], bcast[:, 0:2, :],
                              X_ps[0][:, 0:2 * D].rearrange("p (n d) -> p n d", d=D), ALU.add).then_inc(setup_dve, 1)

            def statistics(n, h, src):
                i = LN.index(n)
                need(dve, normed[n], h * 2)
                dve.memset(scratch[:, 2 * i:2 * i + 1], 0.0)
                for t in range(2):
                    dve.bn_stats(st[:, i, t, :], src[:, t, :]).then_inc(stat[n], 1)
                dve.wait_ge(stat[n], h * 4 + 2)
                dve.memset(scratch[:, 2 * i + 1:2 * i + 2], 0.0)
                for t in range(2):
                    dve.bn_aggr(mv[:, i, t, :], st[:, i, t, :]).then_inc(stat[n], 1)

            def normalise(n, h, src, dst):
                i = LN.index(n)
                dve.wait_ge(rstd_done[n], h + 1)
                dve.wait_ge(stat[n], h * 4 + 4)
                for t in range(2):
                    dve.tensor_scalar(dst[:, t, :], src[:, t, :], mv[:, i, t, 0:1], rstd[:, i, t:t + 1],
                                      ALU.subtract, ALU.mult).then_inc(normed[n], 1)

            def normalise_pair(h, p):
                dve.wait_ge(v_done, UNITS * h + GROUPS * (p + 1))
                need(dve, norm_done, h * 2 + p)
                pv = PV_ps[p][:, 0:16 * VW].rearrange("p (n w) -> p n w", w=VW)
                dve.reciprocal(rden[:, p, :], pv[:, :, 2 * HD]).then_inc(norm_step, 1)
                dve.wait_ge(norm_step, h * 2 + p + 1)
                need(dve, mm["oT"], h)
                for b in range(2):
                    for o in range(2):
                        rows_ = slice(S * o, S * o + S)
                        last = dve.tensor_tensor(
                            O_tok[S * b:S * b + S, p, :, o, :], pv[rows_, 8 * b:8 * b + 8, HD * o:HD * o + HD],
                            rden[rows_, p, 8 * b:8 * b + 8].unsqueeze(2).broadcast_to([S, 8, HD]), ALU.mult)
                last.then_inc(norm_done, 1)

            def step(h, r):
                a, b, c, d = h + 1, h - 1, h - 2, h - 3
                for s in range(UNITS):
                    hm, u = (h, UNITS * h + s + 2)
                    if s >= UNITS - 2:
                        hm = h + 1
                    if valid(hm):
                        dve.wait_ge(m_done, u + 1)
                        need(dve, t_done, u + 1 - 2 * UNITS)
                        slot = (r * UNITS + s + 2) % (2 * UNITS)
                        dve.tensor_reduce(m_bf[:, slot, :], M_ps[s % 2][:, :].rearrange("p (n k) -> p n k", k=SK),
                                          AX.X, ALU.max).then_inc(max_done, 1)
                    back, hb = (s - 1) % UNITS, h if s else h - 1
                    if back not in ON_POOL and valid(hb):
                        low_part(dve, hb, back)
                    if s == 1 and valid(c):
                        dve.wait_ge(mm["s"], c + 1)
                        need(dve, p2_done, 2 * c)
                        dve.tensor_tensor(sm[:, :, :], XB["s"][:, 0:2 * P].rearrange("p (t k) -> p t k", k=P),
                                          causal[:, :].unsqueeze(1).broadcast_to([P, 2, P]), ALU.add).then_inc(ev["s"], 1)
                        dve.wait_ge(ev["s"], c + 1)
                        dve.tensor_reduce(smax[:, :], sm[:, :, :], AX.X, ALU.max).then_inc(sm_max, 1)
                        dve.wait_ge(sm_max, c + 1)
                        dve.tensor_scalar(nbias[:, :], smax[:, :], -ASCALE, None, ALU.mult).then_inc(nbias_done, 1)
                    if s == 1 and valid(b):
                        normalise_pair(b, 1)
                    if s == 5 and valid(h):
                        normalise_pair(h, 0)
                    if s == 0 and valid(h + 2):
                        dve.wait_ge(x_in, (h + 3) * 16)
                        statistics("x", h + 2, x_all[:, two_tiles(h + 2), :])
                    if s == 3 and valid(a):
                        dve.wait_ge(ev["q"], a + 1)
                        need(dve, t_done, UNITS * (a - 1))
                        for j in range(JH):
                            dve.tensor_scalar(qm_hi[1 - r][:, :, j, :],
                                              q_hi[:, :].rearrange("p (b q) -> p b q", q=S),
                                              head_mask[:, j:j + 1], None, ALU.mult).then_inc(qm_hi_ready, 1)
                    if s == 3 and valid(b):
                        dve.wait_ge(mm["y"], b + 1)
                        need(dve, normed["y"], 2 * b)
                        dve.tensor_tensor(yb[:, :, :], XB["y"][:, 0:2 * P].rearrange("p (t k) -> p t k", k=P),
                                          bcast[:, 0:1, :].broadcast_to([P, 2, D]), ALU.add).then_inc(ev["y"], 1)
                        dve.wait_ge(ev["y"], b + 1)
                        statistics("y", b, yb)
                    if s == 3 and valid(d):
                        need(dve, mm["x2T"], d)
                        normalise("x2", d, x_all[:, two_tiles(d), :], x2n)
                        for t in range(2):
                            dve.tensor_scalar(rows_of[:, one_tile(d, t), :, 0:D].rearrange("p t n d -> p (t n) d"),
                                              x_all[:, one_tile(d, t), :].broadcast_to([P, 2, D]),
                                              mv[:, 3, t, 0:1], rstd[:, 3, t:t + 1],
                                              ALU.subtract, ALU.mult).then_inc(rows_full, 1)
                    if s == 4 and valid(a):
                        dve.wait_ge(k_hi_ready, a + 1)
                        dve.scalar_tensor_tensor(k_lo[1 - r][:, :], XB["k"][:, :], vec[:, 1:2],
                                                 k_hi[1 - r][:, :], ALU.add, ALU.subtract).then_inc(ev["k"], 1)
                    if s == 4 and valid(c):
                        dve.wait_ge(p2_done, 2 * c + 2)
                        need(dve, x2_done, 2 * c)
                        dve.reciprocal(rrs[:, :], rs[:, :]).then_inc(rrs_done, 1)
                    if s == 4 and valid(b):
                        need(dve, yg_done, b)
                        normalise("y", b, yb, yn)
                    if s == 5 and valid(a):
                        dve.wait_ge(v_hi_ready, a + 1)
                        dve.tensor_tensor(V_lo[1 - r][:, :, 0:2 * HD], XB["v"][:, :].rearrange("p (n w) -> p n w", w=2 * HD),
                                          V_hi[1 - r][:, :, 0:2 * HD], ALU.subtract).then_inc(ev["v"], 1)
                    if s == 5 and valid(h + 2):
                        dve.wait_ge(mm["xnT"], h + 2)
                        normalise("x", h + 2, x_all[:, two_tiles(h + 2), :], xn)
                    if s == 5 and valid(b):
                        dve.wait_ge(x1_done, b + 1)
                        statistics("x1", b, x1[1 - r])
                    if s == 6 and valid(d):
                        dve.wait_ge(x2T_hi_done, d + 1)
                        dve.tensor_tensor(x2T_lo[:, half_cols(d)], XB["x2T"][:, 0:2 * P],
                                          x2T_hi[:, half_cols(d)], ALU.subtract).then_inc(ev["x2T"], 1)
                    if s == 6 and valid(b):
                        need(dve, mm["x1T"], b)
                        normalise("x1", b, x1[1 - r], x1n)
                    if s == 6 and valid(c):
                        dve.wait_ge(mm["z"], c + 1)
                        dve.wait_ge(rrs_done, c + 1)
                        dve.wait_ge(x1b_done, c + 1)
                        for t in range(2):
                            last = dve.scalar_tensor_tensor(x_all[:, one_tile(c, t), :].rearrange("p t d -> p (t d)"),
                                                            XB["z"][:, t * P:t * P + P],
                                                            rrs[:, t:t + 1], x1b[r][:, t, :], ALU.mult, ALU.add)
                            last.then_inc(x2_done, 1)
                        dve.wait_ge(x2_done, 2 * c + 2)
                        statistics("x2", c, x_all[:, two_tiles(c), :])
            all_steps(dve, step)

            dve.wait_ge(lg_pe, 1)
            dve.tensor_scalar(lg[:, :, :], X_ps[0][:, 0:NT * E].rearrange("p (t e) -> p t e", e=E), 1.0 / WSCALE, None,
                              ALU.mult).then_inc(lg_ev, 1)
            dve.wait_ge(lg_ev, 1)
            for t in range(NT):
                dve.max(top[:, t, :], lg[:, t, :]).then_inc(lg_ev, 1)
            dve.wait_ge(lg_ev, 1 + NT)
            for t in range(NT):
                dve.max_index(idx[:, t, :], top[:, t, :], lg[:, t, :]).then_inc(lg_ev, 1)
            dve.tensor_tensor(g12[:, :, 0], top[:, :, 1], top[:, :, 0], ALU.subtract).then_inc(gate_step, 1)
            dve.wait_ge(lg_ev, 1 + 2 * NT)
            dve.tensor_copy(idxf[:, :, :], idx[:, :, 0:2]).then_inc(gate_step, 1)
            dve.wait_ge(gate_exp, 1)
            dve.tensor_scalar(g12[:, :, 1], gtmp[:, :], 1.0, None, ALU.add).then_inc(gate_step, 1)
            dve.wait_ge(gate_step, 3)
            dve.reciprocal(g12[:, :, 0], g12[:, :, 1]).then_inc(gate_step, 1)
            dve.wait_ge(gate_step, 4)
            dve.tensor_tensor(g12[:, :, 1], g12[:, :, 0], gtmp[:, :], ALU.mult).then_inc(gate_step, 1)
            dve.wait_ge(gate_step, 5)
            for n in range(2):
                dve.tensor_scalar(rows_of[:, :, n, D + 1:D + 2], g12[:, :, n:n + 1], 1.0 / WSCALE, None,
                                  ALU.mult).then_inc(gate_step, 1)
                dve.tensor_tensor(chosen[n][:, :, :], iota8[:, :].unsqueeze(1).broadcast_to([P, NT, E]),
                                  idxf[:, :, n].unsqueeze(2).broadcast_to([P, NT, E]), ALU.is_equal).then_inc(gate_step, 1)
            dve.wait_ge(gate_step, 9)
            dve.tensor_tensor(either[:, :, :], chosen[0][:, :, :], chosen[1][:, :, :], ALU.add).then_inc(picked, 1)
            dve.wait_ge(picked, 1)
            with nc.allow_low_precision(reason="counts up to 32 are exact"):
                dve.tensor_reduce(per_tile[:, :], either[:, :, :].rearrange("p t e -> p e t"), AX.X, ALU.add).then_inc(picked, 1)

            def weights_lo(n):
                dve.wait_ge(wt_hi, n + 1)
                part = slice(n // 2 * HID, n // 2 * HID + HID)
                dve.scalar_tensor_tensor((W1_lo, W2_lo)[n % 2][:, part], X_ps[n % 2][:, :], WSCALE, (W1_hi, W2_hi)[n % 2][:, part],
                                         ALU.mult, ALU.subtract).then_inc(wt_lo, 1)
            weights_lo(0)
            weights_lo(1)
            dve.wait_ge(ranked, 1)
            dve.tensor_tensor(row_at[:, :, :], R_ps[:, 0:NT * E].rearrange("p (t e) -> p t e", e=E),
                              region[:, :].unsqueeze(1).broadcast_to([P, NT, E]), ALU.add).then_inc(placed, 1)
            dve.tensor_copy(load[:, :], R_ps[0:1, NT * E:NT * E + E]).then_inc(table, 1)
            dve.wait_ge(placed, 1)
            for n in range(2):
                need(dve, row_step, 2 * n)
                dve.tensor_tensor(row_pick[:, :, :], row_at[:, :, :], chosen[n][:, :, :], ALU.mult).then_inc(row_step, 1)
                dve.wait_ge(row_step, 2 * n + 1)
                dve.tensor_reduce(row_f[:, :, n], row_pick[:, :, :], AX.X, ALU.add).then_inc(row_step, 1)
                dve.wait_ge(row_step, 2 * n + 2)
                dve.tensor_copy(row_no[:, n, :], row_f[:, :, n]).then_inc(placed, 1)
            dve.wait_ge(table, 1)
            dve.tensor_tensor(fill[:, :, :], load[:, :].unsqueeze(2).broadcast_to([1, E, T // BR]),
                              fills[:, :].unsqueeze(1).broadcast_to([1, E, T // BR]), ALU.is_gt).then_inc(table, 1)
            dve.tensor_tensor(pad0[:, :], load[:, :], region[0:1, :], ALU.add).then_inc(tables_ready, 1)
            dve.wait_ge(table, 2)
            dve.tensor_reduce(nblocks[:, :], fill[:, :, :], AX.X, ALU.add).then_inc(table, 1)
            dve.wait_ge(table, 3)
            dve.tensor_tensor(t88[:, :, :], nblocks[:, :].unsqueeze(1).broadcast_to([1, E, E]), upto[:, :, :],
                              ALU.mult).then_inc(table, 1)
            dve.wait_ge(table, 4)
            dve.tensor_reduce(last_block[:, :], t88[:, :, :], AX.X, ALU.add).then_inc(table, 1)
            dve.wait_ge(table, 5)
            dve.tensor_tensor(passed[:, :, :], block_no[:, :].unsqueeze(2).broadcast_to([1, BLOCKS + 1, E]),
                              last_block[:, :].unsqueeze(1).broadcast_to([1, BLOCKS + 1, E]), ALU.is_ge).then_inc(table, 1)
            dve.wait_ge(table, 6)
            dve.tensor_reduce(b_exp[:, :], passed[:, :, :], AX.X, ALU.add).then_inc(table, 1)
            dve.tensor_tensor(t408[:, :, :], passed[:, :, :], nblocks[:, :].unsqueeze(1).broadcast_to([1, BLOCKS + 1, E]),
                              ALU.mult).then_inc(table, 1)
            dve.wait_ge(table, 8)
            dve.tensor_reduce(b_first[:, :], t408[:, :, :], AX.X, ALU.add).then_inc(table, 1)
            dve.tensor_scalar(w_col[:, :], b_exp[:, :], float(HID), None, ALU.mult).then_inc(tables_ready, 1)
            dve.wait_ge(table, 9)
            dve.tensor_tensor(b_row[:, :], block_no[:, :], b_first[:, :], ALU.subtract).then_inc(table, 1)
            dve.wait_ge(table, 10)
            dve.tensor_scalar(b_first[:, :], b_exp[:, :], float(REGION), None, ALU.mult).then_inc(table, 1)
            dve.wait_ge(table, 11)
            dve.scalar_tensor_tensor(b_row[:, :], b_row[:, :], float(BR), b_first[:, :], ALU.mult, ALU.add).then_inc(table, 1)
            dve.wait_ge(table, 12)
            dve.tensor_scalar(row0[:, :], b_row[:, :], float(E * REGION), None, ALU.min).then_inc(tables_ready, 1)
            for n in range(2, 2 * NE):
                weights_lo(n)

            def unit(n, k):
                dve.wait_ge(hhi_done, n + 1)
                need(dve, d_done, n - RING + 1)
                dve.tensor_tensor(h_lo[k % RING][:, :], h32[k % RING][:, :], h_hi[k % RING][:, :],
                                  ALU.subtract).then_inc(hlo_done, 1)

            def block_in(j, b):
                dve.wait_ge(xT_hi_done, j + 1)
                dve.tensor_tensor(xT_lo[b % 2][:, :], X_ps[b % 2][:, 0:BR], xT_hi[b % 2][:, :],
                                  ALU.subtract).then_inc(xT_lo_done, 1)

            def block_out(i, b):
                dve.wait_ge(d_done, i * (LB * BU) + N0 + b * BU + BU)
                need(dve, scattered[b % RING], i * (32 * LB // RING) + 32 * (b // RING))
                for t in range(BT):
                    last = dve.tensor_scalar(y_sb[b % RING][:, t, :], Y_ps[b % 2][:, t * D:t * D + D],
                                             xrow[b][:, t, D + 1:D + 2], None, ALU.mult)
                last.then_inc(y_done, 1)

            def shared_out(g):
                dve.wait_ge(d_done, (0 if g < BEFORE else N1) + (g % BEFORE + 1) * CH)
                tiles = x_all[:, g * GT:g * GT + GT, :]
                dve.scalar_tensor_tensor(tiles, Y_ps[g % 2][:, :].rearrange("p (t d) -> p t d", d=D), 1.0 / WSCALE, tiles,
                                         ALU.mult, ALU.add).then_inc(y_done, 1)

            def routed_in(g):
                dve.wait_ge(yt_summed, g + 1)
                dve.wait_ge(y_done, g + 1 + (BLOCKS if g >= BEFORE else 0))
                tiles = x_all[:, g * GT:g * GT + GT, :]
                dve.tensor_tensor(tiles, tiles, yt[g % 2][:, 0, :, :], ALU.add).then_inc(routed_added, 1)

            def routed(i, first, end):
                for b in range(LB):
                    for q in range(BU):
                        unit(i * (LB * BU) + N0 + b * BU + q, b * BU + q)
                        if q == 0:
                            if not (end and b == LB - 1):
                                block_in(i * LB + b + 1, b + 1)
                            if first and b == 0:
                                shared_out(BEFORE - 1)
                            else:
                                block_out(i if b else i - 1, (b - 1) % LB)
            for n in range(N0):
                unit(n, n)
                if n == N0 - BU:
                    block_in(0, 0)
                if n % CH == 0 and n > 0:
                    shared_out(n // CH - 1)
            routed(0, True, False)
            with dve.Fori(1, BLOCKS // LB - 1) as i:
                routed(i, False, False)
            routed(BLOCKS // LB - 1, False, True)
            adds = {CH + 1: 0, CH + 2: 1, CH + 3: 2, 2 * CH + 1: 3, 2 * CH + 2: 4, 2 * CH + 3: 5, 3 * CH + 1: 6}
            for n in range(N1, NU):
                unit(n, n)
                if n == N1:
                    block_out(BLOCKS // LB - 1, LB - 1)
                elif (n - N1) % CH == 0:
                    shared_out(BEFORE + (n - N1) // CH - 1)
                if n - N1 in adds:
                    routed_in(adds[n - N1])
            shared_out(FG - 1)
            routed_in(FG - 1)

        @block.tensor
        def _(pe):
            pe.wait_ge(consts_pool, CONSTS)
            pe.wait_ge(mats_in, 16 * len(MATS))
            for n in range(2):
                for m in range(4):
                    last = pe.transpose(X_ps[n][:, m * P:m * P + P], mat_in[:, 4 * n + m, :], ident[:, :])
                last.then_inc(setup_pe, 1)
            pe.wait_ge(rows_in, 16 * (len(ROWS) + 4))
            pe.wait_ge(gate_loaded, 16)
            pe.wait_ge(setup_ev, 1)
            nv = len(ROWS)
            pe.transpose(X_ps[0][:, 0:nv], row_in[:, :], ident[0:nv, 0:nv])
            pe.transpose(X_ps[0][:, nv:nv + E], gate_in[:, :], ident[0:E, 0:E]).then_inc(setup_pe, 1)
            pe.wait_ge(setup_ev, 2)
            pe.matmul(X_ps[1][:, :], ones_row[:, :], row1[:, :, :], start=True, stop=True).then_inc(setup_pe, 1)
            pe.wait_ge(setup_ev, 3)
            for n, (bv, wo) in enumerate((("xbv", "xWo"), ("abv", "aWo"))):
                c = ROWS.index(bv)
                last = pe.matmul(X_ps[0][:, n * D:n * D + D], vec[:, c:c + 1].broadcast_to([P, P]),
                                 WT[:, MATS.index(wo), :], start=True, stop=True)
            last.then_inc(setup_pe, 1)
            pe.wait_ge(setup_ev, 4)
            pe.wait_ge(setup_dve, 3)

            def W(name):
                return WT[:, MATS.index(name), :]

            def shared_bank(name, h):
                x = XB[name]
                if name == "xnT":
                    pe.wait_ge(normed["x"], 2 * h + 2)
                    for t in range(2):
                        last = pe.transpose(x[:, t * P:t * P + P], xn[:, t, :], ident[:, :])
                if name == "ctxT":
                    pe.wait_ge(ctx_loaded, 16 * h + 16)
                    for b in range(CB):
                        last = pe.transpose(x[:, b * P:b * P + P], ctx_in[:, parity["a"], b, :], ident[:, :])
                if name == "q":
                    pe.wait_ge(ev["xnT"], h + 1)
                    last = pe.matmul(x[:, 0:2 * P], W("xWq"), xnT_sb[:, :], start=True, stop=True)
                if name == "k":
                    pe.wait_ge(ev["ctxT"], h + 1)
                    last = pe.matmul(x[:, :], W("xWk"), cT[:, :], start=True, stop=True)
                if name == "v":
                    for b in range(CB):
                        last = pe.matmul(x[:, b * D:b * D + D], cT[:, b * SK:b * SK + SK], W("xWv"), start=True, stop=True)
                if name == "oT":
                    pe.wait_ge(norm_done, 2 * h + 2)
                    for t in range(2):
                        last = pe.transpose(x[:, t * P:t * P + P],
                                            O_tok[:, t, :, :, :].rearrange("p t o d -> p (t o d)"), ident[:, :])
                if name == "y":
                    pe.wait_ge(ev["oT"], h + 1)
                    for t in range(2):
                        last = pe.matmul(x[:, t * D:t * D + D], OT[:, t * P:t * P + P], W("xWo"), start=True, stop=True)
                if name == "x1T":
                    pe.wait_ge(normed["x1"], 2 * h + 2)
                    for t in range(2):
                        last = pe.transpose(x[:, t * P:t * P + P], x1n[:, t, :], ident[:, :])
                if name == "qk":
                    pe.wait_ge(ev["x1T"], h + 1)
                    pe.matmul(x[:, 0:2 * P], W("aWq"), x1T_sb[:, :], start=True, stop=True)
                    last = pe.matmul(x[:, 2 * P:4 * P], W("aWk"), x1T_sb[:, :], start=True, stop=True)
                if name == "v2":
                    for t in range(2):
                        last = pe.matmul(x[:, t * D:t * D + D], x1T_sb[:, t * P:t * P + P], W("aWv"), start=True, stop=True)
                if name == "s":
                    pe.wait_ge(ev["qk"], h + 1)
                    for t in range(2):
                        last = pe.matmul(x[:, t * P:t * P + P], QT[:, t * P:t * P + P], KT[:, t * P:t * P + P],
                                         start=True, stop=True)
                if name == "pT":
                    pe.wait_ge(p2_done, 2 * h + 2)
                    for t in range(2):
                        last = pe.transpose(x[:, t * P:t * P + P], P2[:, t, :], ident[:, :])
                if name == "av":
                    pe.wait_ge(ev["pT"], h + 1)
                    pe.wait_ge(ev["v2"], h + 1)
                    for t in range(2):
                        last = pe.matmul(x[:, t * P:t * P + P], V2[:, t, :], P2T[:, t * P:t * P + P], start=True, stop=True)
                if name == "z":
                    pe.wait_ge(ev["av"], h + 1)
                    for t in range(2):
                        last = pe.matmul(x[:, t * D:t * D + D], AT[:, t * P:t * P + P], W("aWo"), start=True, stop=True)
                if name == "x2T":
                    pe.wait_ge(normed["x2"], 2 * h + 2)
                    for t in range(2):
                        last = pe.transpose(x[:, t * P:t * P + P], x2n[:, t, :], ident[:, :])
                last.then_inc(mm[name], 1)

            parity = {}

            def step(h, r):
                parity["a"] = 1 - r
                for s in range(UNITS):
                    u, p, g = UNITS * h + s, s // GROUPS, s % GROUPS
                    rows_ = slice(g * 32, g * 32 + 32)
                    if valid(h):
                        pe.wait_ge(max_done, u + 1)
                        need(pe, exp_done, u - 1)
                        if s == 0:
                            pe.wait_ge(qm_lo_ready, h + 1)
                            pe.wait_ge(ev["k"], h + 1)
                        for n in range(4):
                            pe.matmul(T_ps[s % 2][:, n * P:n * P + P],
                                      m_bf[:, r * UNITS + s, n:n + 1].broadcast_to([P, P]), neg_ident[:, :],
                                      start=(n == 0), stop=False)
                        for b in range(2):
                            cb = 2 * p + b
                            for n, (kk, qq) in enumerate(((k_hi, qm_hi), (k_hi, qm_lo), (k_lo, qm_hi))):
                                last = pe.matmul(T_ps[s % 2][:, b * 256:b * 256 + 256],
                                                 kk[r][rows_, cb * SK:cb * SK + SK],
                                                 qq[r][rows_, cb, :, :].rearrange("p j q -> p (j q)"),
                                                 start=False, stop=(b == 1 and n == 2))
                        last.then_inc(t_done, 1)
                    hm, sm_ = (h, s + 2) if s < UNITS - 2 else (h + 1, s + 2 - UNITS)
                    if valid(hm):
                        rm = r if sm_ == s + 2 else 1 - r
                        pm, gm = sm_ // GROUPS, sm_ % GROUPS
                        if sm_ == 0:
                            pe.wait_ge(qm_hi_ready, JH * (hm + 1))
                            pe.wait_ge(k_hi_ready, hm + 1)
                        need(pe, max_done, u + 1)
                        mrows = slice(gm * 32, gm * 32 + 32)
                        for b in range(2):
                            cb = 2 * pm + b
                            for jp in range(2):
                                last = pe.matmul(M_ps[s % 2][:, (2 * b + jp) * P:(2 * b + jp) * P + P],
                                                 qm_hi[rm][mrows, cb, 2 * jp:2 * jp + 2, :].rearrange("p j q -> p (j q)"),
                                                 k_hi[rm][mrows, cb * SK:cb * SK + SK], start=True, stop=True)
                        last.then_inc(m_done, 1)
                    hv, sv = (h, s - LAG) if s >= LAG else (h - 1, s - LAG + UNITS)
                    if valid(hv):
                        rv = r if s >= LAG else 1 - r
                        pv, gv = sv // GROUPS, sv % GROUPS
                        pe.wait_ge(*low_of(hv, sv))
                        if sv == 0:
                            pe.wait_ge(ev["v"], hv + 1)
                        if gv == 0:
                            need(pe, norm_done, hv * 2 + pv - 1)
                        for b in range(2):
                            for jp in range(2):
                                t = 2 * gv + jp
                                c0 = (b * 8 + t) * VW
                                w0 = (2 * b + jp) * P
                                for n, (pp, vv) in enumerate(((p_hi, V_hi), (p_hi, V_lo), (p_lo, V_hi))):
                                    last = pe.matmul(PV_ps[pv][:, c0:c0 + VW], pp[:, sv % 4, w0:w0 + P],
                                                     vv[rv][:, (2 * pv + b) * 8 + t, :], start=(n == 0), stop=(n == 2))
                        last.then_inc(v_done, 1)
                    for name, slot, rel, _ in MISC:
                        if slot == s and valid(h + rel):
                            bank_free(pe, name, h)
                            shared_bank(name, h + rel)
            all_steps(pe, step)
            pe.wait_ge(gate_split, 2)

            for name in ("x2T", "x1T", "z"):
                pe.wait_ge(ev[name], HALVES)
            for t in range(NT):
                for n, (part, g) in enumerate(((x2T_hi, gate_hi), (x2T_hi, gate_lo), (x2T_lo, gate_hi))):
                    last = pe.matmul(X_ps[0][:, t * E:t * E + E], part[:, t * P:t * P + P], g[:, :],
                                     start=(n == 0), stop=(n == 2))
            last.then_inc(lg_pe, 1)
            def weights(n):
                pe.wait_ge(w_loaded[n % 2], 16 * (n // 2 + 1))
                if n == 0:
                    pe.wait_ge(lg_ev, 1)
                need(pe, wt_lo, n - 1)
                for c in range(CH):
                    last = pe.transpose(X_ps[n % 2][:, c * P:c * P + P], w_in[:, n % 2, c, :], ident[:, :])
                last.then_inc(wt_pe, 1)
            weights(0)
            weights(1)
            pe.wait_ge(picked, 1)
            pe.matmul(R_ps[:, 0:NT * E], before[:, :], either[:, :, :].rearrange("p t e -> p (t e)"), start=True, stop=False)
            for t in range(NT - 1):
                pe.matmul(R_ps[:, (t + 1) * E:NT * E], ones16[:, :],
                          either[:, t:t + 1, :].broadcast_to([P, NT - 1 - t, E]), start=False, stop=(t == NT - 2))
            pe.wait_ge(picked, 2)
            pe.matmul(R_ps[:, NT * E:NT * E + E], ones16[:, :], per_tile[:, :], start=True, stop=True).then_inc(ranked, 1)
            for n in range(2, 2 * NE):
                weights(n)
            pe.wait_ge(wt_lo, 2 * NE)
            pe.wait_ge(table, 1)
            pe.wait_ge(placed, 1)

            def up(n, k, w, xx, width):
                need(pe, silu_done, n - RING + 1)
                for c in range(U_N // width):
                    for m, (ww, part) in enumerate(((W1_hi, 0), (W1_hi, 1), (W1_lo, 0))):
                        last = pe.matmul(U_ps[k % RING][:, c * width:c * width + width], ww[:, w(c)], xx[part],
                                         start=(m == 0), stop=(m == 2))
                last.then_inc(u_done, 1)

            def down(n, k, w, y, width, first, end):
                pe.wait_ge(hhi_done, n + 1)
                pe.wait_ge(hlo_done, n + 1)
                chunks, tiles = U_N // width, width // P
                for c in range(chunks):
                    for t in range(tiles):
                        cols = slice(c * width + t * P, c * width + t * P + P)
                        for m, (hh, ww) in enumerate(((h_hi, W2_hi), (h_hi, W2_lo), (h_lo, W2_hi))):
                            last = pe.matmul(y[:, t * D:t * D + D], hh[k % RING][:, cols], ww[:, w(c)],
                                             start=(first and c == 0 and t == 0 and m == 0),
                                             stop=(end and c == chunks - 1 and t == tiles - 1 and m == 2))
                last.then_inc(d_done, 1)

            def shared_up(n):
                g, c = (n // CH) if n < N0 else BEFORE + (n - N1) // CH, n % CH
                tokens = slice(g * GT * P, (g + 1) * GT * P)
                up(n, n, lambda _: slice(E * HID + c * P, E * HID + c * P + P), (x2T_hi[:, tokens], x2T_lo[:, tokens]), U_N)

            def shared_down(n):
                g, c = (n // CH) if n < N0 else BEFORE + (n - N1) // CH, n % CH
                if c == 0:
                    need(pe, y_done, g - 1 + (BLOCKS if n >= N1 else 0))
                down(n, n, lambda _: slice(E * HID + c * P, E * HID + c * P + P), Y_ps[g % 2], U_N, c == 0, c == CH - 1)

            def block_rows(j, b, i):
                need(pe, xT_lo_done, j - 1)
                pe.wait_ge(loaded[b % LB], (i + b // LB) * 16 + 16)
                for t in range(BT):
                    last = pe.transpose(X_ps[b % 2][:, t * P:t * P + P], xrow[b % LB][:, t, 0:D], ident[:, :])
                last.then_inc(xT_pe, 1)

            def weights_of(j):
                return pe.value_load(w_col[0:1, one(j)], min_val=0, max_val=E * HID)

            def routed_up(i, b, q, col):
                j = i * LB + b
                if q == 0:
                    pe.wait_ge(xT_hi_done, j + 1)
                    pe.wait_ge(xT_lo_done, j + 1)
                up(i * (LB * BU) + N0 + b * BU + q, b * BU + q, lambda c: bass.ds(col + (q * BU + c) * P, P),
                   (xT_hi[b % 2][:, :], xT_lo[b % 2][:, :]), BR)

            def routed_down(i, b, q, col):
                if q == 0:
                    pe.wait_ge(y_done, i * LB + BEFORE + b - 1)
                down(i * (LB * BU) + N0 + b * BU + q, b * BU + q, lambda c: bass.ds(col + (q * BU + c) * P, P),
                     Y_ps[b % 2], BR, q == 0, q == BU - 1)

            def routed(i, end):
                col = weights_of(i * LB)
                for b in range(LB):
                    final = end and b == LB - 1
                    ahead = None if final else weights_of(i * LB + b + 1)
                    for q in range(BU):
                        if final:
                            shared_up(N1 + q)
                        else:
                            routed_up(i, b + 1, q, ahead)
                        if q == 0 and not (end and b >= LB - 2):
                            block_rows(i * LB + b + 2, b + 2, i)
                        routed_down(i, b, q, col)
                    col = ahead

            for n in range(BU):
                shared_up(n)
            for n in range(N0):
                if n < N0 - BU:
                    shared_up(n + BU)
                else:
                    if n == N0 - BU:
                        pe.wait_ge(tables_ready, 2)
                        ahead = weights_of(0)
                    routed_up(0, 0, n - (N0 - BU), ahead)
                if n == N0 - 2 * BU:
                    block_rows(0, 0, 0)
                if n == N0 - BU:
                    block_rows(1, 1, 0)
                shared_down(n)
            routed(0, False)
            with pe.Fori(1, BLOCKS // LB - 1) as i:
                routed(i, False)
            routed(BLOCKS // LB - 1, True)
            for n in range(N1, NU):
                if n + BU < NU:
                    shared_up(n + BU)
                shared_down(n)

    return nc


_NAMES = {"xWq": "L0_xattn_Wq", "xWk": "L0_xattn_Wk", "xWv": "L0_xattn_Wv", "xWo": "L0_xattn_Wo",
          "aWq": "L0_attn_Wq", "aWk": "L0_attn_Wk", "aWv": "L0_attn_Wv", "aWo": "L0_attn_Wo",
          "xbq": "L0_xattn_bq", "xbk": "L0_xattn_bk", "xbv": "L0_xattn_bv", "xbo": "L0_xattn_bo",
          "abq": "L0_attn_bq", "abk": "L0_attn_bk", "abv": "L0_attn_bv", "abo": "L0_attn_bo",
          "gamma": "L0_xattn_gamma", "beta": "L0_xattn_beta"}


def kernel(**inputs):
    import concourse.bacc as bacc
    from concourse.bass_utils import run_bass_kernel_spmd

    nc = bacc.Bacc("TRN2", target_bir_lowering=False, num_devices=1)
    arrays, aps = {}, {}
    for name, a in inputs.items():
        a = np.ascontiguousarray(a)
        arrays["in_" + name] = a
        aps[name] = nc.dram_tensor("in_" + name, a.shape, mybir.dt.from_np(a.dtype), kind="ExternalInput").ap()
    out = nc.dram_tensor("out_0", (B, S, D), F32, kind="ExternalOutput").ap()
    perceiver(nc, aps["x"], aps["ctx_1024"], [aps[_NAMES[n]] for n in MATS], [aps[_NAMES[n]] for n in ROWS],
              aps["L0_ffn_shared_w1"], aps["L0_ffn_shared_w2"], aps["L0_ffn_experts_w1"],
              aps["L0_ffn_experts_w2"], aps["L0_ffn_gate_w"], out)
    r = run_bass_kernel_spmd(nc, [arrays], core_ids=[0])
    return r.results[0]["out_0"]
```

```python
import numpy as np
import concourse.bass as bass
from concourse import mybir
from contextlib import ExitStack

F32 = mybir.dt.float32
F16 = mybir.dt.float16
BF16 = mybir.dt.bfloat16
U32 = mybir.dt.uint32
I32 = mybir.dt.int32
ALU = mybir.AluOpType
ACT = mybir.ActivationFunctionType
AX = mybir.AxisListType

B, S, SK, D = 64, 64, 128, 128
HEADS = 16
HD = D // HEADS
P = 128
EPS = 1e-5
E, HID = 8, 512
XSCALE = float(HD) ** -0.5
ASCALE = float(D) ** -0.5
MASKED = -1e30
CONSTS = 56

NT = B * S // P
HALVES = 16
PAIRS = 2
CB = 4
GROUPS = 4
JH = 4
UNITS = PAIRS * GROUPS
VW = 2 * HD + 1
NE = E + 1
CH = HID // P
RING = 4

GT = 4
FG = NT // GT
AHEAD = 3
EARLY = 2
BEFORE = 6
BT = 2
BR = BT * P
U_N = GT * P
BU = CH // 2
T = B * S
REGION = T + BR
ROW = D + 2
BLOCKS = -(-((2 * T + E * (BR - 1)) // BR) // 8) * 8
LB = 8
N0 = BEFORE * CH
N1 = N0 + BLOCKS * BU
NU = N1 + (FG - BEFORE) * CH
NOWHERE = 1 << 20

ROWS = ["xbq", "xbk", "xbv", "xbo", "abq", "abk", "abv", "abo", "gamma", "beta"]
MATS = ["xWq", "xWk", "xWv", "xWo", "aWq", "aWk", "aWv", "aWo"]

MISC = [("xnT", 0, 1, 0), ("lg", 0, 0, 0), ("qk", 0, -2, 1),
        ("v2", 1, -2, 0), ("s", 1, -2, 1),
        ("q", 2, 1, 0), ("oT", 2, -1, 1),
        ("ctxT", 3, 1, 0), ("y", 3, -1, 1),
        ("k", 4, 1, 0), ("rank", 4, 0, 0), ("pT", 4, -2, 1),
        ("v", 5, 1, 1), ("av", 5, -2, 0),
        ("x2T", 6, -3, 1), ("z", 6, -2, 0),
        ("x1T", 7, -1, 1)]
ONCE = ("lg", "rank")
GATE_STEPS = 9
PARTS = ((0, NT - 8), (NT - 8, NT))
PART_STEP = HALVES - 1
SENT = {PART_STEP: (0, 0, 0, 0, 0, 0, 1, 1), PART_STEP + 1: (2, 2, 2, 1, 0, 0, 3, 0), PART_STEP + 2: (0, 0, 4, 4, 4, 3, 0, 0)}
assert PARTS[0][1] <= 2 * (PART_STEP - 3)
WEIGHTS_FROM = HALVES * 8 + 2
LAG = 2
ON_POOL = (1, 4, 6)
WSCALE = 256.0
SLOT_OF = {n: s for n, s, _, _ in MISC}


def valid(h):
    return not isinstance(h, int) or 0 <= h < HALVES


def runs(name, h):
    return valid(h) and (name not in ONCE or isinstance(h, int) and h == PART_STEP)


def need(eng, sem, value):
    if not isinstance(value, int) or value > 0:
        eng.wait_ge(sem, value)


def perceiver(nc, x, ctx, mats, rows, sw1, sw2, ew1, ew2, gate_w, out):
    es = ExitStack()
    with es:
        def sb(name, shape, dt=F32):
            return es.enter_context(nc.sbuf_tensor(name, shape, dt))

        def sem(name):
            return es.enter_context(nc.semaphore(name))

        attention = ExitStack()

        def asb(name, shape, dt=F32):
            return attention.enter_context(nc.sbuf_tensor(name, shape, dt))

        x_all = sb("x_all", [P, NT, D])
        x2T_hi = sb("x2T_hi", [P, NT * P], F16)
        x2T_lo = sb("x2T_lo", [P, NT * P], F16)
        rows_of = sb("rows_of", [P, NT, 2, ROW])
        ident = sb("ident", [P, P])
        neg_ident = sb("neg_ident", [P, P], BF16)
        head_sel = sb("head_sel", [P, GROUPS, JH])
        head_mask = sb("head_mask", [P, JH])
        causal = sb("causal", [P, P])
        minus_half = sb("minus_half", [P, 2])
        eps2 = sb("eps2", [P, 2])
        scratch = sb("scratch", [P, 8])
        row_in = sb("row_in", [len(ROWS), D])
        vec = sb("vec", [P, len(ROWS) + E])
        bcast = sb("bcast", [P, 4, D])
        gate_in = sb("gate_in", [E, D])
        gateT = vec[:, len(ROWS):len(ROWS) + E]
        gate_hi = sb("gate_hi", [P, E], F16)
        gate_lo = sb("gate_lo", [P, E], F16)
        iota8 = sb("iota8", [P, E])
        before = sb("before", [P, P], F16)
        ones16 = sb("ones16", [P, P], F16)
        region = sb("region", [P, E])
        block_no = sb("block_no", [1, BLOCKS + 1])
        block_no_i = sb("block_no_i", [1, BLOCKS + 1], I32)
        fills = sb("fills", [1, T // BR])
        fills_i = sb("fills_i", [1, T // BR], I32)
        upto = sb("upto", [1, E, E])
        padding = sb("padding", [P, BT, ROW])
        wait_mark = sb("wait_mark", [P, 1])
        exp_mark = sb("exp_mark", [P, 1])
        w_in = sb("w_in", [P, 4, CH, P])
        W1_hi = sb("W1_hi", [P, NE * HID], F16)
        W1_lo = sb("W1_lo", [P, NE * HID], F16)
        W2_hi = sb("W2_hi", [P, NE * HID], F16)
        W2_lo = sb("W2_lo", [P, NE * HID], F16)
        lg = sb("lg", [P, NT, E])
        top = sb("top", [P, NT, 8])
        idx = sb("idx", [P, NT, 8], U32)
        idxf = sb("idxf", [P, NT, 2])
        gates = sb("gates", [P, NT, 2])
        second_exp = sb("second_exp", [P, NT])
        chosen = [sb(f"chosen{n}", [P, NT, E], F16) for n in range(2)]
        either = sb("either", [P, NT, E], F16)
        row_at = sb("row_at", [P, NT, E])
        row_pick = sb("row_pick", [P, NT, E])
        row_f = sb("row_f", [P, NT, 2])
        row_no = sb("row_no", [P, 2, NT], U32)
        per_tile = sb("per_tile", [P, 2, E], F16)
        load = sb("load", [1, E])
        fill = sb("fill", [1, E, T // BR])
        nblocks = sb("nblocks", [1, E])
        last_block = sb("last_block", [1, E])
        blocks_upto = sb("blocks_upto", [1, E, E])
        passed = sb("passed", [1, BLOCKS + 1, E])
        blocks_passed = sb("blocks_passed", [1, BLOCKS + 1, E])
        block_expert = sb("block_expert", [1, BLOCKS + 1])
        block_row = sb("block_row", [1, BLOCKS + 1])
        expert_first = sb("expert_first", [1, BLOCKS + 1])
        w_col = sb("w_col", [1, BLOCKS + 1], I32)
        row0 = sb("row0", [1, BLOCKS + 1], I32)
        pad0 = sb("pad0", [1, E], I32)
        mv = sb("mv", [P, 4, 2, 2])
        st = sb("st", [P, 4, 2, 6])
        rstd = sb("rstd", [P, 4, 2])
        vpe = sb("vpe", [P, 4, 2])
        x2n = sb("x2n", [P, 2, D])
        mat_in = asb("mat_in", [P, len(MATS), D])
        WT = asb("WT", [P, len(MATS), D])
        ctx_in = asb("ctx_in", [P, 2, CB, D])
        xn = asb("xn", [P, 2, D])
        xnT_sb = asb("xnT_sb", [P, 2 * P])
        cT = asb("cT", [P, CB * SK])
        q32 = asb("q32", [P, 2 * P])
        q_hi = asb("q_hi", [P, 2 * P], F16)
        q_lo = asb("q_lo", [P, 2 * P])
        qm_hi = [asb(f"qm_hi{r}", [P, CB, JH, S], F16) for r in range(2)]
        qm_lo = [asb(f"qm_lo{r}", [P, CB, JH, S], F16) for r in range(2)]
        k_hi = [asb(f"k_hi{r}", [P, CB * SK], F16) for r in range(2)]
        k_lo = [asb(f"k_lo{r}", [P, CB * SK], F16) for r in range(2)]
        V_hi = [asb(f"V_hi{r}", [P, CB * HEADS // 2, VW], F16) for r in range(2)]
        V_lo = [asb(f"V_lo{r}", [P, CB * HEADS // 2, VW], F16) for r in range(2)]
        m_bf = asb("m_bf", [P, 2 * UNITS, 4], BF16)
        p32 = asb("p32", [P, 2, 512])
        p_hi = asb("p_hi", [P, 4, 512], F16)
        p_lo = asb("p_lo", [P, 4, 512], F16)
        rden = asb("rden", [P, 2, 16])
        O_tok = asb("O_tok", [P, PAIRS, HEADS // 2, 2, HD])
        OT = asb("OT", [P, 2 * P])
        yb = asb("yb", [P, 2, D])
        yn = asb("yn", [P, 2, D])
        yg = asb("yg", [P, 2, D])
        xb = asb("xb", [P, 2, D])
        x1 = [asb(f"x1_{r}", [P, 2, D]) for r in range(2)]
        x1b = [asb(f"x1b_{r}", [P, 2, D]) for r in range(2)]
        x1n = asb("x1n", [P, 2, D])
        x1T_sb = asb("x1T_sb", [P, 2 * P])
        QT = asb("QT", [P, 2 * P])
        KT = asb("KT", [P, 2 * P])
        V2 = asb("V2", [P, 2, D])
        sm = asb("sm", [P, 2, P])
        smax = asb("smax", [P, 2])
        nbias = asb("nbias", [P, 2])
        rs = asb("rs", [P, 2])
        rrs = asb("rrs", [P, 2])
        P2 = asb("P2", [P, 2, P])
        P2T = asb("P2T", [P, 2 * P])
        AT = asb("AT", [P, 2 * P])
        attention.close()
        h32 = [sb(f"h32_{r}", [P, U_N]) for r in range(RING)]
        h_hi = [sb(f"h_hi{r}", [P, U_N], F16) for r in range(RING)]
        h_lo = [sb(f"h_lo{r}", [P, U_N], F16) for r in range(RING)]
        xrow = [sb(f"xrow{r}", [P, BT, ROW]) for r in range(LB)]
        xT_hi = [sb(f"xT_hi{r}", [P, BR], F16) for r in range(2)]
        xT_lo = [sb(f"xT_lo{r}", [P, BR], F16) for r in range(2)]
        y_sb = [sb(f"y_sb{r}", [P, BT, D]) for r in range(RING)]
        yt = [sb(f"yt{g}", [P, 2, GT, D]) for g in range(FG)]

        listed = nc.dram_tensor("listed", (E * REGION + BR, ROW), F32).ap()
        results = nc.dram_tensor("results", (2 * T, D), F32).ap()

        bank = [es.enter_context(nc.psum_tensor(f"bank{n}", [P, 512], F32)) for n in range(8)]
        T_ps = bank[0:2]
        M_ps = bank[2:4]
        PV_ps = bank[4:6]
        X_ps = bank[6:8]
        XB = {n: X_ps[b] for n, _, _, b in MISC}
        W_ps = bank[2:6]
        G_ps = X_ps[0]
        U_ps = bank[0:4]
        Y_ps = bank[4:6]
        R_ps = X_ps[0]

        x_mats_in, a_mats_in = sem("x_mats_in"), sem("a_mats_in")
        rows_in, x_in, ctx_loaded = sem("rows_in"), sem("x_in"), sem("ctx_loaded")
        w_loaded = [sem(f"w_loaded{r}") for r in range(4)]
        gate_loaded, gate_split = sem("gate_loaded"), sem("gate_split")
        consts_pool = sem("consts_pool")
        setup_pe, setup_ev, setup_dve = sem("setup_pe"), sem("setup_ev"), sem("setup_dve")
        mm = {n: sem(f"mm_{n}") for n in SLOT_OF}
        ev = {n: sem(f"ev_{n}") for n in SLOT_OF}
        m_done, max_done = sem("m_done"), sem("max_done")
        t_done, exp_done = sem("t_done"), sem("exp_done")
        v_done, norm_done, norm_step = sem("v_done"), sem("norm_done"), sem("norm_step")
        p_hi_done, p_lo_dve, p_lo_pool = sem("p_hi_done"), sem("p_lo_dve"), sem("p_lo_pool")
        q_ready, k_hi_ready, v_hi_ready = sem("q_ready"), sem("k_hi_ready"), sem("v_hi_ready")
        qm_hi_ready, qlo_full, qm_lo_ready = sem("qm_hi_ready"), sem("qlo_full"), sem("qm_lo_ready")
        LN = ["x", "y", "x1", "x2"]
        stat = {n: sem(f"stat_{n}") for n in LN}
        vpe_done = {n: sem(f"vpe_{n}") for n in LN}
        rstd_done = {n: sem(f"rstd_{n}") for n in LN}
        normed = {n: sem(f"normed_{n}") for n in LN}
        xb_done, yg_done, x1_done, x1b_done = sem("xb_done"), sem("yg_done"), sem("x1_done"), sem("x1b_done")
        x2_done = ev["z"]
        sm_max, nbias_done, p2_done, rrs_done = sem("sm_max"), sem("nbias_done"), sem("p2_done"), sem("rrs_done")
        x2T_hi_done = sem("x2T_hi_done")
        wt_pe, wt_hi, wt_lo = sem("wt_pe"), sem("wt_hi"), sem("wt_lo")
        top_done, gate_step, gate_exp = sem("top_done"), sem("gate_step"), sem("gate_exp")
        u_done, silu_done, hhi_done, hlo_done = sem("u_done"), sem("silu_done"), sem("hhi_done"), sem("hlo_done")
        d_done, y_done = sem("d_done"), sem("y_done")
        picked, placed, padded = sem("picked"), sem("placed"), sem("padded")
        table, tables_ready = sem("table"), sem("tables_ready")
        row_step, rows_full, block_seen = sem("row_step"), sem("rows_full"), sem("block_seen")
        listed_done = sem("listed_done")
        loaded = [sem(f"loaded{r}") for r in range(LB)]
        xT_pe, xT_hi_done, xT_lo_done = sem("xT_pe"), sem("xT_hi_done"), sem("xT_lo_done")
        scattered = [sem(f"scattered{r}") for r in range(RING)]
        yt_loaded = [sem(f"yt_loaded{g}") for g in range(FG)]
        yt_summed, odd_summed, routed_added = sem("yt_summed"), sem("odd_summed"), sem("routed_added")
        stored = sem("stored")

        block = es.enter_context(nc.Block())

        x_v = x.rearrange("(t two) s d -> (two s) t d", two=2)
        out_v = out.rearrange("(t two) s d -> (two s) t d", two=2)
        ctx_v = ctx.rearrange("b k d -> k b d")

        def two_tiles(h):
            return slice(2 * h, 2 * h + 2) if isinstance(h, int) else bass.ds(h * 2, 2)

        def one_tile(h, t):
            return slice(2 * h + t, 2 * h + t + 1) if isinstance(h, int) else bass.ds(h * 2 + t, 1)

        def half_cols(h):
            return slice(2 * P * h, 2 * P * (h + 1)) if isinstance(h, int) else bass.ds(h * (2 * P), 2 * P)

        def most_steps(eng, step, setup):
            for h in range(-2, 4):
                if h == 0:
                    setup()
                step(h, h % 2)
            with eng.Fori(2, (HALVES - 2) // 2) as i:
                step(i * 2, 0)
                step(i * 2 + 1, 1)
            for h in range(HALVES - 2, HALVES + 2):
                step(h, h % 2)

        def beside(h, s):
            return s if isinstance(h, int) and h == PART_STEP else None

        def weights_at(h, s):
            n = h * UNITS + s - WEIGHTS_FROM if isinstance(h, int) else -1
            slots = (HALVES + 2) * UNITS - WEIGHTS_FROM
            twice = 2 * NE - slots
            if not 0 <= n < slots:
                return range(0)
            n2 = n - (slots - twice)
            return range(n, n + 1) if n2 < 0 else range(slots - twice + 2 * n2, slots - twice + 2 * n2 + 2)

        def low_of(h, s):
            if s in ON_POOL:
                return p_lo_pool, h * len(ON_POOL) + ON_POOL.index(s) + 1
            others = [n for n in range(UNITS) if n not in ON_POOL]
            return p_lo_dve, h * len(others) + others.index(s) + 1

        def low_part(eng, h, s):
            eng.wait_ge(p_hi_done, UNITS * h + s + 1)
            need(eng, v_done, UNITS * h + s - 3)
            eng.tensor_tensor(p_lo[:, s % 4, :], p32[:, s % 2, :], p_hi[:, s % 4, :],
                              ALU.subtract).then_inc(low_of(h, s)[0], 1)

        def bank_free(eng, name, h):
            at = [n for n, *_ in MISC].index(name)
            own = MISC[at][3]
            for back in list(range(at - 1, -1, -1)) + list(range(len(MISC) - 1, at, -1)):
                n, _, rel, b = MISC[back]
                hh = h + rel - (1 if back > at else 0)
                if b == own and runs(n, hh):
                    eng.wait_ge(ev[n], 1 if n in ONCE else (hh + 1) * (2 if n == "z" else 1))
                    return

        def one(n):
            return slice(n, n + 1) if isinstance(n, int) else bass.ds(n, 1)

        @block.sync
        def _(sp):
            def load_mats(first, loaded_sem):
                for n in range(first, first + 4):
                    sp.dma_start(mat_in[:, n, :], mats[n]).then_inc(loaded_sem, 16)

            def load_x(h):
                tiles = two_tiles(h)
                need(sp, x_in, 16 * h)
                sp.dma_start(x_all[:, tiles, :], x_v[:, tiles, :]).then_inc(x_in, 16)

            def load_ctx(h, r):
                batches = slice(CB * h, CB * h + CB) if isinstance(h, int) else bass.ds(h * CB, CB)
                need(sp, mm["ctxT"], h - 1)
                need(sp, ctx_loaded, 16 * h)
                sp.dma_start(ctx_in[:, r, :, :],
                             ctx_v[:, batches, :]).then_inc(ctx_loaded, 16)

            def load(h, r):
                load_x(h)
                load_ctx(h, r)
            load_x(0)
            load_mats(0, x_mats_in)
            load_ctx(0, 0)
            sp.wait_ge(rows_in, 16 * len(ROWS))
            load_mats(4, a_mats_in)
            load(1, 1)
            with sp.Fori(1, HALVES // 2) as i:
                load(i * 2, 0)
                load(i * 2 + 1, 1)
            for n in range(2 * NE):
                e = n // 2
                w = ((ew1, ew2)[n % 2][e] if e < E else (sw1, sw2)[n % 2])
                need(sp, wt_pe, n - 3)
                sp.dma_start(w_in[:, n % 4, :, :],
                             w.rearrange("(c p) d -> p c d", p=P) if n % 2 == 0 else w.rearrange("d (c h) -> d c h", h=P)
                             ).then_inc(w_loaded[n % 4], 16)
            sp.wait_ge(consts_pool, CONSTS)
            sp.dma_start(listed[E * REGION:E * REGION + BR, :].rearrange("(a p) d -> p a d", p=P),
                         padding[:, :, :]).then_inc(padded, 16)
            sp.wait_ge(tables_ready, 3)
            for e in range(E):
                first = sp.value_load(pad0[0:1, e:e + 1], min_val=0, max_val=E * REGION - BR)
                sp.dma_start(listed[bass.ds(first, BR), :].rearrange("(a p) d -> p a d", p=P),
                             padding[:, :, :]).then_inc(padded, 16)
            sp.wait_ge(padded, 16 * (E + 1))
            sp.wait_ge(listed_done, 16 * 2 * NT)

            def fetch(i):
                for b in range(LB):
                    need(sp, scattered[b % RING], i * (32 * LB // RING) + 32 * (b // RING - 1))
                    first = sp.value_load(row0[0:1, one(i * LB + b)], min_val=0, max_val=E * REGION)
                    sp.dma_start(xrow[b][:, :, :], listed[bass.ds(first, BR), :].rearrange("(a p) d -> p a d", p=P)
                                 ).then_inc(loaded[b], 16)
            fetch(0)
            with sp.Fori(1, BLOCKS // LB) as i:
                fetch(i)
            for r in range(RING):
                sp.wait_ge(scattered[r], 32 * (BLOCKS // RING))
            res = results.rearrange("(n t p) d -> p n t d", p=P, n=2)
            for g in range(FG):
                for n in range(2):
                    sp.dma_start(yt[g][:, n, :, :], res[:, n, g * GT:g * GT + GT, :]).then_inc(yt_loaded[g], 16)
            for g in range(FG):
                tiles = slice(g * GT, g * GT + GT)
                sp.wait_ge(routed_added, g + 1)
                if g >= BEFORE:
                    sp.wait_ge(y_done, BEFORE + BLOCKS + g - BEFORE + 1)
                sp.dma_start(out_v[:, tiles, :], x_all[:, tiles, :]).then_inc(stored, 16)
            sp.wait_ge(stored, 16 * FG)

        @block.gpsimd
        def _(pool):
            pool.dma_start(gate_in[:, :], gate_w).then_inc(gate_loaded, 16)
            pool.memset(ident[:, :], 0.0).then_inc(consts_pool, 1)
            pool.memset(head_sel[:, :, :], 1.0).then_inc(consts_pool, 1)
            pool.memset(causal[:, :], 0.0).then_inc(consts_pool, 1)
            pool.wait_ge(consts_pool, 3)
            pool.affine_select(out=ident[:, :], in_=ident[:, :], compare_op=ALU.not_equal, fill=1.0, base=0,
                               pattern=[[-1, P]], channel_multiplier=1).then_inc(consts_pool, 1)
            pool.affine_select(out=head_sel[:, :, :], in_=head_sel[:, :, :], compare_op=ALU.is_ge, fill=0.0, base=0,
                               pattern=[[-JH * HD, GROUPS], [-HD, JH]], channel_multiplier=1).then_inc(consts_pool, 1)
            pool.affine_select(out=causal[:, :], in_=causal[:, :], compare_op=ALU.is_ge, fill=MASKED, base=0,
                               pattern=[[-1, P]], channel_multiplier=1).then_inc(consts_pool, 1)
            pool.wait_ge(consts_pool, 6)
            pool.affine_select(out=head_sel[:, :, :], in_=head_sel[:, :, :], compare_op=ALU.is_ge, fill=0.0,
                               base=HD - 1, pattern=[[JH * HD, GROUPS], [HD, JH]],
                               channel_multiplier=-1).then_inc(consts_pool, 1)
            pool.wait_ge(consts_pool, 7)
            pool.memset(causal[S:P, 0:S], MASKED).then_inc(consts_pool, 1)
            pool.wait_ge(consts_pool, 8)
            pool.memset(minus_half[:, :], -0.5).then_inc(consts_pool, 1)
            pool.memset(eps2[:, :], EPS).then_inc(consts_pool, 1)

            def root(n, h):
                i = LN.index(n)
                pool.wait_ge(stat[n], h * 4 + 4)
                need(pool, normed[n], h * 2)
                pool.tensor_tensor(vpe[:, i, :], mv[:, i, :, 1], eps2[:, :], ALU.add).then_inc(vpe_done[n], 1)
                pool.wait_ge(vpe_done[n], h + 1)
                pool.tensor_tensor(rstd[:, i, :], vpe[:, i, :], minus_half[:, :], ALU.pow).then_inc(rstd_done[n], 1)

            def send(part, m):
                t0, t1 = PARTS[part]
                n, t = m // (t1 - t0), t0 + m % (t1 - t0)
                if m == 0:
                    pool.wait_ge(rows_full, t1 // 2)
                if t == t0:
                    pool.wait_ge(placed, 2 * part + 1 + n)
                pool.indirect_dma_start(out=listed[:, :], out_offset=bass.IndirectOffsetOnAxis(ap=row_no[:, n, t:t + 1], axis=0),
                                        in_=rows_of[:, t, n, :], in_offset=None).then_inc(listed_done, 16)
            sent = [0]

            def step(h, r):
                for s in range(UNITS):
                    for m in range(SENT[h][s] if isinstance(h, int) and h in SENT else 0):
                        send(0, sent[0])
                        sent[0] += 1
                    back, hb = (s - 1) % UNITS, h if s else h - 1
                    if back in ON_POOL and valid(hb):
                        low_part(pool, hb, back)
                    if s == 2 and valid(h + 2):
                        root("x", h + 2)
                    if s == 3 and valid(h + 1):
                        pool.wait_ge(q_ready, h + 2)
                        pool.wait_ge(ev["q"], h + 2)
                        need(pool, qm_lo_ready, h + 1)
                        pool.tensor_tensor(q_lo[:, :], q32[:, :], q_hi[:, :], ALU.subtract).then_inc(qlo_full, 1)
                        pool.wait_ge(qlo_full, h + 2)
                        need(pool, t_done, UNITS * h)
                        pool.tensor_tensor(qm_lo[1 - r][:, :, :, :],
                                           q_lo[:, :].rearrange("p (b q) -> p b q", q=S).unsqueeze(2).broadcast_to([P, CB, JH, S]),
                                           head_mask[:, :].unsqueeze(1).unsqueeze(3).broadcast_to([P, CB, JH, S]),
                                           ALU.mult).then_inc(qm_lo_ready, 1)
                    if s == 4 and valid(h - 1):
                        root("y", h - 1)
                        pool.wait_ge(normed["y"], (h - 1) * 2 + 2)
                        pool.tensor_tensor(yg[:, :, :], yn[:, :, :],
                                           bcast[:, 2:3, :].broadcast_to([P, 2, D]), ALU.mult).then_inc(yg_done, 1)
                        pool.wait_ge(yg_done, h)
                        pool.wait_ge(xb_done, h)
                        need(pool, x2_done, (h - 2) * 2)
                        need(pool, normed["x1"], (h - 2) * 2)
                        pool.tensor_tensor(x1[1 - r][:, :, :], yg[:, :, :], xb[:, :, :], ALU.add).then_inc(x1_done, 1)
                    if s == 5 and valid(h - 1):
                        root("x1", h - 1)
                        pool.wait_ge(x1_done, h)
                        pool.tensor_tensor(x1b[1 - r][:, :, :], x1[1 - r][:, :, :],
                                           bcast[:, 1:2, :].broadcast_to([P, 2, D]), ALU.add).then_inc(x1b_done, 1)
                    if s == 0 and valid(h - 3):
                        root("x2", h - 3)
                    if s == 7 and valid(h):
                        pool.wait_ge(x_in, (h + 1) * 16)
                        need(pool, x1_done, h)
                        pool.tensor_tensor(xb[:, :, :], x_all[:, two_tiles(h), :],
                                           bcast[:, 3:4, :].broadcast_to([P, 2, D]), ALU.add).then_inc(xb_done, 1)

            def setup():
                for r in range(2):
                    pool.memset(V_hi[r][:, :, 2 * HD:VW], 1.0).then_inc(consts_pool, 1)
                    pool.memset(V_lo[r][:, :, 2 * HD:VW], 0.0).then_inc(consts_pool, 1)
                for e in range(E):
                    pool.memset(iota8[:, e:e + 1], float(e)).then_inc(consts_pool, 1)
                    pool.memset(region[:, e:e + 1], float(e * REGION)).then_inc(consts_pool, 1)
                    pool.memset(upto[:, e, 0:e + 1], 1.0).then_inc(consts_pool, 1)
                    if e < E - 1:
                        pool.memset(upto[:, e, e + 1:E], 0.0).then_inc(consts_pool, 1)
                pool.memset(ones16[:, :], 1.0).then_inc(consts_pool, 1)
                pool.memset(padding[:, :, :], 0.0).then_inc(consts_pool, 1)
                pool.memset(before[:, :], 1.0).then_inc(consts_pool, 1)
                pool.iota(block_no_i[:, :], pattern=[[1, BLOCKS + 1]], base=0, channel_multiplier=0).then_inc(consts_pool, 1)
                pool.iota(fills_i[:, :], pattern=[[BR, T // BR]], base=0, channel_multiplier=0).then_inc(consts_pool, 1)
                for n in range(2):
                    pool.iota(rows_of[:, :, n, D:D + 1].bitcast(I32), pattern=[[P, NT], [0, 1]], base=n * T,
                              channel_multiplier=1).then_inc(consts_pool, 1)
                pool.wait_ge(consts_pool, CONSTS - 4)
                pool.affine_select(out=before[:, :], in_=before[:, :], compare_op=ALU.is_gt, fill=0.0, base=0,
                                   pattern=[[1, P]], channel_multiplier=-1).then_inc(consts_pool, 1)
                pool.memset(padding[:, :, D:D + 1].bitcast(I32), NOWHERE).then_inc(consts_pool, 1)
                pool.tensor_copy(block_no[:, :], block_no_i[:, :]).then_inc(consts_pool, 1)
                pool.tensor_copy(fills[:, :], fills_i[:, :]).then_inc(consts_pool, 1)
                pool.wait_ge(setup_dve, 3)
            pool.wait_ge(setup_dve, 1)
            pool.wait_ge(consts_pool, 10)
            most_steps(pool, step, setup)
            step(HALVES + 2, 0)
            for m in range(sent[0], 2 * (PARTS[0][1] - PARTS[0][0])):
                send(0, m)
            for m in range(2 * (PARTS[1][1] - PARTS[1][0])):
                send(1, m)
            def scatter(i):
                for b in range(LB):
                    pool.wait_ge(y_done, i * LB + BEFORE + b + 1)
                    need(pool, block_seen, i * LB + b)
                    pool.tensor_tensor(wait_mark[:, :], eps2[:, 0:1], eps2[:, 0:1], ALU.add).then_inc(block_seen, 1)
                    for t in range(BT):
                        pool.indirect_dma_start(out=results[:, :],
                                                out_offset=bass.IndirectOffsetOnAxis(ap=xrow[b][:, t, D:D + 1].bitcast(U32), axis=0),
                                                in_=y_sb[b % RING][:, t, :], in_offset=None,
                                                bounds_check=2 * T - 1, oob_is_err=False).then_inc(scattered[b % RING], 16)
            scatter(0)
            with pool.Fori(1, BLOCKS // LB) as i:
                scatter(i)
            for g in range(0, FG, 2):
                pool.wait_ge(yt_loaded[g], 32)
                pool.tensor_tensor(yt[g][:, 0, :, :], yt[g][:, 0, :, :], yt[g][:, 1, :, :],
                                   ALU.add).then_inc(yt_summed, 1)

        @block.scalar
        def _(act):
            for n, v in enumerate(rows):
                act.dma_start(row_in[n:n + 1, :], v.rearrange("(a n) -> a n", a=1)).then_inc(rows_in, 16)
            act.wait_ge(consts_pool, 10)
            act.activation(exp_mark[:, :], eps2[:, 0:1], ACT.Exp)
            act.wait_ge(setup_pe, 1)
            act.activation(WT[:, 0:4, :], T_ps[0][:, :], ACT.Copy).then_inc(setup_ev, 1)
            act.wait_ge(setup_pe, 2)
            act.activation(vec[:, :], T_ps[1][:, 0:len(ROWS) + E], ACT.Copy).then_inc(setup_ev, 1)
            act.wait_ge(setup_ev, 2)

            def setup():
                act.wait_ge(setup_pe, 3)
                act.activation(WT[:, 4:8, :], T_ps[0][:, :], ACT.Copy).then_inc(setup_ev, 1)
                act.wait_ge(setup_pe, 4)
                act.activation(bcast[:, :, :], T_ps[1][:, :], ACT.Copy).then_inc(setup_ev, 1)

            def col(name):
                n = ROWS.index(name)
                return vec[:, n:n + 1]

            def weights_hi(n):
                act.wait_ge(wt_pe, n + 1)
                dst = (W1_hi, W2_hi)[n % 2]
                act.activation(dst[:, n // 2 * HID:n // 2 * HID + HID], W_ps[n % 4][:, :], ACT.Copy, scale=WSCALE).then_inc(wt_hi, 1)

            def second_weight(part):
                tiles = slice(*PARTS[part])
                act.wait_ge(gate_step, GATE_STEPS * part + 1)
                act.activation(second_exp[:, tiles], gates[:, tiles, 0], ACT.Exp).then_inc(gate_exp, 1)

            def evacuate(name, h, dst, src, func=ACT.Copy, **kw):
                act.wait_ge(mm[name], h + 1)
                act.activation(dst, src, func, **kw).then_inc(ev[name], 1)

            def step(h, r):
                a, b, c, d = h + 1, h - 1, h - 2, h - 3
                for s in range(UNITS):
                    u = UNITS * h + s
                    if valid(h):
                        act.wait_ge(t_done, u + 1)
                        hl, sl = (h, s - 2) if s > 1 else (h - 1, s + UNITS - 2)
                        if valid(hl):
                            act.wait_ge(*low_of(hl, sl))
                        act.activation(p32[:, s % 2, :], T_ps[s % 2][:, :], ACT.Exp,
                                       scale=XSCALE).then_inc(exp_done, 1)
                    if valid(h):
                        act.wait_ge(exp_done, u + 1)
                        need(act, v_done, u - 3)
                        act.activation(p_hi[:, s % 4, :], p32[:, s % 2, :], ACT.Copy).then_inc(p_hi_done, 1)
                    if s == 0 and valid(a):
                        need(act, mm["q"], a)
                        evacuate("xnT", a, xnT_sb[:, :], XB["xnT"][:, 0:2 * P])
                    if s == 0 and valid(c):
                        act.wait_ge(mm["qk"], c + 1)
                        need(act, mm["s"], c)
                        act.activation(QT[:, :], XB["qk"][:, 0:2 * P], ACT.Identity, bias=col("abq"))
                        act.activation(KT[:, :], XB["qk"][:, 2 * P:4 * P], ACT.Identity, bias=col("abk")).then_inc(ev["qk"], 1)
                    if s == 1 and valid(c):
                        need(act, mm["av"], c)
                        evacuate("v2", c, V2[:, :, :], XB["v2"][:, 0:2 * P])
                    if s == 2 and valid(a):
                        act.wait_ge(mm["q"], a + 1)
                        need(act, qm_lo_ready, a)
                        need(act, qm_hi_ready, JH * a)
                        act.activation(q32[:, :], XB["q"][:, 0:2 * P], ACT.Identity, bias=col("xbq")).then_inc(q_ready, 1)
                        act.activation(q_hi[:, :], XB["q"][:, 0:2 * P], ACT.Identity,
                                       bias=col("xbq")).then_inc(ev["q"], 1)
                    if s == 2 and valid(b):
                        need(act, mm["y"], b)
                        evacuate("oT", b, OT[:, :], XB["oT"][:, 0:2 * P])
                    if s == 3 and valid(a):
                        need(act, mm["v"], a)
                        evacuate("ctxT", a, cT[:, :], XB["ctxT"][:, :])
                    if s == 3 and valid(c):
                        act.wait_ge(nbias_done, c + 1)
                        need(act, mm["pT"], c)
                        for t in range(2):
                            act.activation(P2[:, t, :], sm[:, t, :], ACT.Exp, bias=nbias[:, t:t + 1], scale=ASCALE,
                                           accum_out=rs[:, t:t + 1]).then_inc(p2_done, 1)
                    if s == 3 and valid(d):
                        act.wait_ge(normed["x2"], 2 * d + 2)
                        for t in range(2):
                            last = act.activation(rows_of[:, one_tile(d, t), :, 0:D].rearrange("p t n d -> p (t n) d"),
                                                  x2n[:, t:t + 1, :].broadcast_to([P, 2, D]), ACT.Copy)
                        last.then_inc(rows_full, 1)
                    if s == 4 and valid(a):
                        act.wait_ge(mm["k"], a + 1)
                        need(act, t_done, UNITS * (a - 1))
                        act.activation(k_hi[1 - r][:, :], XB["k"][:, :], ACT.Identity, bias=col("xbk")).then_inc(k_hi_ready, 1)
                    if s == 4 and valid(c):
                        need(act, mm["av"], c)
                        evacuate("pT", c, P2T[:, :], XB["pT"][:, 0:2 * P])
                    if s == 5 and valid(a):
                        act.wait_ge(mm["v"], a + 1)
                        need(act, v_done, UNITS * (a - 1))
                        act.activation(V_hi[1 - r][:, :, 0:2 * HD], XB["v"][:, :].rearrange("p (n w) -> p n w", w=2 * HD),
                                       ACT.Copy).then_inc(v_hi_ready, 1)
                    if s == 5 and valid(c):
                        need(act, mm["z"], c)
                        evacuate("av", c, AT[:, :], XB["av"][:, 0:2 * P])
                    if s == 6 and valid(d):
                        act.wait_ge(mm["x2T"], d + 1)
                        act.activation(x2T_hi[:, half_cols(d)], XB["x2T"][:, 0:2 * P], ACT.Copy).then_inc(x2T_hi_done, 1)
                    if s == 7 and valid(b):
                        need(act, mm["v2"], b)
                        evacuate("x1T", b, x1T_sb[:, :], XB["x1T"][:, 0:2 * P])
                    if beside(h, s) == 2:
                        second_weight(0)
                    for n in weights_at(h, s):
                        weights_hi(n)

            def unit(n, k):
                act.wait_ge(u_done, n + 1)
                need(act, hlo_done, n - RING + 1)
                act.activation(h32[k % RING][:, :], U_ps[k % RING][:, :], ACT.Silu, scale=1.0 / WSCALE).then_inc(silu_done, 1)
                act.wait_ge(silu_done, n + 1)
                need(act, d_done, n - RING + 1)
                act.activation(h_hi[k % RING][:, :], h32[k % RING][:, :], ACT.Copy).then_inc(hhi_done, 1)

            def block_in(j, b):
                act.wait_ge(xT_pe, j + 1)
                if not isinstance(j, int) or j > 1:
                    act.wait_ge(u_done, j * BU + (N0 - 2 * BU + BU))
                act.activation(xT_hi[b % 2][:, :], X_ps[b % 2][:, 0:BR], ACT.Copy).then_inc(xT_hi_done, 1)

            def routed(i, end):
                for b in range(LB):
                    for q in range(BU):
                        if q == 0 and not (end and b == LB - 1):
                            block_in(i * LB + b + 1, b + 1)
                        unit(i * (LB * BU) + N0 + b * BU + q, b * BU + q)
            most_steps(act, step, setup)
            for n in range(EARLY * CH):
                unit(n, n)
            step(HALVES + 2, 0)
            second_weight(1)

            for n in range(EARLY * CH, N0):
                if n == N0 - BU:
                    block_in(0, 0)
                unit(n, n)
            routed(0, False)
            with act.Fori(1, BLOCKS // LB - 1) as i:
                routed(i, False)
            routed(BLOCKS // LB - 1, True)
            for n in range(N1, NU):
                unit(n, n)

        @block.vector
        def _(dve):
            dve.wait_ge(consts_pool, 7)
            dve.tensor_reduce(head_mask[:, :], head_sel[:, :, :].rearrange("p a j -> p j a"), AX.X,
                              ALU.add).then_inc(setup_dve, 1)
            dve.tensor_scalar(neg_ident[:, :], ident[:, :], -1.0, None, ALU.mult).then_inc(setup_dve, 1)

            def setup():
                dve.wait_ge(consts_pool, CONSTS)
                dve.wait_ge(setup_ev, 2)
                dve.tensor_scalar(gate_hi[:, :], gateT, WSCALE, None, ALU.mult).then_inc(gate_split, 1)
                dve.wait_ge(gate_split, 1)
                dve.scalar_tensor_tensor(gate_lo[:, :], gateT, WSCALE, gate_hi[:, :], ALU.mult, ALU.subtract).then_inc(gate_split, 1)
                dve.wait_ge(setup_ev, 4)
                dve.wait_ge(setup_pe, 5)
                dve.tensor_tensor(bcast[:, 0:2, :], bcast[:, 0:2, :],
                                  PV_ps[0][:, 0:2 * D].rearrange("p (n d) -> p n d", d=D), ALU.add).then_inc(setup_dve, 1)

            def statistics(n, h, src):
                i = LN.index(n)
                need(dve, normed[n], h * 2)
                dve.memset(scratch[:, 2 * i:2 * i + 1], 0.0)
                for t in range(2):
                    dve.bn_stats(st[:, i, t, :], src[:, t, :]).then_inc(stat[n], 1)
                dve.wait_ge(stat[n], h * 4 + 2)
                dve.memset(scratch[:, 2 * i + 1:2 * i + 2], 0.0)
                for t in range(2):
                    dve.bn_aggr(mv[:, i, t, :], st[:, i, t, :]).then_inc(stat[n], 1)

            def normalise(n, h, src, dst):
                i = LN.index(n)
                dve.wait_ge(rstd_done[n], h + 1)
                dve.wait_ge(stat[n], h * 4 + 4)
                for t in range(2):
                    dve.tensor_scalar(dst[:, t, :], src[:, t, :], mv[:, i, t, 0:1], rstd[:, i, t:t + 1],
                                      ALU.subtract, ALU.mult).then_inc(normed[n], 1)

            def weights_lo(n):
                dve.wait_ge(wt_hi, n + 1)
                part = slice(n // 2 * HID, n // 2 * HID + HID)
                dve.scalar_tensor_tensor((W1_lo, W2_lo)[n % 2][:, part], W_ps[n % 4][:, :], WSCALE, (W1_hi, W2_hi)[n % 2][:, part],
                                         ALU.mult, ALU.subtract).then_inc(wt_lo, 1)

            def route(part, stage):
                t0, t1 = PARTS[part]
                nt = t1 - t0
                tiles = slice(t0, t1)
                base = GATE_STEPS * part
                logs = 2 * (PARTS[0][1] - PARTS[0][0]) * part
                if stage == 0:
                    dve.wait_ge(mm["lg"], part + 1)
                    dve.tensor_scalar(lg[:, tiles, :], G_ps[:, t0 * E:t1 * E].rearrange("p (t e) -> p t e", e=E),
                                      1.0 / WSCALE, None, ALU.mult).then_inc(ev["lg"], 1)
                    dve.wait_ge(ev["lg"], part + 1)
                    for t in range(t0, t1):
                        dve.max(top[:, t, :], lg[:, t, :]).then_inc(top_done, 1)
                if stage == 1:
                    dve.wait_ge(top_done, logs + nt)
                    dve.tensor_tensor(gates[:, tiles, 0], top[:, tiles, 1], top[:, tiles, 0], ALU.subtract).then_inc(gate_step, 1)
                    for t in range(t0, t1):
                        dve.max_index(idx[:, t, :], top[:, t, :], lg[:, t, :]).then_inc(top_done, 1)
                    dve.wait_ge(top_done, logs + 2 * nt)
                    dve.tensor_copy(idxf[:, tiles, :], idx[:, tiles, 0:2]).then_inc(gate_step, 1)
                if stage == 2:
                    dve.wait_ge(gate_exp, part + 1)
                    dve.tensor_scalar(gates[:, tiles, 1], second_exp[:, tiles], 1.0, None, ALU.add).then_inc(gate_step, 1)
                    dve.wait_ge(gate_step, base + 3)
                    dve.reciprocal(gates[:, tiles, 0], gates[:, tiles, 1]).then_inc(gate_step, 1)
                    dve.wait_ge(gate_step, base + 4)
                    dve.tensor_tensor(gates[:, tiles, 1], gates[:, tiles, 0], second_exp[:, tiles], ALU.mult).then_inc(gate_step, 1)
                if stage == 3:
                    dve.wait_ge(gate_step, base + 5)
                    for n in range(2):
                        dve.tensor_scalar(rows_of[:, tiles, n, D + 1:D + 2], gates[:, tiles, n:n + 1], 1.0 / WSCALE, None,
                                          ALU.mult).then_inc(gate_step, 1)
                        dve.tensor_tensor(chosen[n][:, tiles, :], iota8[:, :].unsqueeze(1).broadcast_to([P, nt, E]),
                                          idxf[:, tiles, n].unsqueeze(2).broadcast_to([P, nt, E]),
                                          ALU.is_equal).then_inc(gate_step, 1)
                    dve.wait_ge(gate_step, base + 9)
                    dve.tensor_tensor(either[:, tiles, :], chosen[0][:, tiles, :], chosen[1][:, tiles, :],
                                      ALU.add).then_inc(picked, 1)
                    dve.wait_ge(picked, 2 * part + 1)
                    with nc.allow_low_precision(reason="counts up to a part's tiles are exact"):
                        dve.tensor_reduce(per_tile[:, part, :], either[:, tiles, :].rearrange("p t e -> p e t"), AX.X,
                                          ALU.add).then_inc(picked, 1)
                if stage == 5:
                    dve.wait_ge(mm["rank"], part + 1)
                    dve.tensor_tensor(row_at[:, tiles, :], R_ps[:, t0 * E:t1 * E].rearrange("p (t e) -> p t e", e=E),
                                      region[:, :].unsqueeze(1).broadcast_to([P, nt, E]), ALU.add).then_inc(ev["rank"], 1)
                    if part == 1:
                        dve.tensor_copy(load[:, :], R_ps[0:1, NT * E:NT * E + E]).then_inc(table, 1)
                    dve.wait_ge(ev["rank"], part + 1)
                    for n in range(2):
                        need(dve, row_step, 4 * part + 2 * n)
                        dve.tensor_tensor(row_pick[:, tiles, :], row_at[:, tiles, :], chosen[n][:, tiles, :],
                                          ALU.mult).then_inc(row_step, 1)
                        dve.wait_ge(row_step, 4 * part + 2 * n + 1)
                        dve.tensor_reduce(row_f[:, tiles, n], row_pick[:, tiles, :], AX.X, ALU.add).then_inc(row_step, 1)
                        dve.wait_ge(row_step, 4 * part + 2 * n + 2)
                        dve.tensor_copy(row_no[:, n, tiles], row_f[:, tiles, n]).then_inc(placed, 1)

            def normalise_pair(h, p):
                dve.wait_ge(v_done, UNITS * h + GROUPS * (p + 1))
                need(dve, norm_done, h * 2 + p)
                pv = PV_ps[p][:, 0:16 * VW].rearrange("p (n w) -> p n w", w=VW)
                dve.reciprocal(rden[:, p, :], pv[:, :, 2 * HD]).then_inc(norm_step, 1)
                dve.wait_ge(norm_step, h * 2 + p + 1)
                need(dve, mm["oT"], h)
                for b in range(2):
                    for o in range(2):
                        rows_ = slice(S * o, S * o + S)
                        last = dve.tensor_tensor(
                            O_tok[S * b:S * b + S, p, :, o, :], pv[rows_, 8 * b:8 * b + 8, HD * o:HD * o + HD],
                            rden[rows_, p, 8 * b:8 * b + 8].unsqueeze(2).broadcast_to([S, 8, HD]), ALU.mult)
                last.then_inc(norm_done, 1)

            def step(h, r):
                a, b, c, d = h + 1, h - 1, h - 2, h - 3
                for s in range(UNITS):
                    hm, u = (h, UNITS * h + s + 2)
                    if s >= UNITS - 2:
                        hm = h + 1
                    if valid(hm):
                        dve.wait_ge(m_done, u + 1)
                        need(dve, t_done, u + 1 - 2 * UNITS)
                        slot = (r * UNITS + s + 2) % (2 * UNITS)
                        dve.tensor_reduce(m_bf[:, slot, :], M_ps[s % 2][:, :].rearrange("p (n k) -> p n k", k=SK),
                                          AX.X, ALU.max).then_inc(max_done, 1)
                    back, hb = (s - 1) % UNITS, h if s else h - 1
                    if back not in ON_POOL and valid(hb):
                        low_part(dve, hb, back)
                    if s == 1 and valid(c):
                        dve.wait_ge(mm["s"], c + 1)
                        need(dve, p2_done, 2 * c)
                        dve.tensor_tensor(sm[:, :, :], XB["s"][:, 0:2 * P].rearrange("p (t k) -> p t k", k=P),
                                          causal[:, :].unsqueeze(1).broadcast_to([P, 2, P]), ALU.add).then_inc(ev["s"], 1)
                    if s == 1 and valid(b):
                        normalise_pair(b, 1)
                    if s == 1 and valid(c):
                        dve.wait_ge(ev["s"], c + 1)
                        dve.tensor_reduce(smax[:, :], sm[:, :, :], AX.X, ALU.max).then_inc(sm_max, 1)
                        dve.wait_ge(sm_max, c + 1)
                        dve.tensor_scalar(nbias[:, :], smax[:, :], -ASCALE, None, ALU.mult).then_inc(nbias_done, 1)
                    if s == 5 and valid(h):
                        normalise_pair(h, 0)
                    if s == 0 and valid(h + 2):
                        dve.wait_ge(x_in, (h + 3) * 16)
                        statistics("x", h + 2, x_all[:, two_tiles(h + 2), :])
                    if s == 2 and valid(d):
                        need(dve, rows_full, d)
                        need(dve, mm["x2T"], d)
                        normalise("x2", d, x_all[:, two_tiles(d), :], x2n)
                    if s == 3 and valid(a):
                        dve.wait_ge(ev["q"], a + 1)
                        need(dve, t_done, UNITS * (a - 1))
                        for j in range(JH):
                            dve.tensor_scalar(qm_hi[1 - r][:, :, j, :],
                                              q_hi[:, :].rearrange("p (b q) -> p b q", q=S),
                                              head_mask[:, j:j + 1], None, ALU.mult).then_inc(qm_hi_ready, 1)
                    if s == 3 and valid(b):
                        dve.wait_ge(mm["y"], b + 1)
                        need(dve, normed["y"], 2 * b)
                        dve.tensor_tensor(yb[:, :, :], XB["y"][:, 0:2 * P].rearrange("p (t k) -> p t k", k=P),
                                          bcast[:, 0:1, :].broadcast_to([P, 2, D]), ALU.add).then_inc(ev["y"], 1)
                        dve.wait_ge(ev["y"], b + 1)
                        statistics("y", b, yb)
                    if s == 4 and valid(b):
                        need(dve, yg_done, b)
                        normalise("y", b, yb, yn)
                    if s == 4 and valid(a):
                        dve.wait_ge(k_hi_ready, a + 1)
                        dve.scalar_tensor_tensor(k_lo[1 - r][:, :], XB["k"][:, :], vec[:, 1:2],
                                                 k_hi[1 - r][:, :], ALU.add, ALU.subtract).then_inc(ev["k"], 1)
                    if s == 4 and valid(c):
                        dve.wait_ge(p2_done, 2 * c + 2)
                        need(dve, x2_done, 2 * c)
                        dve.reciprocal(rrs[:, :], rs[:, :]).then_inc(rrs_done, 1)
                    if s == 5 and valid(a):
                        dve.wait_ge(v_hi_ready, a + 1)
                        dve.tensor_tensor(V_lo[1 - r][:, :, 0:2 * HD], XB["v"][:, :].rearrange("p (n w) -> p n w", w=2 * HD),
                                          V_hi[1 - r][:, :, 0:2 * HD], ALU.subtract).then_inc(ev["v"], 1)
                    if s == 5 and valid(b):
                        dve.wait_ge(x1_done, b + 1)
                        statistics("x1", b, x1[1 - r])
                    if s == 6 and valid(b):
                        need(dve, mm["x1T"], b)
                        normalise("x1", b, x1[1 - r], x1n)
                    if s == 6 and valid(d):
                        dve.wait_ge(x2T_hi_done, d + 1)
                        dve.tensor_tensor(x2T_lo[:, half_cols(d)], XB["x2T"][:, 0:2 * P],
                                          x2T_hi[:, half_cols(d)], ALU.subtract).then_inc(ev["x2T"], 1)
                    if s == 6 and valid(c):
                        dve.wait_ge(mm["z"], c + 1)
                        dve.wait_ge(rrs_done, c + 1)
                        dve.wait_ge(x1b_done, c + 1)
                        for t in range(2):
                            last = dve.scalar_tensor_tensor(x_all[:, one_tile(c, t), :].rearrange("p t d -> p (t d)"),
                                                            XB["z"][:, t * P:t * P + P],
                                                            rrs[:, t:t + 1], x1b[r][:, t, :], ALU.mult, ALU.add)
                            last.then_inc(x2_done, 1)
                    if s == 7 and valid(h + 2):
                        dve.wait_ge(mm["xnT"], h + 2)
                        normalise("x", h + 2, x_all[:, two_tiles(h + 2), :], xn)
                    if s == 7 and valid(c):
                        dve.wait_ge(x2_done, 2 * c + 2)
                        statistics("x2", c, x_all[:, two_tiles(c), :])
                    if beside(h, s) is not None and s < 6:
                        route(0, s)
                    for n in weights_at(h, s):
                        weights_lo(n)

            def unit(n, k):
                dve.wait_ge(hhi_done, n + 1)
                need(dve, d_done, n - RING + 1)
                dve.tensor_tensor(h_lo[k % RING][:, :], h32[k % RING][:, :], h_hi[k % RING][:, :],
                                  ALU.subtract).then_inc(hlo_done, 1)

            def block_in(j, b):
                dve.wait_ge(xT_hi_done, j + 1)
                dve.tensor_tensor(xT_lo[b % 2][:, :], X_ps[b % 2][:, 0:BR], xT_hi[b % 2][:, :],
                                  ALU.subtract).then_inc(xT_lo_done, 1)

            def block_out(i, b):
                dve.wait_ge(d_done, i * (LB * BU) + N0 + b * BU + BU)
                need(dve, scattered[b % RING], i * (32 * LB // RING) + 32 * (b // RING))
                for t in range(BT):
                    last = dve.tensor_scalar(y_sb[b % RING][:, t, :], Y_ps[b % 2][:, t * D:t * D + D],
                                             xrow[b][:, t, D + 1:D + 2], None, ALU.mult)
                last.then_inc(y_done, 1)

            def shared_out(g):
                dve.wait_ge(d_done, (g + 1) * CH if g < BEFORE else N1 + (g - BEFORE + 1) * CH)
                tiles = x_all[:, g * GT:g * GT + GT, :]
                dve.scalar_tensor_tensor(tiles, Y_ps[g % 2][:, :].rearrange("p (t d) -> p t d", d=D), 1.0 / WSCALE, tiles,
                                         ALU.mult, ALU.add).then_inc(y_done, 1)

            def routed_in(g):
                buf = yt[g]
                if g % 2 == 0:
                    dve.wait_ge(yt_summed, g // 2 + 1)
                else:
                    dve.wait_ge(yt_loaded[g], 32)
                    dve.tensor_tensor(buf[:, 0, :, :], buf[:, 0, :, :], buf[:, 1, :, :], ALU.add).then_inc(odd_summed, 1)
                    dve.wait_ge(odd_summed, g // 2 + 1)
                dve.wait_ge(y_done, g + 1 + (BLOCKS if g >= BEFORE else 0))
                tiles = x_all[:, g * GT:g * GT + GT, :]
                dve.tensor_tensor(tiles, tiles, buf[:, 0, :, :], ALU.add).then_inc(routed_added, 1)

            def routed(i, first, end):
                for b in range(LB):
                    for q in range(BU):
                        if q == 0 and not (end and b == LB - 1):
                            block_in(i * LB + b + 1, b + 1)
                        unit(i * (LB * BU) + N0 + b * BU + q, b * BU + q)
                        if q == BU - 1:
                            if first and b == 0:
                                shared_out(BEFORE - 1)
                            else:
                                block_out(i if b else i - 1, (b - 1) % LB)

            def shared_before(first, end):
                for n in range(first, end):
                    if n == N0 - BU:
                        block_in(0, 0)
                    unit(n, n)
                    if n % CH == 1 and n > 1:
                        shared_out(n // CH - 1)

            most_steps(dve, step, setup)
            shared_before(0, EARLY * CH)
            step(HALVES + 2, 0)

            for stage in range(6):
                route(1, stage)
            dve.wait_ge(table, 1)
            dve.tensor_tensor(fill[:, :, :], load[:, :].unsqueeze(2).broadcast_to([1, E, T // BR]),
                              fills[:, :].unsqueeze(1).broadcast_to([1, E, T // BR]), ALU.is_gt).then_inc(table, 1)
            dve.tensor_tensor(pad0[:, :], load[:, :], region[0:1, :], ALU.add).then_inc(tables_ready, 1)
            dve.wait_ge(table, 2)
            dve.tensor_reduce(nblocks[:, :], fill[:, :, :], AX.X, ALU.add).then_inc(table, 1)
            dve.wait_ge(table, 3)
            dve.tensor_tensor(blocks_upto[:, :, :], nblocks[:, :].unsqueeze(1).broadcast_to([1, E, E]), upto[:, :, :],
                              ALU.mult).then_inc(table, 1)
            dve.wait_ge(table, 4)
            dve.tensor_reduce(last_block[:, :], blocks_upto[:, :, :], AX.X, ALU.add).then_inc(table, 1)
            dve.wait_ge(table, 5)
            dve.tensor_tensor(passed[:, :, :], block_no[:, :].unsqueeze(2).broadcast_to([1, BLOCKS + 1, E]),
                              last_block[:, :].unsqueeze(1).broadcast_to([1, BLOCKS + 1, E]), ALU.is_ge).then_inc(table, 1)
            dve.wait_ge(table, 6)
            dve.tensor_reduce(block_expert[:, :], passed[:, :, :], AX.X, ALU.add).then_inc(table, 1)
            dve.tensor_tensor(blocks_passed[:, :, :], passed[:, :, :], nblocks[:, :].unsqueeze(1).broadcast_to([1, BLOCKS + 1, E]),
                              ALU.mult).then_inc(table, 1)
            dve.wait_ge(table, 8)
            dve.tensor_reduce(expert_first[:, :], blocks_passed[:, :, :], AX.X, ALU.add).then_inc(table, 1)
            dve.tensor_scalar(w_col[:, :], block_expert[:, :], float(HID), None, ALU.mult).then_inc(tables_ready, 1)
            dve.wait_ge(table, 9)
            dve.tensor_tensor(block_row[:, :], block_no[:, :], expert_first[:, :], ALU.subtract).then_inc(table, 1)
            dve.wait_ge(table, 10)
            dve.tensor_scalar(expert_first[:, :], block_expert[:, :], float(REGION), None, ALU.mult).then_inc(table, 1)
            dve.wait_ge(table, 11)
            dve.scalar_tensor_tensor(block_row[:, :], block_row[:, :], float(BR), expert_first[:, :], ALU.mult,
                                     ALU.add).then_inc(table, 1)
            dve.wait_ge(table, 12)
            dve.tensor_scalar(row0[:, :], block_row[:, :], float(E * REGION), None, ALU.min).then_inc(tables_ready, 1)
            shared_before(EARLY * CH, N0)
            routed(0, True, False)
            with dve.Fori(1, BLOCKS // LB - 1) as i:
                routed(i, False, False)
            routed(BLOCKS // LB - 1, False, True)
            adds = {N1 + CH + 1: (0,), N1 + CH + 2: (1, 2), N1 + CH + 3: (3, 4, 5, 6)}
            for n in range(N1, NU):
                unit(n, n)
                if n == N1 + 1:
                    block_out(BLOCKS // LB - 1, LB - 1)
                elif (n - N1) % CH == 1:
                    shared_out(BEFORE + (n - N1) // CH - 1)
                for g in adds.get(n, ()):
                    routed_in(g)
            shared_out(FG - 1)
            routed_in(FG - 1)

        @block.tensor
        def _(pe):
            pe.wait_ge(consts_pool, 4)
            pe.wait_ge(x_mats_in, 16 * 4)
            for m in range(4):
                last = pe.transpose(T_ps[0][:, m * P:m * P + P], mat_in[:, m, :], ident[:, :])
            last.then_inc(setup_pe, 1)
            pe.wait_ge(rows_in, 16 * len(ROWS))
            pe.wait_ge(gate_loaded, 16)
            nv = len(ROWS)
            pe.transpose(T_ps[1][:, 0:nv], row_in[:, :], ident[0:nv, 0:nv])
            pe.transpose(T_ps[1][:, nv:nv + E], gate_in[:, :], ident[0:E, 0:E]).then_inc(setup_pe, 1)

            def setup():
                pe.wait_ge(consts_pool, CONSTS)
                pe.wait_ge(a_mats_in, 16 * 4)
                pe.wait_ge(setup_ev, 1)
                for m in range(4):
                    last = pe.transpose(T_ps[0][:, m * P:m * P + P], mat_in[:, 4 + m, :], ident[:, :])
                last.then_inc(setup_pe, 1)
                pe.wait_ge(setup_ev, 2)
                for n, name in enumerate(("xbo", "abo", "gamma", "beta")):
                    r = ROWS.index(name)
                    last = pe.matmul(T_ps[1][:, n * D:n * D + D], ident[0:nv, r:r + 1].broadcast_to([nv, P]), row_in[:, :],
                                     start=True, stop=True)
                last.then_inc(setup_pe, 1)
                pe.wait_ge(setup_ev, 3)
                for n, (bv, wo) in enumerate((("xbv", "xWo"), ("abv", "aWo"))):
                    c = ROWS.index(bv)
                    last = pe.matmul(PV_ps[0][:, n * D:n * D + D], vec[:, c:c + 1].broadcast_to([P, P]),
                                     WT[:, MATS.index(wo), :], start=True, stop=True)
                last.then_inc(setup_pe, 1)
                pe.wait_ge(setup_ev, 4)
                pe.wait_ge(setup_dve, 3)

            def W(name):
                return WT[:, MATS.index(name), :]

            def shared_bank(name, h, ring):
                x = XB[name]
                if name == "xnT":
                    pe.wait_ge(normed["x"], 2 * h + 2)
                    for t in range(2):
                        last = pe.transpose(x[:, t * P:t * P + P], xn[:, t, :], ident[:, :])
                if name == "ctxT":
                    pe.wait_ge(ctx_loaded, 16 * h + 16)
                    for b in range(CB):
                        last = pe.transpose(x[:, b * P:b * P + P], ctx_in[:, ring, b, :], ident[:, :])
                if name == "q":
                    pe.wait_ge(ev["xnT"], h + 1)
                    last = pe.matmul(x[:, 0:2 * P], W("xWq"), xnT_sb[:, :], start=True, stop=True)
                if name == "k":
                    pe.wait_ge(ev["ctxT"], h + 1)
                    last = pe.matmul(x[:, :], W("xWk"), cT[:, :], start=True, stop=True)
                if name == "v":
                    for b in range(CB):
                        last = pe.matmul(x[:, b * D:b * D + D], cT[:, b * SK:b * SK + SK], W("xWv"), start=True, stop=True)
                if name == "oT":
                    pe.wait_ge(norm_done, 2 * h + 2)
                    for t in range(2):
                        last = pe.transpose(x[:, t * P:t * P + P],
                                            O_tok[:, t, :, :, :].rearrange("p t o d -> p (t o d)"), ident[:, :])
                if name == "y":
                    pe.wait_ge(ev["oT"], h + 1)
                    for t in range(2):
                        last = pe.matmul(x[:, t * D:t * D + D], OT[:, t * P:t * P + P], W("xWo"), start=True, stop=True)
                if name == "x1T":
                    pe.wait_ge(normed["x1"], 2 * h + 2)
                    for t in range(2):
                        last = pe.transpose(x[:, t * P:t * P + P], x1n[:, t, :], ident[:, :])
                if name == "qk":
                    pe.wait_ge(ev["x1T"], h + 1)
                    pe.matmul(x[:, 0:2 * P], W("aWq"), x1T_sb[:, :], start=True, stop=True)
                    last = pe.matmul(x[:, 2 * P:4 * P], W("aWk"), x1T_sb[:, :], start=True, stop=True)
                if name == "v2":
                    for t in range(2):
                        last = pe.matmul(x[:, t * D:t * D + D], x1T_sb[:, t * P:t * P + P], W("aWv"), start=True, stop=True)
                if name == "s":
                    pe.wait_ge(ev["qk"], h + 1)
                    for t in range(2):
                        last = pe.matmul(x[:, t * P:t * P + P], QT[:, t * P:t * P + P], KT[:, t * P:t * P + P],
                                         start=True, stop=True)
                if name == "pT":
                    pe.wait_ge(p2_done, 2 * h + 2)
                    for t in range(2):
                        last = pe.transpose(x[:, t * P:t * P + P], P2[:, t, :], ident[:, :])
                if name == "av":
                    pe.wait_ge(ev["pT"], h + 1)
                    pe.wait_ge(ev["v2"], h + 1)
                    for t in range(2):
                        last = pe.matmul(x[:, t * P:t * P + P], V2[:, t, :], P2T[:, t * P:t * P + P], start=True, stop=True)
                if name == "z":
                    pe.wait_ge(ev["av"], h + 1)
                    for t in range(2):
                        last = pe.matmul(x[:, t * D:t * D + D], AT[:, t * P:t * P + P], W("aWo"), start=True, stop=True)
                if name == "x2T":
                    pe.wait_ge(normed["x2"], 2 * h + 2)
                    for t in range(2):
                        last = pe.transpose(x[:, t * P:t * P + P], x2n[:, t, :], ident[:, :])
                last.then_inc(mm[name], 1)

            def logits(part):
                for t in range(*PARTS[part]):
                    for n, (xx, g) in enumerate(((x2T_hi, gate_hi), (x2T_hi, gate_lo), (x2T_lo, gate_hi))):
                        last = pe.matmul(G_ps[:, t * E:t * E + E], xx[:, t * P:t * P + P], g[:, :],
                                         start=(n == 0), stop=(n == 2))
                last.then_inc(mm["lg"], 1)

            def ranks(part):
                t0, t1 = PARTS[part]
                pe.wait_ge(picked, 2 * part + 2)
                pe.matmul(R_ps[:, t0 * E:t1 * E], before[:, :], either[:, t0:t1, :].rearrange("p t e -> p (t e)"),
                          start=True, stop=False)
                for t in range(t0, t1 - 1):
                    last = pe.matmul(R_ps[:, (t + 1) * E:t1 * E], ones16[:, :],
                                     either[:, t:t + 1, :].broadcast_to([P, t1 - 1 - t, E]), start=False,
                                     stop=(part == 0 and t == t1 - 2))
                if part == 1:
                    pe.matmul(R_ps[:, t0 * E:t1 * E], ones16[:, :], per_tile[:, 0:1, :].broadcast_to([P, t1 - t0, E]),
                              start=False, stop=True)
                    for n in range(2):
                        last = pe.matmul(R_ps[:, NT * E:NT * E + E], ones16[:, :], per_tile[:, n, :],
                                         start=(n == 0), stop=(n == 1))
                last.then_inc(mm["rank"], 1)

            def weights(n):
                pe.wait_ge(w_loaded[n % 4], 16 * (n // 4 + 1))
                need(pe, wt_lo, n - 3)
                if n < 4:
                    pe.wait_ge(max_done, UNITS * HALVES)
                    pe.wait_ge(norm_done, PAIRS * HALVES)
                for c in range(CH):
                    last = pe.transpose(W_ps[n % 4][:, c * P:c * P + P], w_in[:, n % 4, c, :], ident[:, :])
                last.then_inc(wt_pe, 1)

            def step(h, r):
                for s in range(UNITS):
                    u, p, g = UNITS * h + s, s // GROUPS, s % GROUPS
                    rows_ = slice(g * 32, g * 32 + 32)
                    if valid(h):
                        pe.wait_ge(max_done, u + 1)
                        need(pe, exp_done, u - 1)
                        if s == 0:
                            pe.wait_ge(qm_lo_ready, h + 1)
                            pe.wait_ge(ev["k"], h + 1)
                        for n in range(4):
                            pe.matmul(T_ps[s % 2][:, n * P:n * P + P],
                                      m_bf[:, r * UNITS + s, n:n + 1].broadcast_to([P, P]), neg_ident[:, :],
                                      start=(n == 0), stop=False)
                        for b in range(2):
                            cb = 2 * p + b
                            for n, (kk, qq) in enumerate(((k_hi, qm_hi), (k_hi, qm_lo), (k_lo, qm_hi))):
                                last = pe.matmul(T_ps[s % 2][:, b * 256:b * 256 + 256],
                                                 kk[r][rows_, cb * SK:cb * SK + SK],
                                                 qq[r][rows_, cb, :, :].rearrange("p j q -> p (j q)"),
                                                 start=False, stop=(b == 1 and n == 2))
                        last.then_inc(t_done, 1)
                    hm, unit_m = (h, s + 2) if s < UNITS - 2 else (h + 1, s + 2 - UNITS)
                    if valid(hm):
                        rm = r if unit_m == s + 2 else 1 - r
                        pm, gm = unit_m // GROUPS, unit_m % GROUPS
                        if unit_m == 0:
                            pe.wait_ge(qm_hi_ready, JH * (hm + 1))
                            pe.wait_ge(k_hi_ready, hm + 1)
                        need(pe, max_done, u + 1)
                        mrows = slice(gm * 32, gm * 32 + 32)
                        for b in range(2):
                            cb = 2 * pm + b
                            for jp in range(2):
                                last = pe.matmul(M_ps[s % 2][:, (2 * b + jp) * P:(2 * b + jp) * P + P],
                                                 qm_hi[rm][mrows, cb, 2 * jp:2 * jp + 2, :].rearrange("p j q -> p (j q)"),
                                                 k_hi[rm][mrows, cb * SK:cb * SK + SK], start=True, stop=True)
                        last.then_inc(m_done, 1)
                    hv, sv = (h, s - LAG) if s >= LAG else (h - 1, s - LAG + UNITS)
                    if valid(hv):
                        rv = r if s >= LAG else 1 - r
                        pv, gv = sv // GROUPS, sv % GROUPS
                        pe.wait_ge(*low_of(hv, sv))
                        if sv == 0:
                            pe.wait_ge(ev["v"], hv + 1)
                        if gv == 0:
                            need(pe, norm_done, hv * 2 + pv - 1)
                        for b in range(2):
                            for jp in range(2):
                                t = 2 * gv + jp
                                c0 = (b * 8 + t) * VW
                                w0 = (2 * b + jp) * P
                                for n, (pp, vv) in enumerate(((p_hi, V_hi), (p_hi, V_lo), (p_lo, V_hi))):
                                    last = pe.matmul(PV_ps[pv][:, c0:c0 + VW], pp[:, sv % 4, w0:w0 + P],
                                                     vv[rv][:, (2 * pv + b) * 8 + t, :], start=(n == 0), stop=(n == 2))
                        last.then_inc(v_done, 1)
                    for name, slot, rel, _ in MISC:
                        if slot == s and runs(name, h + rel):
                            bank_free(pe, name, h)
                            if name == "lg":
                                pe.wait_ge(gate_split, 2)
                                pe.wait_ge(ev["x2T"], PARTS[0][1] // 2)
                                logits(0)
                            elif name == "rank":
                                ranks(0)
                            else:
                                shared_bank(name, h + rel, 1 - r if rel % 2 else r)
                    for n in weights_at(h, s):
                        weights(n)

            def up(n, k, w, xx, width):
                need(pe, silu_done, n - RING + 1)
                for c in range(U_N // width):
                    for m, (ww, part) in enumerate(((W1_hi, 0), (W1_hi, 1), (W1_lo, 0))):
                        last = pe.matmul(U_ps[k % RING][:, c * width:c * width + width], ww[:, w(c)], xx[part],
                                         start=(m == 0), stop=(m == 2))
                last.then_inc(u_done, 1)

            def down(n, k, w, y, width, first, end):
                pe.wait_ge(hhi_done, n + 1)
                pe.wait_ge(hlo_done, n + 1)
                chunks, tiles = U_N // width, width // P
                for c in range(chunks):
                    for t in range(tiles):
                        cols = slice(c * width + t * P, c * width + t * P + P)
                        for m, (hh, ww) in enumerate(((h_hi, W2_hi), (h_hi, W2_lo), (h_lo, W2_hi))):
                            last = pe.matmul(y[:, t * D:t * D + D], hh[k % RING][:, cols], ww[:, w(c)],
                                             start=(first and c == 0 and t == 0 and m == 0),
                                             stop=(end and c == chunks - 1 and t == tiles - 1 and m == 2))
                last.then_inc(d_done, 1)

            def shared_up(n):
                g, c = (n // CH) if n < N0 else BEFORE + (n - N1) // CH, n % CH
                tokens = slice(g * GT * P, (g + 1) * GT * P)
                up(n, n, lambda _: slice(E * HID + c * P, E * HID + c * P + P), (x2T_hi[:, tokens], x2T_lo[:, tokens]), U_N)

            def shared_down(n):
                g, c = (n // CH) if n < N0 else BEFORE + (n - N1) // CH, n % CH
                if c == 0:
                    need(pe, y_done, g - 1 + (BLOCKS if n >= N1 else 0))
                down(n, n, lambda _: slice(E * HID + c * P, E * HID + c * P + P), Y_ps[g % 2], U_N, c == 0, c == CH - 1)

            def block_rows(j, b, i):
                need(pe, xT_lo_done, j - 1)
                pe.wait_ge(loaded[b % LB], (i + b // LB) * 16 + 16)
                for t in range(BT):
                    last = pe.transpose(X_ps[b % 2][:, t * P:t * P + P], xrow[b % LB][:, t, 0:D], ident[:, :])
                last.then_inc(xT_pe, 1)

            def weights_of(j):
                return pe.value_load(w_col[0:1, one(j)], min_val=0, max_val=E * HID)

            def routed_up(i, b, q, col):
                j = i * LB + b
                if q == 0:
                    pe.wait_ge(xT_hi_done, j + 1)
                    pe.wait_ge(xT_lo_done, j + 1)
                up(i * (LB * BU) + N0 + b * BU + q, b * BU + q, lambda c: bass.ds(col + (q * BU + c) * P, P),
                   (xT_hi[b % 2][:, :], xT_lo[b % 2][:, :]), BR)

            def routed_down(i, b, q, col):
                if q == 0:
                    pe.wait_ge(y_done, i * LB + BEFORE + b - 1)
                down(i * (LB * BU) + N0 + b * BU + q, b * BU + q, lambda c: bass.ds(col + (q * BU + c) * P, P),
                     Y_ps[b % 2], BR, q == 0, q == BU - 1)

            def routed(i, end):
                for m in range(LB * BU):
                    b, q = (m + AHEAD) // BU, (m + AHEAD) % BU
                    if q == 0 and not (end and b >= LB):
                        col[i * LB + b] = weights_of(i * LB + b)
                    if q == 0 and not (end and b + 1 >= LB):
                        block_rows(i * LB + b + 1, b + 1, i)
                    if end and b >= LB:
                        shared_up(N1 + m + AHEAD - LB * BU)
                    else:
                        routed_up(i, b, q, col[i * LB + b])
                    routed_down(i, m // BU, m % BU, col[i * LB + m // BU])

            def shared_before(first, end):
                for n in range(first, end):
                    m = n + AHEAD - N0
                    if m == -BU:
                        pe.wait_ge(table, 1)
                        pe.wait_ge(ev["rank"], 2)
                    if m >= -BU and m % BU == 0:
                        block_rows(m // BU + 1, m // BU + 1, 0)
                    if m < 0:
                        shared_up(n + AHEAD)
                    else:
                        if m == 0:
                            pe.wait_ge(tables_ready, 2)
                        if m % BU == 0:
                            col[m // BU] = weights_of(m // BU)
                        routed_up(0, m // BU, m % BU, col[m // BU])
                    shared_down(n)
            col = {}

            most_steps(pe, step, setup)
            pe.wait_ge(exp_done, UNITS * HALVES)
            pe.wait_ge(wt_lo, 2 * NE)
            for n in range(AHEAD):
                shared_up(n)
            shared_before(0, EARLY * CH)
            step(HALVES + 2, 0)

            for name in ("x2T", "x1T", "z"):
                pe.wait_ge(ev[name], HALVES)
            logits(1)
            ranks(1)
            shared_before(EARLY * CH, N0)
            for i in range(BLOCKS // LB):
                routed(i, i == BLOCKS // LB - 1)
            for n in range(N1, NU):
                if n + AHEAD < NU:
                    shared_up(n + AHEAD)
                shared_down(n)

    return nc


_NAMES = {"xWq": "L0_xattn_Wq", "xWk": "L0_xattn_Wk", "xWv": "L0_xattn_Wv", "xWo": "L0_xattn_Wo",
          "aWq": "L0_attn_Wq", "aWk": "L0_attn_Wk", "aWv": "L0_attn_Wv", "aWo": "L0_attn_Wo",
          "xbq": "L0_xattn_bq", "xbk": "L0_xattn_bk", "xbv": "L0_xattn_bv", "xbo": "L0_xattn_bo",
          "abq": "L0_attn_bq", "abk": "L0_attn_bk", "abv": "L0_attn_bv", "abo": "L0_attn_bo",
          "gamma": "L0_xattn_gamma", "beta": "L0_xattn_beta"}


def kernel(**inputs):
    import concourse.bacc as bacc
    from concourse.bass_utils import run_bass_kernel_spmd

    nc = bacc.Bacc("TRN2", target_bir_lowering=False, num_devices=1)
    arrays, aps = {}, {}
    for name, a in inputs.items():
        a = np.ascontiguousarray(a)
        arrays["in_" + name] = a
        aps[name] = nc.dram_tensor("in_" + name, a.shape, mybir.dt.from_np(a.dtype), kind="ExternalInput").ap()
    out = nc.dram_tensor("out_0", (B, S, D), F32, kind="ExternalOutput").ap()
    perceiver(nc, aps["x"], aps["ctx_1024"], [aps[_NAMES[n]] for n in MATS], [aps[_NAMES[n]] for n in ROWS],
              aps["L0_ffn_shared_w1"], aps["L0_ffn_shared_w2"], aps["L0_ffn_experts_w1"],
              aps["L0_ffn_experts_w2"], aps["L0_ffn_gate_w"], out)
    r = run_bass_kernel_spmd(nc, [arrays], core_ids=[0])
    return r.results[0]["out_0"]
```
